# Optimizing a Trainium2 kernel written in Bass

```python
import numpy as np
import jax
import jax.numpy as jnp

def _softmax(x, axis=-1):
    return jax.nn.softmax(x, axis=axis)

def _gelu(x):
    return jax.nn.gelu(x, approximate=True)

def _silu(x):
    return jax.nn.silu(x)

def _sigmoid(x):
    return jax.nn.sigmoid(x)

def _layernorm(x, axis=-1, eps=1e-05):
    m = jnp.mean(x, axis=axis, keepdims=True)
    v = jnp.var(x, axis=axis, keepdims=True)
    return (x - m) / jnp.sqrt(v + eps)

def _scatter_add(tgt, idx, src, axis=0):
    return tgt.at[idx].add(src)

def _segment_sum(src, seg, n):
    return jax.ops.segment_sum(src, seg, n)
kernel_name = 'mk_gps_d1_gnn_r8_103355'

def setup_inputs(seed: int=0):
    np.random.seed(seed)
    _w = jnp.asarray

    def _rec_inputs():
        import jax
        import jax.numpy as jnp
        _gk = jax.random.key(seed)
        x = -0.0003713 + 1 * jax.random.normal(jax.random.fold_in(_gk, 1), (6250, 256), jnp.float32)
        _s = jax.random.randint(jax.random.fold_in(_gk, 2), (50000,), 0, 6250, jnp.int32)
        _d = jax.random.randint(jax.random.fold_in(_gk, 3), (50000,), 0, 6250, jnp.int32)
        _loop = jnp.arange(6250, dtype=jnp.int32)
        src = jnp.concatenate([_s, _d, _loop])
        dst = jnp.concatenate([_d, _s, _loop])
        _o = jnp.argsort(dst, stable=True)
        src = src[_o]
        dst = dst[_o]
        edge_weight = jax.random.uniform(jax.random.fold_in(_gk, 12), (106250,), jnp.float32, 0.0, 0.999998)
        return (x, src, dst, edge_weight)
    x, src, dst, edge_weight = _rec_inputs()

    def _L0_gnn_setup():
        import jax, jax.numpy as jnp
        import numpy as np
        N, E, DIN, H, DOUT = (6250, 100000, 256, 4, 64)
        NEG_SLOPE = 0.2
        key = jax.random.key(seed)
        ks = jax.random.split(key, 7)
        x = jax.random.normal(ks[0], (N, DIN), dtype=jnp.float32)
        edge_index = jax.random.randint(ks[1], (2, E), 0, N, dtype=jnp.int64)
        edge_weight = jax.random.uniform(ks[2], (E,), dtype=jnp.float32)
        W = jax.random.normal(ks[3], (DIN, H * DOUT), dtype=jnp.float32) * (1.0 / np.sqrt(DIN))
        att_src = jax.random.normal(ks[4], (H, DOUT), dtype=jnp.float32) * (1.0 / np.sqrt(DOUT))
        att_dst = jax.random.normal(ks[5], (H, DOUT), dtype=jnp.float32) * (1.0 / np.sqrt(DOUT))
        bias = jnp.zeros((H * DOUT,), dtype=jnp.float32)
        return {'x': x, 'edge_index': edge_index, 'edge_weight': edge_weight, 'W': W, 'att_src': att_src, 'att_dst': att_dst, 'bias': bias}
    _L0_gnn_all = _L0_gnn_setup()
    _L0_gnn_in = {k: v for k, v in _L0_gnn_all.items() if k in ('W', 'att_src', 'att_dst', 'bias')}
    del _L0_gnn_all

    def _L0_mix_setup():
        import jax, jax.numpy as jnp
        import numpy as np
        B, N, C, H = (8, 2048, 256, 8)
        D = C // H
        GH = C // 4
        key = jax.random.key(seed)
        ks = jax.random.split(key, 6)
        s = 0.02
        return {'x': jax.random.normal(ks[0], (B, N, C), dtype=jnp.float32), 'Wqkv': jax.random.normal(ks[1], (C, 3 * C), dtype=jnp.float32) * s, 'Wproj': jax.random.normal(ks[2], (C, C), dtype=jnp.float32) * s, 'bproj': jnp.zeros((C,), dtype=jnp.float32), 'ln_g': jnp.ones((C,), dtype=jnp.float32), 'ln_b': jnp.zeros((C,), dtype=jnp.float32), 'Wg1': jax.random.normal(ks[3], (C, GH), dtype=jnp.float32) * s, 'bg1': jnp.zeros((GH,), dtype=jnp.float32), 'Wg2': jax.random.normal(ks[4], (GH, C), dtype=jnp.float32) * s, 'bg2': jnp.zeros((C,), dtype=jnp.float32)}
    _L0_mix_all = _L0_mix_setup()
    _L0_mix_in = {k: v for k, v in _L0_mix_all.items() if k in ('Wqkv', 'Wproj', 'bproj', 'ln_g', 'ln_b', 'Wg1', 'bg1', 'Wg2', 'bg2')}
    del _L0_mix_all

    def _L0_ffn_setup():
        import jax, jax.numpy as jnp
        import numpy as np
        B, S, D = (8, 512, 256)
        H = 4 * D
        CAPACITY = 0.5
        key = jax.random.key(seed)
        ks = jax.random.split(key, 6)
        x = jax.random.normal(ks[0], (B, S, D), dtype=jnp.float32)
        attention_mask = jnp.zeros((B, 1, 1, S), dtype=jnp.float32)
        wr = jax.random.normal(ks[1], (D, 1), dtype=jnp.float32) * 0.02
        br = jnp.zeros((1,), dtype=jnp.float32)
        w1 = jax.random.normal(ks[2], (D, H), dtype=jnp.float32) * 0.02
        b1 = jnp.zeros((H,), dtype=jnp.float32)
        w2 = jax.random.normal(ks[3], (H, D), dtype=jnp.float32) * 0.02
        b2 = jnp.zeros((D,), dtype=jnp.float32)
        return {'x': x, 'attention_mask': attention_mask, 'wr': wr, 'br': br, 'w1': w1, 'b1': b1, 'w2': w2, 'b2': b2}
    _L0_ffn_all = _L0_ffn_setup()
    _L0_ffn_in = {k: v for k, v in _L0_ffn_all.items() if k in ('attention_mask', 'wr', 'br', 'w1', 'b1', 'w2', 'b2')}
    del _L0_ffn_all
    return {'x': x, 'src': src, 'dst': dst, 'edge_weight': edge_weight, 'L0_gnn_W': _L0_gnn_in['W'], 'L0_gnn_att_src': _L0_gnn_in['att_src'], 'L0_gnn_att_dst': _L0_gnn_in['att_dst'], 'L0_gnn_bias': _L0_gnn_in['bias'], 'L0_mix_Wqkv': _L0_mix_in['Wqkv'], 'L0_mix_Wproj': _L0_mix_in['Wproj'], 'L0_mix_bproj': _L0_mix_in['bproj'], 'L0_mix_ln_g': _L0_mix_in['ln_g'], 'L0_mix_ln_b': _L0_mix_in['ln_b'], 'L0_mix_Wg1': _L0_mix_in['Wg1'], 'L0_mix_bg1': _L0_mix_in['bg1'], 'L0_mix_Wg2': _L0_mix_in['Wg2'], 'L0_mix_bg2': _L0_mix_in['bg2'], 'L0_ffn_attention_mask': _L0_ffn_in['attention_mask'], 'L0_ffn_wr': _L0_ffn_in['wr'], 'L0_ffn_br': _L0_ffn_in['br'], 'L0_ffn_w1': _L0_ffn_in['w1'], 'L0_ffn_b1': _L0_ffn_in['b1'], 'L0_ffn_w2': _L0_ffn_in['w2'], 'L0_ffn_b2': _L0_ffn_in['b2']}

def reference(x, src, dst, edge_weight, L0_gnn_W, L0_gnn_att_src, L0_gnn_att_dst, L0_gnn_bias, L0_mix_Wqkv, L0_mix_Wproj, L0_mix_bproj, L0_mix_ln_g, L0_mix_ln_b, L0_mix_Wg1, L0_mix_bg1, L0_mix_Wg2, L0_mix_bg2, L0_ffn_attention_mask, L0_ffn_wr, L0_ffn_br, L0_ffn_w1, L0_ffn_b1, L0_ffn_w2, L0_ffn_b2):
    import jax
    import jax.numpy as jnp

    def _L0_gnn_ref(x, edge_index, edge_weight, W, att_src, att_dst, bias):
        import jax, jax.numpy as jnp
        import numpy as np
        N, E, DIN, H, DOUT = (6250, 100000, 256, 4, 64)
        NEG_SLOPE = 0.2
        src, dst = (edge_index[0], edge_index[1])
        h = (x @ W).reshape(-1, H, DOUT)
        a_src = jnp.einsum('nhd,hd->nh', h, att_src)
        a_dst = jnp.einsum('nhd,hd->nh', h, att_dst)
        e = jax.nn.leaky_relu(a_src[src] + a_dst[dst], NEG_SLOPE)
        m = jax.ops.segment_max(e, dst, num_segments=N)
        m = jnp.where(jnp.isfinite(m), m, 0.0)
        ex = jnp.exp(e - m[dst])
        s = jax.ops.segment_sum(ex, dst, num_segments=N)
        alpha = ex / jnp.where(s[dst] > 0, s[dst], 1.0)
        msgs = alpha[:, :, None] * h[src]
        out = jax.ops.segment_sum(msgs, dst, num_segments=N)
        out = out.reshape(-1, H * DOUT) + bias
        return jax.nn.sigmoid(out)

    def _L0_mix_ref(x, Wqkv, Wproj, bproj, ln_g, ln_b, Wg1, bg1, Wg2, bg2):
        import jax, jax.numpy as jnp
        import numpy as np
        B, N, C, H = (8, 2048, 256, 8)
        D = C // H
        GH = C // 4
        b, n, c = x.shape
        h, d = (H, D)
        qkv = (x @ Wqkv).reshape(b, n, 3, h, d)
        q, k, v = (qkv[:, :, 0], qkv[:, :, 1], qkv[:, :, 2])
        k = jax.nn.softmax(k, axis=1)
        context = jnp.einsum('bnhd,bnhv->bhdv', k, v)
        out = jnp.einsum('bnhd,bhdv->bnhv', q, context).reshape(b, n, c)
        mu = jnp.mean(x, axis=-1, keepdims=True)
        var = jnp.var(x, axis=-1, keepdims=True)
        xn = (x - mu) * jax.lax.rsqrt(var + 1e-05) * ln_g + ln_b
        hgate = jax.nn.gelu(xn @ Wg1 + bg1, approximate=False)
        gate = jax.nn.sigmoid(hgate @ Wg2 + bg2)
        return out * gate @ Wproj + bproj

    def _L0_ffn_ref(x, attention_mask, wr, br, w1, b1, w2, b2):
        import jax, jax.numpy as jnp
        import numpy as np
        B, S, D = (8, 512, 256)
        H = 4 * D
        CAPACITY = 0.5
        b, s, d = x.shape
        weights = (jnp.einsum('bsd,do->bso', x, wr) + br)[..., 0]
        k = max(1, int(CAPACITY * s))
        kk = k - 1 if k > 1 else 1
        _, idx = jax.lax.top_k(weights, k)
        sel_idx = idx[:, :kk]
        sel = jnp.take_along_axis(x, sel_idx[:, :, None], axis=1)
        h = jax.nn.gelu(jnp.einsum('bkd,dh->bkh', sel, w1) + b1)
        y = jnp.einsum('bkh,hd->bkd', h, w2) + b2
        w_sel = jnp.take_along_axis(weights, sel_idx, axis=1)
        y = y * w_sel[..., None]
        batch_idx = jnp.arange(b)[:, None]
        processed = jnp.zeros_like(x).at[batch_idx, sel_idx].set(y)
        return processed + x
    edge_index = jnp.stack([src, dst])
    xn = _layernorm(x, axis=-1)
    x = x + _L0_gnn_ref(xn, edge_index, edge_weight, L0_gnn_W, L0_gnn_att_src, L0_gnn_att_dst, L0_gnn_bias) + _L0_mix_ref(xn[None], L0_mix_Wqkv, L0_mix_Wproj, L0_mix_bproj, L0_mix_ln_g, L0_mix_ln_b, L0_mix_Wg1, L0_mix_bg1, L0_mix_Wg2, L0_mix_bg2)[0]
    x = x + _L0_ffn_ref(_layernorm(x, axis=-1)[None], L0_ffn_attention_mask, L0_ffn_wr, L0_ffn_br, L0_ffn_w1, L0_ffn_b1, L0_ffn_w2, L0_ffn_b2)[0]
    return x

_drawn_inputs = setup_inputs


def setup_inputs(seed=0):
    import zlib

    import numpy as np

    out = dict(_drawn_inputs(seed))
    spreads = {'L0_gnn_bias': (0.0, 2.0),
     'L0_mix_bproj': (0.0, 0.8),
     'L0_mix_ln_g': (1.0, 0.6),
     'L0_mix_ln_b': (0.0, 0.8),
     'L0_mix_bg1': (0.0, 0.8),
     'L0_mix_bg2': (0.0, 0.8),
     'L0_ffn_b1': (0.0, 0.8),
     'L0_ffn_b2': (0.0, 0.77)}
    factors = {'L0_gnn_att_dst': 28.312,
     'L0_mix_Wqkv': 8.0,
     'L0_mix_Wproj': 8.0,
     'L0_mix_Wg1': 8.0,
     'L0_mix_Wg2': 8.0,
     'L0_ffn_wr': 4.061,
     'L0_ffn_w1': 4.854,
     'L0_ffn_w2': 4.538,
     'L0_gnn_W': 8.0,
     'L0_gnn_att_src': 8.0}
    for name, (base, spread) in spreads.items():
        noise = np.random.default_rng([zlib.crc32(name.encode()), seed]).standard_normal(out[name].shape)
        drawn = base * np.exp(spread * noise) if base else spread * noise
        out[name] = jnp.asarray(drawn.astype(out[name].dtype))
    for name, factor in factors.items():
        out[name] = (out[name] * factor).astype(out[name].dtype)
    return out
```

```python
from contextlib import ExitStack

import numpy as np

import concourse.bass as bass
from concourse import mybir

F32 = mybir.dt.float32
BF16 = mybir.dt.bfloat16
I32 = mybir.dt.int32
ALU = mybir.AluOpType
ACT = mybir.ActivationFunctionType
AX_X = mybir.AxisListType.X
RMAX = bass.bass_isa.ReduceOp.max

P = 128
C = 256
CT = C // P
HEADS = 4
HD = C // HEADS
GH = 64
FF = 1024
FT = FF // P
MIX_HD = 32
EPS = 1e-5
BIG = 1e30
LOWEST = -3e38

TG = 4
GI = 4
TI = TG * GI
GE = TG * P
IE = TI * P
AW = C + HEADS
WA = C + 2 * HEADS + GH
RW = 266
SW = C + 2 * HEADS + 1
LAG_MERGE, LAG_SUM, LAG_FF1, LAG_FF2 = 6, 7, 8, 9


def sweep(eng, lo, hi, peel, body):
    i = lo
    while i < hi and (i < lo + peel or i % 2):
        body(i, i % 2)
        i += 1
    pairs = (hi - i) // 2
    if pairs > 1:
        with eng.Fori(i // 2, i // 2 + pairs) as half:
            for u in range(2):
                body(half * 2 + u, u)
        i += 2 * pairs
    while i < hi:
        body(i, i % 2)
        i += 1


def known_below(i, n):
    return isinstance(i, int) and i < n


def number(eng, v):
    return v if isinstance(v, int) else eng.snap(eng.to_reg(v))


def gps_layer(nc, x, src, dst, W, att_src, att_dst, gnn_bias, Wqkv, Wproj, bproj, ln_g, ln_b, Wg1, bg1, Wg2, bg2,
              wr, br, w1, b1, w2, b2, out, n_nodes):
    NT = x.shape[0] // P
    NI = src.shape[0] // IE
    NG = NI * GI
    KEEP = n_nodes // 2 - 1
    ROWS = NT * P + P
    XC = NT // 7

    with ExitStack() as ctx:
        def sb(name, shape, dt=F32):
            return ctx.enter_context(nc.sbuf_tensor(name, shape, dt))

        named = {}

        def S(name):
            if name not in named:
                named[name] = ctx.enter_context(nc.semaphore(name))
            return named[name]

        bank = [ctx.enter_context(nc.psum_tensor(f"bank{n}", [P, 512], F32)) for n in range(8)]

        def scratch(name, shape, dt=F32):
            return nc.dram_tensor(name, shape, dt, kind="Internal").ap()

        feat_d = scratch("feat_d", [NT * P, AW])
        adst_d = scratch("adst_d", [ROWS, HEADS])
        hid_d = scratch("hid_d", [NT, GH, P])
        part_d = [scratch(f"part{n}_d", [ROWS, SW]) for n in range(2)]
        brk_d = scratch("brk_d", [NI, GI, HEADS, GE])
        dloc_d = scratch("dloc_d", [NI, IE], BF16)
        srow_d = scratch("srow_d", [1, C])

        xnT = sb("xnT", [P, NT, C])
        big = sb("big", [P, NT, C])
        ring = sb("ring", [P, 2 * TI, RW])
        hot = sb("hot", [P, TI, P])
        hotT = sb("hotT", [P, IE])
        ident = sb("ident", [P, P])
        ones = sb("ones", [P, P])
        iota_row = sb("iota_row", [P, P])
        iota_col = sb("iota_col", [P, 1])
        iota_i = sb("iota_i", [P, P], I32)
        iota_ci = sb("iota_ci", [P, 1], I32)
        srcT = sb("srcT", [P, NI, TI], I32)
        dlocT = sb("dlocT", [P, NI, TI], BF16)
        lastT = sb("lastT", [P, NI, TI], BF16)
        idx = sb("idx", [P, 2, TI], I32)
        base_i = sb("base_i", [1, NG], I32)
        acol = sb("acol", [P, TG, TI])
        stat = sb("stat", [P, 2, GI, TI])
        brk = sb("brk", [TI, GE + 1])
        dlb = sb("dlb", [P, IE], BF16)
        w1_s = sb("w1_s", [P, CT, FF])
        w2_s = sb("w2_s", [P, FT, C])
        b1_s = sb("b1_s", [P, FT])
        wproj_s = sb("wproj_s", [P, CT, C])
        wqc_s = sb("wqc_s", [P, CT, C])
        wg2_s = sb("wg2_s", [GH, C])
        hbg2 = sb("hbg2", [P, CT])
        lng = sb("lng", [P, CT])
        lnb = sb("lnb", [P, CT])
        b1row = sb("b1row", [P, GH])
        gbrow = sb("gbrow", [P, C])
        prow = sb("prow", [P, C])
        wrrow = sb("wrrow", [P, C])
        b2row = sb("b2row", [P, C])
        brc = sb("brc", [P, 1])
        epsc = sb("epsc", [P, 1])
        padneg = sb("padneg", [P, NT])
        wts = sb("wts", [P, NT])
        rstd = sb("rstd", [P, NT])
        rstd2 = sb("rstd2", [P, NT])
        mean = sb("mean", [P, NT])
        xs = sb("xs", [P, 2, C])
        sa = sb("sa", [P, 2, C])
        sc = sb("sc", [P, 2, C])
        sd = sb("sd", [P, 2, C])
        parts = sb("parts", [P, 2, 2, SW])
        late = sb("late", [P, 3 * C])
        xn2, xn2T = late[:, 0:C], late[:, C:2 * C]
        junk = sb("junk", [P, C], BF16)
        hidT = sb("hidT", [GH, 2, P])
        hT = sb("hT", [P, FT, P])
        dm = sb("dm", [48, GE])
        srow = sb("srow", [TI, 2, GE])
        wout = sb("wout", [P, 2, SW])
        mg = sb("mg", [P, 2, 64])
        bn = sb("bn", [P, 2, 10])

        wk_s = hT[:, 0:4, :].rearrange("p a b -> p (a b)").rearrange("p (t n) -> p t n", t=CT)
        st = hT[:, 4:8, :].rearrange("p a b -> p (a b)")[:, 0:6 * NT].rearrange("p (t s) -> p t s", s=6)
        wa_s = late[:, 0:CT * WA].rearrange("p (t n) -> p t n", t=CT)
        rmax = wout[:, 0, 0:C]
        cmax = wout[:, 1, 0:C]

        def row(v, n):
            return v.rearrange("(a n) -> a n", a=1).to_broadcast([P, n])

        flat_ring = ring[:, :, :].rearrange("p a b -> p (a b)")
        ed_i = flat_ring.bitcast(I32)[0:NI, 0:2 * IE]
        ed_f = xnT[:, 2:18, :].rearrange("p a b -> p (a b)")[0:NI, 0:2 * IE]
        br_f = flat_ring[0:NI, 2 * IE:3 * IE]
        dl_f = hotT[0:NI, :]
        dl_b = dlb[0:NI, :]
        V = nc.vector
        A = nc.scalar
        T = nc.tensor

        def chain(eng, name):
            count = [0]

            def then(ins):
                count[0] += 1
                ins.then_inc(S(name), 1)

            def settle():
                eng.wait_ge(S(name), count[0])

            return then, settle

        with nc.Block() as block:
            wide = [
                (wa_s[:, :, 0:C], W.rearrange("(t p) n -> p t n", p=P)),
                (wa_s[:, :, C + 2 * HEADS:WA], Wg1.rearrange("(t p) n -> p t n", p=P)),
                (wk_s, Wqkv.rearrange("(t p) n -> p t n", p=P)[:, :, C:2 * C]),
                (wproj_s[:, :, :], Wproj.rearrange("(t p) n -> p t n", p=P)),
                (w1_s[:, :, :], w1.rearrange("(t p) n -> p t n", p=P)),
                (w2_s[:, :, :], w2.rearrange("(t p) n -> p t n", p=P)),
                (wg2_s[:, :], Wg2),
                (sa[:, 0, :], row(att_src.rearrange("h d -> (h d)"), C)),
                (sa[:, 1, :], row(att_dst.rearrange("h d -> (h d)"), C)),
                (gbrow[:, :], row(gnn_bias, C)),
                (prow[:, :], row(bproj, C)),
                (wrrow[:, :], row(wr.rearrange("c o -> (c o)"), C)),
                (b2row[:, :], row(b2, C)),
                (b1row[:, :], row(bg1, GH)),
                (brc[:, :], row(br, 1)),
            ]
            columns = [
                (b1_s[:, :], b1.rearrange("(t p) -> p t", p=P)),
                (hbg2[:, :], bg2.rearrange("(t p) -> p t", p=P)),
                (lng[:, :], ln_g.rearrange("(t p) -> p t", p=P)),
                (lnb[:, :], ln_b.rearrange("(t p) -> p t", p=P)),
                (base_i[:, :], dst.rearrange("(a g e) -> a g e", a=1, e=GE)[:, :, 0]),
            ]
            n_weights = 16 * len(wide + columns)

            @block.sync
            def _(sp):
                sp.dma_start(ed_i[:, 0:IE], src.rearrange("(k e) -> k e", e=IE)).then_inc(S("edges_in"), 16)
                sp.dma_start(ed_i[:, IE:2 * IE], dst.rearrange("(k e) -> k e", e=IE)).then_inc(S("edges_in"), 16)
                for o, i in wide:
                    sp.dma_start(o, i).then_inc(S("weights_in"), 16)
                with nc.allow_non_contiguous_dma(reason="small columns"):
                    for o, i in columns:
                        sp.dma_start(o, i).then_inc(S("weights_in"), 16)
                for n in range(7):
                    sp.dma_start(big[:, n * XC:(n + 1) * XC, :],
                                 x.rearrange("(t p) c -> p t c", p=P)[:, n * XC:(n + 1) * XC, :]).then_inc(S(f"x{n}_in"), 16)
                sp.wait_ge(S("zeroed"), 1)
                zero = xnT[:, 0:2, :].rearrange("p a b -> p (a b)")[:, 0:SW]
                for n in range(2):
                    for t in range(ROWS // P):
                        sp.dma_start(part_d[n][t * P:(t + 1) * P, :], zero).then_inc(S("lists_out"), 16)
                sp.dma_start(adst_d[NT * P:ROWS, :], zero[:, 0:HEADS]).then_inc(S("lists_out"), 16)
                sp.wait_ge(S("breaks_made"), 1)
                for h in range(HEADS):
                    sp.dma_start(brk_d[:, :, h, :], br_f.rearrange("k (g e) -> k g e", g=GI)).then_inc(S("lists_out"), 16)
                sp.wait_ge(S("dloc_made"), 1)
                sp.dma_start(dloc_d, dl_b).then_inc(S("lists_out"), 16)
                sp.wait_ge(S("lists_out"), 16 * (HEADS + 2 + 2 * (ROWS // P)))
                sp.wait_ge(S("weights_in"), n_weights)

            @block.gpsimd
            def _(pool):
                pool.iota(iota_i[:, :], pattern=[[1, P]], base=0, channel_multiplier=0).then_inc(S("pool_made"), 1)
                pool.iota(iota_ci[:, :], pattern=[[0, 1]], base=0, channel_multiplier=1).then_inc(S("pool_made"), 1)
                pool.memset(xnT[:, 0:2, :], 0.0).then_inc(S("zeroed"), 1)
                for a, v in ((ones[:, :], 1.0), (stat[:, :, :, :], 0.0), (brk[:, :], 0.0), (dm[:, :], 0.0),
                             (padneg[:, :], 0.0), (rmax, LOWEST), (epsc[:, :], EPS)):
                    pool.memset(a, v).then_inc(S("pool_made"), 1)

            @block.vector
            def _(dve):
                then, settle = chain(dve, "dve1")
                dve.wait_ge(S("pool_made"), 9)
                then(V.tensor_copy(iota_row[:, :], iota_i[:, :]))
                then(V.tensor_copy(iota_col[:, :], iota_ci[:, :]))
                settle()
                dve.wait_ge(S("edges_in"), 32)
                then(V.tensor_copy(ed_f, ed_i))
                V.tensor_scalar(ident[:, :], iota_row[:, :], iota_col[:, 0:1], None, ALU.is_equal).then_inc(S("ident_made"), 1)
                then(V.tensor_scalar(padneg[:, NT - 1:NT], iota_col[:, 0:1], float(n_nodes - (NT - 1) * P), -BIG,
                                     ALU.is_ge, ALU.mult))
                settle()
                d = ed_f[:, IE:2 * IE]
                then(V.tensor_tensor(br_f[:, 0:IE - 1], d[:, 1:IE], d[:, 0:IE - 1], ALU.not_equal))
                for g in range(GI):
                    then(V.tensor_scalar(dl_f[:, g * GE:(g + 1) * GE], d[:, g * GE:(g + 1) * GE],
                                         d[:, g * GE:g * GE + 1], None, ALU.subtract))
                settle()
                for g in range(GI):
                    then(V.memset(br_f[:, (g + 1) * GE - 1:(g + 1) * GE], 1.0))
                V.tensor_copy(dl_b, dl_f).then_inc(S("dloc_made"), 1)
                settle()
                dve.wait_ge(S("dloc_made"), 1)
                V.memset(mg[:, 0, 0:1], 0.0).then_inc(S("lists_made"), 1)
                for n, to in enumerate((srcT, dlocT, lastT)):
                    for half in range(2):
                        dve.wait_ge(S("lists_turned"), 2 * n + half + 1)
                        V.tensor_copy(to[:, :, half * 8:half * 8 + 8].rearrange("p k q -> p q k"),
                                      bank[2 + half][:, 0:8 * NI].rearrange("p (q k) -> p q k", q=8)
                                      ).then_inc(S("lists_copied"), 1)
                V.tensor_scalar(br_f, br_f, LOWEST, None, ALU.mult).then_inc(S("breaks_made"), 1)
                dve.wait_ge(S("weights_in"), n_weights)
                for n in range(2):
                    for t in range(CT):
                        then(V.tensor_tensor(xs[:, t, :], wa_s[:, t, 0:C], sa[:, n, :], ALU.mult))
                    settle()
                    for t in range(CT):
                        then(V.tensor_reduce(wa_s[:, t, C + n * HEADS:C + (n + 1) * HEADS],
                                             xs[:, t, :].rearrange("p (h d) -> p h d", h=HEADS), AX_X, ALU.add))
                    settle()
                then(V.tensor_scalar(wproj_s[:, :, :], wproj_s[:, :, :], 0.5, None, ALU.mult))
                then(V.tensor_scalar(hbg2[:, :], hbg2[:, :], 0.5, None, ALU.mult))
                then(V.tensor_scalar(prow[:, :], prow[:, :], 0.5, None, ALU.add))
                for t in range(CT):
                    V.tensor_scalar(sc[:, 0, t * P:(t + 1) * P], ones[:, :], lnb[:, t:t + 1], None,
                                    ALU.mult).then_inc(S("lnb_spread"), 1)
                dve.wait_ge(S("lnb_used"), 1)
                then(V.tensor_tensor(b1row[:, :], b1row[:, :], bank[0][:, 0:GH], ALU.add))
                for t in range(CT):
                    then(V.tensor_scalar(wa_s[:, t, C + 2 * HEADS:WA], wa_s[:, t, C + 2 * HEADS:WA], lng[:, t:t + 1],
                                         None, ALU.mult))
                for n in range(7):
                    dve.wait_ge(S(f"x{n}_in"), 16)
                    for t in range(n * XC, (n + 1) * XC):
                        then(V.bn_stats(st[:, t, :], big[:, t, :]))
                settle()
                a, b, c, e = (xs[:, 0, j * 64:j * 64 + NT] for j in range(4))
                then(V.tensor_tensor(a, st[:, :, 1], st[:, :, 4], ALU.add))
                then(V.tensor_tensor(b, st[:, :, 1], st[:, :, 4], ALU.subtract))
                then(V.tensor_tensor(c, st[:, :, 2], st[:, :, 5], ALU.add))
                settle()
                then(V.tensor_scalar(mean[:, :], a, 0.5, None, ALU.mult))
                then(V.tensor_tensor(b, b, b, ALU.mult))
                then(V.tensor_scalar(c, c, 1.0 / C, None, ALU.mult))
                settle()
                then(V.scalar_tensor_tensor(c, b, 0.25, c, ALU.mult, ALU.add))
                settle()
                then(V.tensor_copy(b, c))
                settle()

                def inverse_root(o, v, s, n):
                    then(V.tensor_scalar(v, v, EPS, None, ALU.add))
                    settle()
                    V.tensor_copy(s, v).then_inc(S("root_asked"), 1)
                    dve.wait_ge(S("root_made"), n)
                    then(V.reciprocal(o, s))
                    settle()
                    then(V.tensor_tensor(s, o, o, ALU.mult))
                    settle()
                    then(V.tensor_tensor(s, s, v, ALU.mult))
                    settle()
                    then(V.tensor_scalar(s, s, -0.5, 1.5, ALU.mult, ALU.add))
                    settle()
                    then(V.tensor_tensor(o, o, s, ALU.mult))
                    settle()

                inverse_root(rstd[:, :], c, e, 1)
                then(V.tensor_tensor(b, b, rstd[:, :], ALU.mult))
                settle()
                then(V.tensor_tensor(b, b, rstd[:, :], ALU.mult))
                settle()
                inverse_root(rstd2[:, :], b, e, 2)

            @block.scalar
            def _(act):
                for n in range(2):
                    act.wait_ge(S("root_asked"), n + 1)
                    e = xs[:, 0, 192:192 + NT]
                    A.activation(e, e, ACT.Sqrt).then_inc(S("root_made"), 1)

            @block.tensor
            def _(pe):
                pe.wait_ge(S("ident_made"), 1)
                pe.wait_ge(S("lists_made"), 1)
                for n, lists in enumerate((ed_f[:, 0:IE], dl_f, br_f)):
                    for half in range(2):
                        if n:
                            pe.wait_ge(S("lists_copied"), 2 * n - 1 + half)
                        for q in range(8 * half, 8 * half + 8):
                            at = lists.rearrange("k (g p j) -> k g p j", g=GI, j=TG)[:, q // TG, :, q % TG]
                            mm = T.transpose(bank[2 + half][:, (q % 8) * NI:(q % 8 + 1) * NI], at, ident[0:NI, 0:NI])
                        mm.then_inc(S("lists_turned"), 1)
                pe.wait_ge(S("lnb_spread"), CT)
                for t in range(CT):
                    mm = T.matmul(bank[0][:, 0:GH], sc[:, 0, t * P:(t + 1) * P], wa_s[:, t, C + 2 * HEADS:WA],
                                  start=(t == 0), stop=(t == CT - 1))
                mm.then_inc(S("lnb_used"), 1)

        gate_cols = slice(C + 2 * HEADS, WA)
        feat = parts[:, :, :, :].rearrange("p u a b -> p u (a b)")
        with nc.Block() as block:
            @block.sync
            def _(sp):
                def store(i, u):
                    sp.wait_ge(S("feat_made"), i + 1)
                    rows = bass.ds(i * P, P)
                    sp.dma_start(feat_d[rows, :], feat[:, u, 0:AW]).then_inc(S(f"feat_out{u}"), 16)
                    sp.dma_start(adst_d[rows, :], feat[:, u, AW:AW + HEADS]).then_inc(S(f"feat_out{u}"), 16)
                    sp.wait_ge(S("hidT_made"), i + 1)
                    sp.dma_start(hid_d[bass.ds(i, 1), :, :].rearrange("a b c -> (a b) c"),
                                 hidT[:, u, :]).then_inc(S(f"feat_out{u}"), 16)

                sweep(sp, 0, NT, 0, store)
                for u in range(2):
                    sp.wait_ge(S(f"feat_out{u}"), 48 * ((NT + 1 - u) // 2))

            @block.vector
            def _(dve):
                def first(i, u):
                    if not known_below(i, 2):
                        dve.wait_ge(S("turned"), i - 1)
                    V.tensor_scalar(xs[:, u, :], big[:, bass.ds(i, 1), :].rearrange("p a c -> p (a c)"),
                                    mean[:, bass.ds(i, 1)], rstd[:, bass.ds(i, 1)], ALU.subtract,
                                    ALU.mult).then_inc(S("normed"), 1)

                def second(i, u):
                    dve.wait_ge(S("turned"), i + 1)
                    if not known_below(i, 2):
                        dve.wait_ge(S("keys_done"), i - 1)
                        dve.wait_ge(S("xnT_kept"), i - 1)
                    V.tensor_copy(sa[:, u, :], bank[u][:, 0:C]).then_inc(S("turn_copied"), 1)

                def third(i, u):
                    dve.wait_ge(S("feat_done"), i + 1)
                    if not known_below(i, 2):
                        dve.wait_ge(S(f"feat_out{u}"), 24 * (i - u))
                    V.tensor_copy(feat[:, u, 0:AW + HEADS], bank[2 + u][:, 0:AW + HEADS]).then_inc(S("feat_made"), 1)
                    if not known_below(i, 2):
                        dve.wait_ge(S("hid_made"), i - 1)
                    V.scalar_tensor_tensor(sc[:, u, 0:GH], bank[2 + u][:, gate_cols], rstd2[:, bass.ds(i, 1)],
                                           b1row[:, :], ALU.mult, ALU.add).then_inc(S("hid_asked"), 1)
                    dve.wait_ge(S("keys_kept"), i + 1)
                    if not known_below(i, 1):
                        dve.wait_ge(S("key_max"), i)
                    V.tensor_tensor(rmax, rmax, big[:, bass.ds(i, 1), :].rearrange("p a c -> p (a c)"),
                                    ALU.max).then_inc(S("key_max"), 1)
                    dve.wait_ge(S("hid_turned"), i + 1)
                    V.tensor_copy(hidT[:, u, :], bank[6 + u][0:GH, 0:P]).then_inc(S("hidT_made"), 1)

                def body(i, u):
                    if not known_below(i, NT - 1) and isinstance(i, int):
                        second(i, u)
                        third(i, u)
                        return
                    first(i + 1, 1 - u)
                    second(i, u)
                    third(i, u)

                first(0, 0)
                sweep(dve, 0, NT, 2, body)

            @block.scalar
            def _(act):
                def body(i, u):
                    act.wait_ge(S("turn_copied"), i + 1)
                    A.activation(xnT[:, bass.ds(i, 1), :].rearrange("p a c -> p (a c)"), sa[:, u, :],
                                 ACT.Copy).then_inc(S("xnT_kept"), 1)
                    act.wait_ge(S("keys_done"), i + 1)
                    A.activation(big[:, bass.ds(i, 1), :].rearrange("p a c -> p (a c)"), bank[4 + u][:, 0:C],
                                 ACT.Identity, bias=padneg[:, bass.ds(i, 1)]).then_inc(S("keys_kept"), 1)
                    act.wait_ge(S("hid_asked"), i + 1)
                    if not known_below(i, 2):
                        act.wait_ge(S("hid_turned"), i - 1)
                    A.activation(sd[:, u, 0:GH], sc[:, u, 0:GH], ACT.Gelu).then_inc(S("hid_made"), 1)

                sweep(act, 0, NT, 2, body)

            @block.tensor
            def _(pe):
                def turn(i, u):
                    pe.wait_ge(S("normed"), i + 1)
                    if not known_below(i, 2):
                        pe.wait_ge(S("turn_copied"), i - 1)
                    for t in range(CT):
                        mm = T.transpose(bank[u][:, t * P:(t + 1) * P], xs[:, u, t * P:(t + 1) * P], ident[:, :])
                    mm.then_inc(S("turned"), 1)

                def products(i, u):
                    pe.wait_ge(S("turn_copied"), i + 1)
                    if not known_below(i, 2):
                        pe.wait_ge(S("hid_asked"), i - 1)
                    for t in range(CT):
                        mm = T.matmul(bank[2 + u][:, 0:WA], sa[:, u, t * P:(t + 1) * P], wa_s[:, t, :],
                                      start=(t == 0), stop=(t == CT - 1))
                    mm.then_inc(S("feat_done"), 1)
                    if not known_below(i, 2):
                        pe.wait_ge(S("keys_kept"), i - 1)
                    for t in range(CT):
                        mm = T.matmul(bank[4 + u][:, 0:C], sa[:, u, t * P:(t + 1) * P], wk_s[:, t, :],
                                      start=(t == 0), stop=(t == CT - 1))
                    mm.then_inc(S("keys_done"), 1)

                def hidden(i, u):
                    pe.wait_ge(S("hid_made"), i + 1)
                    if not known_below(i, 2):
                        pe.wait_ge(S("hidT_made"), i - 1)
                    T.matmul(bank[6 + u][0:GH, 0:P], sd[:, u, 0:GH], ident[:, :], start=True, stop=True).then_inc(S("hid_turned"), 1)

                def body(i, u):
                    if not (isinstance(i, int) and i == NT - 1):
                        turn(i + 1, 1 - u)
                    products(i, u)
                    hidden(i, u)

                turn(0, 0)
                sweep(pe, 0, NT, 2, body)

        wq_s = hT[:, 0:4, :].rearrange("p a b -> p (a b)").rearrange("p (t n) -> p t n", t=CT)
        with nc.Block() as block:
            @block.gpsimd
            def _(pool):
                pool.partition_all_reduce(cmax, rmax, P, RMAX).then_inc(S("cmax_made"), 1)

            @block.sync
            def _(sp):
                sp.dma_start(wq_s, Wqkv.rearrange("(t p) n -> p t n", p=P)[:, :, 0:C]).then_inc(S("wqv_in"), 16)
                sp.dma_start(feat[:, :, 0:C], Wqkv.rearrange("(t p) n -> p t n", p=P)[:, :, 2 * C:3 * C]
                             ).then_inc(S("wqv_in"), 16)

                def load(i, u):
                    if not known_below(i, 2):
                        sp.wait_ge(S("renormed"), i - 1)
                    sp.dma_start(xs[:, u, :], x[bass.ds(i * P, P), :]).then_inc(S(f"x_again{u}"), 16)

                sweep(sp, 0, NT, 2, load)

            @block.vector
            def _(dve):
                def body(i, u):
                    if not known_below(i, 2):
                        dve.wait_ge(S("context_added"), i - 1)
                    V.tensor_tensor(sa[:, u, :], big[:, bass.ds(i, 1), :].rearrange("p a c -> p (a c)"), cmax,
                                    ALU.subtract).then_inc(S("keys_less"), 1)
                    dve.wait_ge(S(f"x_again{u}"), 8 * (i - u) + 16)
                    V.tensor_scalar(sc[:, u, :], xs[:, u, :], mean[:, bass.ds(i, 1)], rstd[:, bass.ds(i, 1)],
                                    ALU.subtract, ALU.mult).then_inc(S("renormed"), 1)

                dve.wait_ge(S("cmax_made"), 1)
                sweep(dve, 0, NT, 2, body)
                then, settle = chain(dve, "dve3")
                dve.wait_ge(S("context_added"), NT)
                V.tensor_copy(srow[0:1, 0, 0:C], bank[2][0:1, 0:C]).then_inc(S("totals_kept"), 1)
                for t in range(CT):
                    V.tensor_copy(sc[:, t, :], bank[t][:, 0:C]).then_inc(S("totals_kept"), 1)
                then(V.memset(sd[:, 0, 0:P], 0.0))
                settle()
                for b in range(P // MIX_HD):
                    s = slice(b * MIX_HD, (b + 1) * MIX_HD)
                    then(V.memset(sd[s, 0, s], 1.0))
                dve.wait_ge(S("sums_turned"), 1)
                then(V.reciprocal(mg[:, 0, 0:CT], bank[3][:, 0:CT]))
                settle()
                for t in range(CT):
                    dve.wait_ge(S("context_made"), CT)
                    V.scalar_tensor_tensor(xs[:, 0, t * P:(t + 1) * P], bank[4][:, t * P:(t + 1) * P],
                                           mg[:, 0, t:t + 1], sd[:, 0, 0:P], ALU.mult,
                                           ALU.mult).then_inc(S("context_kept"), 1)
                dve.wait_ge(S("wq_turned"), 1)
                for t in range(CT):
                    V.tensor_copy(sa[:, t, :], bank[5 + t][:, 0:C]).then_inc(S("wq_kept"), 1)
                dve.wait_ge(S("folded"), 1)
                then(V.tensor_copy(wqc_s[:, :, :], bank[7][:, :].rearrange("p (t n) -> p t n", t=CT)))
                settle()

            @block.scalar
            def _(act):
                def body(i, u):
                    act.wait_ge(S("keys_less"), i + 1)
                    A.activation(sa[:, u, :], sa[:, u, :], ACT.Exp).then_inc(S("keys_exp"), 1)

                sweep(act, 0, NT, 2, body)

            @block.tensor
            def _(pe):
                def body(i, u):
                    pe.wait_ge(S("keys_exp"), i + 1)
                    pe.wait_ge(S("renormed"), i + 1)
                    s, e = known_below(i, 1), isinstance(i, int) and i == NT - 1
                    for t in range(CT):
                        T.matmul(bank[t][:, 0:C], sc[:, u, t * P:(t + 1) * P], sa[:, u, :], start=s, stop=e)
                    T.matmul(bank[2][0:1, 0:C], ones[:, 0:1], sa[:, u, :], start=s, stop=e
                             ).then_inc(S("context_added"), 1)

                sweep(pe, 0, NT, 2, body)
                pe.wait_ge(S("totals_kept"), 1 + CT)
                for t in range(CT):
                    mm = T.matmul(bank[3][:, t:t + 1], srow[0:1, 0, t * P:(t + 1) * P], ones[0:1, 0:1], start=True, stop=True)
                mm.then_inc(S("sums_turned"), 1)
                pe.wait_ge(S("wqv_in"), 32)
                for t in range(CT):
                    for c in range(CT):
                        mm = T.matmul(bank[4][:, t * P:(t + 1) * P], sc[:, c, t * P:(t + 1) * P],
                                      feat[:, c, t * P:(t + 1) * P], start=(c == 0), stop=(c == CT - 1))
                    mm.then_inc(S("context_made"), 1)
                for t in range(CT):
                    for c in range(CT):
                        mm = T.transpose(bank[5 + t][:, c * P:(c + 1) * P], wq_s[:, c, t * P:(t + 1) * P], ident[:, :])
                mm.then_inc(S("wq_turned"), 1)
                pe.wait_ge(S("wq_kept"), CT)
                pe.wait_ge(S("context_kept"), CT)
                for c in range(CT):
                    for t in range(CT):
                        mm = T.matmul(bank[7][:, c * C + t * P:c * C + (t + 1) * P], sa[:, t, c * P:(c + 1) * P],
                                      xs[:, 0, t * P:(t + 1) * P], start=True, stop=True)
                mm.then_inc(S("folded"), 1)

        bk_e, bk_t, bk_m, bk_o = bank[0], bank[1], bank[4], bank[5]
        slot = [slice(u * TI, (u + 1) * TI) for u in range(2)]

        def tile(a, i):
            return a[:, bass.ds(i, 1), :].rearrange("p a c -> p (a c)")

        def by_head(a):
            return a.rearrange("p (h d) -> p h d", h=HEADS)

        def steps(eng, parts_of_body):
            def body(k, u):
                for lo, hi, f in parts_of_body:
                    if not isinstance(k, int) or lo <= k < hi:
                        f(k - lo, (u - lo) % 2)
            loop_from = LAG_FF2 + 2 + (LAG_FF2 % 2)
            for k in range(loop_from):
                body(k, k % 2)
            loop_to = NI - 2 - NI % 2
            with eng.Fori(loop_from // 2, loop_to // 2) as half:
                for u in range(2):
                    body(half * 2 + u, u)
            for k in range(loop_to, NT + LAG_FF2):
                body(k, k % 2)

        EDGES = lambda f: (0, NI, f)
        MERGE = lambda f: (LAG_MERGE, NT + LAG_MERGE, f)
        SUM = lambda f: (LAG_SUM, NT + LAG_SUM, f)
        FF1 = lambda f: (LAG_FF1, NT + LAG_FF1, f)
        FF2 = lambda f: (LAG_FF2, NT + LAG_FF2, f)

        with nc.Block() as block:
            @block.gpsimd
            def _(pool):
                def gather(k, u):
                    for g in range(GI):
                        made, used = number(pool, k + 1), None
                        if not known_below(k, 2):
                            used = number(pool, GI * (k - 2) + g + 1)
                        pool.wait_ge(S("idx_made"), 2)
                        if g == 0:
                            pool.wait_ge(S("idx_made"), made)
                        if used is not None:
                            pool.wait_ge(S("sums_done"), used)
                        for j in range(TG):
                            q = g * TG + j
                            pool.indirect_dma_start(
                                out=ring[:, u * TI + q, 0:AW], out_offset=None, in_=feat_d,
                                in_offset=bass.IndirectOffsetOnAxis(ap=idx[:, u, q:q + 1], axis=0),
                            ).then_inc(S(f"rows_in{u}{g}"), 16)

                steps(pool, [EDGES(gather)])

            @block.sync
            def _(sp):
                def base(k, g):
                    return sp.value_load(base_i[0:1, bass.ds(k * GI + g, 1)], min_val=0, max_val=n_nodes - 1)

                def prefetch(k, u):
                    if not known_below(k, 1):
                        sp.wait_ge(S("hotT_made"), k)
                    sp.dma_start(dlb[:, :], dloc_d[bass.ds(k, 1), :].to_broadcast([P, IE])).then_inc(S("dlb_in"), 16)
                    if not known_below(k, 1):
                        sp.wait_ge(S("max_made"), k)
                    sp.dma_start(brk[:, 1:GE + 1], brk_d[bass.ds(k, 1), :, :, :].rearrange("a g h e -> (a g h) e")
                                 ).then_inc(S("brk_in"), 16)
                    first = [base(k, g) for g in range(GI)]
                    if not known_below(k, 2):
                        sp.wait_ge(S("scores_done"), k - 1)
                    for g in range(GI):
                        sp.dma_start(stat[:, u, g, g * HEADS:(g + 1) * HEADS], adst_d[bass.ds(first[g], P), :]
                                     ).then_inc(S(f"stat_in{u}"), 16)

                def ahead(k, u):
                    prefetch(k + 1, 1 - u)

                def windows(k, u):
                    for g in range(GI):
                        first = base(k, g)
                        sp.wait_ge(S("sums_kept"), GI * k + g + 1)
                        if not (known_below(k, 1) and g < 2):
                            sp.wait_ge(S(f"window_out{g % 2}"), 16 * (2 * k + g // 2))
                        sp.dma_start(part_d[g % 2][bass.ds(first, P), :], wout[:, g % 2, :]
                                     ).then_inc(S(f"window_out{g % 2}"), 16)

                def load_node(i, u):
                    upto = number(sp, 32 * (min(i + LAG_MERGE, NI) if isinstance(i, int) else i + LAG_MERGE))
                    free = None if known_below(i, 2) else number(sp, i - 1)
                    sp.wait_ge(S("idx_made"), 2)
                    if free is not None:
                        sp.wait_ge(S("x1_made"), free)
                        sp.wait_ge(S("merged"), free)
                        sp.wait_ge(S("gate_done"), free)
                    for n in range(2):
                        sp.wait_ge(S(f"window_out{n}"), upto)
                    rows = bass.ds(i * P, P)
                    sp.dma_start(hidT[:, u, :], hid_d[bass.ds(i, 1), :, :].rearrange("a b c -> (a b) c")
                                 ).then_inc(S(f"node_in{u}"), 16)
                    for n in range(2):
                        sp.dma_start(parts[:, u, n, :], part_d[n][rows, :]).then_inc(S(f"node_in{u}"), 16)
                    sp.dma_start(xs[:, u, :], x[rows, :]).then_inc(S(f"node_in{u}"), 16)

                prefetch(0, 0)
                steps(sp, [MERGE(load_node), (0, NI - 1, ahead), EDGES(windows)])

            @block.vector
            def _(dve):
                def products(i, u):
                    dve.wait_ge(S("gate_made"), i + 1)
                    dve.wait_ge(S("mix_done"), i + 1)
                    V.scalar_tensor_tensor(sc[:, u, :], sc[:, u, :], 1.0, bk_m[:, 0:C], ALU.add,
                                           ALU.mult).then_inc(S("prod_made"), 1)

                def one_hots(k, u):
                    dve.wait_ge(S("dlb_in"), 16 * k + 16)
                    if not known_below(k, 1):
                        dve.wait_ge(S("scores_done"), k)
                    V.tensor_scalar(hotT[:, :], dlb[:, :], iota_col[:, 0:1], None, ALU.is_equal
                                    ).then_inc(S("hotT_made"), 1)

                def edge_hots(k, u):
                    for g in range(GI):
                        if not known_below(k, 1):
                            dve.wait_ge(S("sums_done"), GI * (k - 1) + g + 1)
                        tiles = slice(g * TG, (g + 1) * TG)
                        V.tensor_tensor(hot[:, tiles, :], iota_row[:, :].unsqueeze(1).to_broadcast([P, TG, P]),
                                        dlocT[:, bass.ds(k, 1), tiles].rearrange("p a q -> p (a q)").unsqueeze(2)
                                        .to_broadcast([P, TG, P]), ALU.is_equal).then_inc(S("hot_made"), 1)

                def merge_weights(i, u):
                    m = mg[:, u, :]
                    dve.wait_ge(S(f"node_in{u}"), 32 * (i - u) + 64)
                    V.tensor_scalar(m[:, 0:2], parts[:, u, :, SW - 1], 1.0, BIG, ALU.subtract, ALU.mult
                                    ).then_inc(S("merge_a"), 1)
                    dve.wait_ge(S("merge_a"), i + 1)
                    V.tensor_tensor(m[:, 2:10].rearrange("p (n h) -> p n h", n=2), parts[:, u, :, C + HEADS:C + 2 * HEADS],
                                    m[:, 0:2].unsqueeze(2).to_broadcast([P, 2, HEADS]), ALU.add).then_inc(S("merge_b"), 1)
                    dve.wait_ge(S("merge_b"), i + 1)
                    V.tensor_tensor(m[:, 10:14], m[:, 2:6], m[:, 6:10], ALU.max).then_inc(S("merge_c"), 1)
                    dve.wait_ge(S("merge_c"), i + 1)
                    V.tensor_tensor(m[:, 14:22].rearrange("p (n h) -> p n h", n=2),
                                    m[:, 2:10].rearrange("p (n h) -> p n h", n=2),
                                    m[:, 10:14].unsqueeze(1).to_broadcast([P, 2, HEADS]), ALU.subtract
                                    ).then_inc(S("merge_asked"), 1)

                def maxima(k, u):
                    dve.wait_ge(S("scores_done"), k + 1)
                    if not known_below(k, 1):
                        dve.wait_ge(S("max_moved"), k)
                    V.tensor_scalar(srow[:, 1, :], bk_e[0:TI, :], 0.2, None, ALU.mult).then_inc(S("slope_made"), 1)
                    dve.wait_ge(S("slope_made"), k + 1)
                    V.tensor_tensor(srow[:, 0, :], bk_e[0:TI, :], srow[:, 1, :], ALU.max).then_inc(S("leaky_made"), 1)
                    dve.wait_ge(S("leaky_made"), k + 1)
                    dve.wait_ge(S("brk_in"), 16 * k + 16)
                    if not known_below(k, 1):
                        dve.wait_ge(S("diff_turned"), k)
                    V.tensor_tensor_scan(dm[0:TI, :], brk[:, 0:GE], srow[:, 0, :], LOWEST, ALU.add, ALU.max
                                         ).then_inc(S("forth_made"), 1)
                    dve.wait_ge(S("forth_made"), k + 1)
                    V.tensor_tensor_scan(srow[:, 1, :][:, ::-1], brk[:, 1:GE + 1][:, ::-1], dm[0:TI, :][:, ::-1],
                                         LOWEST, ALU.add, ALU.max).then_inc(S("max_made"), 1)
                    dve.wait_ge(S("max_made"), k + 1)
                    V.tensor_tensor(dm[0:TI, :], srow[:, 0, :], srow[:, 1, :], ALU.subtract).then_inc(S("diff_made"), 1)

                def outputs(i, u):
                    dve.wait_ge(S("ff2_done"), i + 1)
                    V.tensor_tensor(tile(big, i), bk_o[:, 0:C], b2row[:, :], ALU.add).then_inc(S("out_kept"), 1)

                def messages(k, u):
                    last = lastT[:, bass.ds(k, 1), :].rearrange("p a q -> p (a q)")
                    V.tensor_copy(ring[:, slot[u], SW - 1], last).then_inc(S("lastcol_made"), 1)
                    dve.wait_ge(S("ex_made"), k + 1)
                    V.tensor_tensor(ring[:, slot[u], C + HEADS:C + 2 * HEADS].rearrange("p (g j) h -> p g j h", g=GI),
                                    bk_t[:, 0:48 * TG].rearrange("p (j x) -> p j x", j=TG)[:, :, 32:48]
                                    .rearrange("p j (g h) -> p g j h", g=GI),
                                    last.rearrange("p (g j) -> p g j", g=GI).unsqueeze(3)
                                    .to_broadcast([P, GI, TG, HEADS]), ALU.mult).then_inc(S("maxcol_made"), 1)
                    if not (isinstance(k, int) and k + 2 >= NI):
                        V.tensor_copy(idx[:, u, :], srcT[:, bass.ds(k + 2, 1), :].rearrange("p a q -> p (a q)")
                                      ).then_inc(S("idx_made"), 1)
                    for g in range(GI):
                        rows = ring[:, u * TI + g * TG:u * TI + (g + 1) * TG, :]
                        feats = rows[:, :, 0:C].rearrange("p q (h d) -> p q h d", h=HEADS)
                        V.tensor_tensor(feats, feats, rows[:, :, C:C + HEADS].unsqueeze(3)
                                        .to_broadcast([P, TG, HEADS, HD]), ALU.mult).then_inc(S("scaled"), 1)

                def merge(i, u):
                    m = mg[:, u, :]
                    two = lambda a: a.rearrange("p (n h) -> p n h", n=2)
                    dve.wait_ge(S("merge_exp"), i + 1)
                    V.tensor_tensor(two(m[:, 30:38]), two(m[:, 22:30]), parts[:, u, :, C:C + HEADS], ALU.mult
                                    ).then_inc(S("merge_d"), 1)
                    dve.wait_ge(S("merge_d"), i + 1)
                    V.tensor_tensor(m[:, 38:42], m[:, 30:34], m[:, 34:38], ALU.add).then_inc(S("merge_e"), 1)
                    dve.wait_ge(S("merge_e"), i + 1)
                    V.scalar_tensor_tensor(m[:, 42:46], m[:, 38:42], 0.0, m[:, 38:42], ALU.is_equal, ALU.add
                                           ).then_inc(S("merge_f"), 1)
                    dve.wait_ge(S("merge_f"), i + 1)
                    V.reciprocal(m[:, 46:50], m[:, 42:46]).then_inc(S("merge_g"), 1)
                    dve.wait_ge(S("merge_g"), i + 1)
                    V.tensor_tensor(two(m[:, 50:58]), two(m[:, 22:30]), m[:, 46:50].unsqueeze(1)
                                    .to_broadcast([P, 2, HEADS]), ALU.mult).then_inc(S("merge_h"), 1)
                    dve.wait_ge(S("merge_h"), i + 1)
                    for n, to in enumerate((sa[:, u, :], parts[:, u, 1, 0:C])):
                        V.tensor_tensor(by_head(to), by_head(parts[:, u, n, 0:C]),
                                        m[:, 50 + 4 * n:54 + 4 * n].unsqueeze(2).to_broadcast([P, HEADS, HD]), ALU.mult
                                        ).then_inc(S("merge_i"), 1)
                    dve.wait_ge(S("merge_i"), 2 * i + 2)
                    V.tensor_tensor(sa[:, u, :], sa[:, u, :], parts[:, u, 1, 0:C], ALU.add).then_inc(S("merged"), 1)
                    dve.wait_ge(S("merged"), i + 1)
                    V.tensor_tensor(sa[:, u, :], sa[:, u, :], gbrow[:, :], ALU.add).then_inc(S("gnn_made"), 1)

                def normed(i, u):
                    dve.wait_ge(S("rstd_made"), i + 1)
                    if not known_below(i, 1):
                        dve.wait_ge(S("xn2_turned"), i)
                    V.tensor_scalar(xn2, sd[:, u, :], bn[:, u, 6:7], bn[:, u, 9:10], ALU.subtract, ALU.mult
                                    ).then_inc(S("xn2_made"), 1)
                    dve.wait_ge(S("xn2_made"), i + 1)
                    if not known_below(i, 1):
                        dve.wait_ge(S("routed"), i)
                    V.tensor_tensor_reduce(junk[:, :], xn2, wrrow[:, :], 1.0, brc[:, 0:1], ALU.mult, ALU.add,
                                           mg[:, u, 60:61]).then_inc(S("route_made"), 1)
                    V.tensor_tensor(tile(xnT, i), sd[:, u, :], xn2, ALU.add).then_inc(S("rest_made"), 1)
                    dve.wait_ge(S("route_made"), i + 1)
                    V.tensor_tensor(wts[:, bass.ds(i, 1)], mg[:, u, 60:61], padneg[:, bass.ds(i, 1)], ALU.add
                                    ).then_inc(S("routed"), 1)

                def sums(i, u):
                    dve.wait_ge(S("proj_done"), i + 1)
                    V.tensor_tensor(sd[:, u, :], bk_o[:, C:2 * C], prow[:, :], ALU.add).then_inc(S("proj_read"), 1)
                    dve.wait_ge(S("proj_read"), i + 1)
                    dve.wait_ge(S("gnn_tanh"), i + 1)
                    V.scalar_tensor_tensor(sd[:, u, :], sa[:, u, :], 0.5, sd[:, u, :], ALU.mult, ALU.add
                                           ).then_inc(S("gnn_added"), 1)
                    dve.wait_ge(S("gnn_added"), i + 1)
                    V.tensor_tensor(sd[:, u, :], sd[:, u, :], xs[:, u, :], ALU.add).then_inc(S("x1_made"), 1)
                    dve.wait_ge(S("x1_made"), i + 1)
                    V.bn_stats(bn[:, u, 0:6], sd[:, u, :]).then_inc(S("bn_made"), 1)
                    dve.wait_ge(S("idx_made"), 2)
                    dve.wait_ge(S("bn_made"), i + 1)
                    V.bn_aggr(bn[:, u, 6:8], bn[:, u, 0:6]).then_inc(S("var_made"), 1)

                for u in range(2):
                    V.tensor_copy(idx[:, u, :], srcT[:, u, :]).then_inc(S("idx_made"), 1)
                steps(dve, [SUM(products), EDGES(one_hots), MERGE(merge_weights), EDGES(maxima), EDGES(edge_hots), FF2(outputs),
                            EDGES(messages), MERGE(merge), FF1(normed), SUM(sums)])

            @block.scalar
            def _(act):
                def collect(k, u):
                    for g in range(GI):
                        act.wait_ge(S(f"rows_in{u}{g}"), 32 * (k - u) + 64)
                    if not known_below(k, 1):
                        act.wait_ge(S("scores_done"), k)
                    A.activation(acol[:, :, :].rearrange("p j (g h) -> p g j h", g=GI),
                                 ring[:, slot[u], C:C + HEADS].rearrange("p (g j) h -> p g j h", g=GI), ACT.Copy
                                 ).then_inc(S("acol_made"), 1)

                def move_max(k, u):
                    act.wait_ge(S("max_made"), k + 1)
                    if not known_below(k, 1):
                        act.wait_ge(S("diff_turned"), k)
                    A.activation(dm[32:48, :], srow[:, 1, :], ACT.Copy).then_inc(S("max_moved"), 1)

                def exps(k, u):
                    act.wait_ge(S("diff_turned"), k + 1)
                    A.activation(ring[:, slot[u], C:C + HEADS].rearrange("p (g j) h -> p g j h", g=GI),
                                 bk_t[:, 0:48 * TG].rearrange("p (j x) -> p j x", j=TG)[:, :, 0:16]
                                 .rearrange("p j (g h) -> p g j h", g=GI), ACT.Exp).then_inc(S("ex_made"), 1)

                def merge_exp(i, u):
                    act.wait_ge(S("merge_asked"), i + 1)
                    A.activation(mg[:, u, 22:30], mg[:, u, 14:22], ACT.Exp).then_inc(S("merge_exp"), 1)

                def inverse_root(i, u):
                    act.wait_ge(S("var_made"), i + 1)
                    A.activation(bn[:, u, 8:9], bn[:, u, 7:8], ACT.Ln, bias=epsc[:, 0:1]).then_inc(S("ln_made"), 1)
                    act.wait_ge(S("ln_made"), i + 1)
                    A.activation(bn[:, u, 9:10], bn[:, u, 8:9], ACT.Exp, scale=-0.5).then_inc(S("rstd_made"), 1)

                def keep_sums(k, u):
                    for g in range(GI):
                        act.wait_ge(S("sums_done"), GI * k + g + 1)
                        if not (known_below(k, 1) and g < 2):
                            act.wait_ge(S(f"window_out{g % 2}"), 16 * (2 * k + g // 2))
                        A.activation(wout[:, g % 2, :], bank[2 + g % 2][:, 0:SW], ACT.Copy).then_inc(S("sums_kept"), 1)

                def gates(i, u):
                    act.wait_ge(S("gate_done"), i + 1)
                    if not known_below(i, 2):
                        act.wait_ge(S("proj_done"), i - 1)
                    for t in range(CT):
                        a = A.activation(sc[:, u, t * P:(t + 1) * P], bk_m[:, C + t * P:C + (t + 1) * P], ACT.Tanh,
                                         bias=hbg2[:, t:t + 1], scale=0.5)
                    a.then_inc(S("gate_made"), 1)
                    act.wait_ge(S("gnn_made"), i + 1)
                    A.activation(sa[:, u, :], sa[:, u, :], ACT.Tanh, scale=0.5).then_inc(S("gnn_tanh"), 1)

                def hidden(i, u):
                    act.wait_ge(S("xn2_turned"), i + 1)
                    if not known_below(i, 1):
                        act.wait_ge(S("ff1_done"), FT * i)
                    A.activation(xn2T, bank[7][:, 0:C], ACT.Copy).then_inc(S("xn2T_kept"), 1)
                    if not known_below(i, 1):
                        act.wait_ge(S("ff2_done"), i)
                    for m in range(FT):
                        act.wait_ge(S("ff1_done"), FT * i + m // 4 * 4 + 4)
                        A.activation(hT[:, m, :], bank[6 + m // 4][:, (m % 4) * P:(m % 4 + 1) * P], ACT.Gelu_apprx_tanh,
                                     bias=b1_s[:, m:m + 1]).then_inc(S("gelu_made"), 1)

                steps(act, [EDGES(collect), EDGES(move_max), EDGES(exps), MERGE(merge_exp), FF1(inverse_root), EDGES(keep_sums),
                            MERGE(gates), FF1(hidden)])

            @block.tensor
            def _(pe):
                def mixer(i, u):
                    if not known_below(i, 1):
                        pe.wait_ge(S("prod_made"), i)
                    for t in range(CT):
                        for c in range(CT):
                            mm = T.matmul(bk_m[:, t * P:(t + 1) * P], wqc_s[:, c, t * P:(t + 1) * P],
                                          xnT[:, bass.ds(i, 1), c * P:(c + 1) * P].rearrange("p a c -> p (a c)"),
                                          start=(c == 0), stop=(c == CT - 1))
                    mm.then_inc(S("mix_done"), 1)
                    pe.wait_ge(S(f"node_in{u}"), 32 * (i - u) + 64)
                    if not known_below(i, 1):
                        pe.wait_ge(S("gate_made"), i)
                    for t in range(CT):
                        mm = T.matmul(bk_m[:, C + t * P:C + (t + 1) * P], wg2_s[:, t * P:(t + 1) * P], hidT[:, u, :],
                                      start=True, stop=True)
                    mm.then_inc(S("gate_done"), 1)

                def scores(k, u):
                    pe.wait_ge(S("hotT_made"), k + 1)
                    pe.wait_ge(S(f"stat_in{u}"), 32 * (k - u) + 64)
                    if not known_below(k, 1):
                        pe.wait_ge(S("leaky_made"), k)
                    for g in range(GI):
                        T.matmul(bk_e[0:TI, :], stat[:, u, g, :], hotT[:, g * GE:(g + 1) * GE], start=(g == 0), stop=False)
                    pe.wait_ge(S("acol_made"), k + 1)
                    for j in range(TG):
                        mm = T.matmul(bk_e[0:TI, :].rearrange("r (e j) -> r j e", j=TG)[:, j, :], acol[:, j, :],
                                      ident[:, :], start=False, stop=(j == TG - 1))
                    mm.then_inc(S("scores_done"), 1)

                def ff2(i, u):
                    pe.wait_ge(S("gelu_made"), FT * i + FT)
                    if not known_below(i, 1):
                        pe.wait_ge(S("out_kept"), i)
                    before = i + LAG_FF2 - LAG_SUM
                    pe.wait_ge(S("proj_read"), min(before, NT) if isinstance(i, int) else before)
                    for m in range(FT):
                        mm = T.matmul(bk_o[:, 0:C], hT[:, m, :], w2_s[:, m, :], start=(m == 0), stop=(m == FT - 1))
                    mm.then_inc(S("ff2_done"), 1)

                def turn_scores(k, u):
                    pe.wait_ge(S("diff_made"), k + 1)
                    pe.wait_ge(S("max_moved"), k + 1)
                    if not known_below(k, 1):
                        pe.wait_ge(S("ex_made"), k)
                        pe.wait_ge(S("maxcol_made"), k)
                    for j in range(TG):
                        mm = T.matmul(bk_t[:, j * 48:(j + 1) * 48], dm[:, :].rearrange("r (e j) -> r j e", j=TG)[:, j, :],
                                      ident[0:48, 0:48], start=True, stop=True)
                    mm.then_inc(S("diff_turned"), 1)

                def window_sums(k, u):
                    pe.wait_ge(S("lastcol_made"), k + 1)
                    pe.wait_ge(S("maxcol_made"), k + 1)
                    for g in range(GI):
                        pe.wait_ge(S("hot_made"), GI * k + g + 1)
                        pe.wait_ge(S("scaled"), GI * k + g + 1)
                        if not (known_below(k, 1) and g < 2):
                            pe.wait_ge(S("sums_kept"), GI * k + g - 1)
                        for j in range(TG):
                            q = u * TI + g * TG + j
                            mm = T.matmul(bank[2 + g % 2][:, 0:SW], hot[:, g * TG + j, :], ring[:, q, 0:SW],
                                          start=(j == 0), stop=(j == TG - 1))
                        mm.then_inc(S("sums_done"), 1)

                def project(i, u):
                    pe.wait_ge(S("prod_made"), i + 1)
                    if not known_below(i, 1):
                        pe.wait_ge(S("proj_read"), i)
                    if not known_below(i, LAG_FF2 - LAG_SUM):
                        pe.wait_ge(S("out_kept"), i - (LAG_FF2 - LAG_SUM) + 1)
                    for t in range(CT):
                        mm = T.matmul(bk_o[:, C:2 * C], sc[:, u, t * P:(t + 1) * P], wproj_s[:, t, :],
                                      start=(t == 0), stop=(t == CT - 1))
                    mm.then_inc(S("proj_done"), 1)

                def ff1(i, u):
                    pe.wait_ge(S("xn2_made"), i + 1)
                    if not known_below(i, 1):
                        pe.wait_ge(S("gelu_made"), FT * i)
                    for t in range(CT):
                        mm = T.transpose(bank[7][:, t * P:(t + 1) * P], xn2[:, t * P:(t + 1) * P], ident[:, :])
                    mm.then_inc(S("xn2_turned"), 1)
                    pe.wait_ge(S("xn2T_kept"), i + 1)
                    for m in range(FT):
                        if m % 4 == 0 and not known_below(i, 1):
                            pe.wait_ge(S("gelu_made"), FT * (i - 1) + m + 4)
                        for t in range(CT):
                            mm = T.matmul(bank[6 + m // 4][:, (m % 4) * P:(m % 4 + 1) * P], w1_s[:, t, m * P:(m + 1) * P],
                                          xn2T[:, t * P:(t + 1) * P], start=(t == 0), stop=(t == CT - 1))
                        mm.then_inc(S("ff1_done"), 1)

                steps(pe, [MERGE(mixer), EDGES(scores), FF2(ff2), EDGES(turn_scores), EDGES(window_sums), SUM(project),
                           FF1(ff1)])

        ROUNDS = 8
        tail = flat_ring[:, 0:64 * P].rearrange("p (a b) -> p a b", b=P)
        lower, jtab = tail[:, 0, :], tail[:, 1, 0:15].bitcast(I32)
        v_s = tail[:, 2, 0:NT]
        cmp_s = tail[:, 4:12, :].rearrange("p a b -> p (a b)")[:, 0:15 * NT].rearrange("p (j t) -> p j t", j=15)
        cand = tail[:, 12, 0:15]
        cnt = tail[:, 13, 0:15]
        one = lambda n: tail[:, 14, n:n + 1]
        t_bits, sign, want, dig, more, thr, need = (one(n) for n in range(7))
        dig_i = one(8)
        eq_s, gt_s, pre_s, off_s, sel_s = (tail[:, 16 + n, 0:NT] for n in range(5))
        tot_s = tail[:, 21, 0:NT]
        n_steps = ROUNDS + 2
        with nc.Block() as block:
            @block.gpsimd
            def _(pool):
                pool.iota(hotT[:, 0:15].bitcast(I32), pattern=[[1, 15]], base=1, channel_multiplier=0
                          ).then_inc(S("digits_made"), 1)

            @block.tensor
            def _(pe):
                for n in range(n_steps):
                    pe.wait_ge(S("counted"), n + 1)
                    T.matmul(bank[n % 2][:, 0:15], ones[:, :], cnt, start=True, stop=True).then_inc(S("totalled"), 1)
                pe.wait_ge(S("ties_made"), 1)
                T.matmul(bank[2][:, 0:NT], lower, eq_s, start=True, stop=True)
                T.matmul(bank[3][:, 0:NT], ones[:, :], eq_s, start=True, stop=True).then_inc(S("ties_counted"), 1)

            @block.vector
            def _(dve):
                then, settle = chain(dve, "dve5")
                n_counts = [0]

                def total():
                    settle()
                    V.tensor_copy(off_s[:, 0:1], cnt[:, 0:1]).then_inc(S("counted"), 1)
                    n_counts[0] += 1
                    dve.wait_ge(S("totalled"), n_counts[0])
                    return bank[(n_counts[0] - 1) % 2]

                then(V.tensor_scalar(lower, iota_row[:, :], iota_col[:, 0:1], None, ALU.is_gt))
                then(V.memset(cnt, 0.0))
                settle()
                then(V.tensor_scalar(sel_s, wts[:, :], 0.0, 0.0, ALU.is_ge, ALU.add, accum_out=cnt[:, 0:1]))
                b = total()
                then(V.tensor_scalar(dig, b[:, 0:1], float(KEEP), None, ALU.is_ge))
                settle()
                then(V.tensor_scalar(sign, dig, 2.0, -1.0, ALU.mult, ALU.add))
                then(V.tensor_scalar(want, dig, float(2 * KEEP - NT * P - 1), float(NT * P + 1 - KEEP), ALU.mult, ALU.add))
                settle()
                then(V.tensor_scalar(v_s, wts[:, :], sign, None, ALU.mult))
                then(V.memset(t_bits, 0.0))
                dve.wait_ge(S("digits_made"), 1)
                for r in range(ROUNDS):
                    shift = 28 - 4 * r
                    J = 7 if r == 0 else 15
                    settle()
                    then(V.tensor_scalar(jtab, hotT[:, 0:15].bitcast(I32), shift, None, ALU.logical_shift_left))
                    settle()
                    then(V.tensor_tensor(cand[:, 0:J].bitcast(I32), jtab[:, 0:J], t_bits.bitcast(I32).to_broadcast([P, J]),
                                         ALU.bitwise_or))
                    settle()
                    then(V.tensor_tensor(cmp_s[:, 0:J, :], v_s.unsqueeze(1).to_broadcast([P, J, NT]),
                                         cand[:, 0:J].unsqueeze(2).to_broadcast([P, J, NT]), ALU.is_ge))
                    settle()
                    then(V.tensor_reduce(cnt[:, 0:J], cmp_s[:, 0:J, :], AX_X, ALU.add))
                    b = total()
                    then(V.tensor_scalar(sel_s[:, 0:J], b[:, 0:J], want, 0.0, ALU.is_ge, ALU.add, accum_out=dig))
                    settle()
                    then(V.tensor_scalar(dig_i.bitcast(I32), dig, float(1 << shift), None, ALU.mult))
                    settle()
                    then(V.tensor_tensor(t_bits.bitcast(I32), t_bits.bitcast(I32), dig_i.bitcast(I32), ALU.bitwise_or))
                settle()
                then(V.tensor_tensor(thr, t_bits, sign, ALU.mult))
                settle()
                then(V.tensor_scalar(gt_s, wts[:, :], thr, 0.0, ALU.is_gt, ALU.add, accum_out=cnt[:, 0:1]))
                V.tensor_scalar(eq_s, wts[:, :], thr, None, ALU.is_equal).then_inc(S("ties_made"), 1)
                b = total()
                then(V.tensor_scalar(need, b[:, 0:1], -1.0, float(KEEP), ALU.mult, ALU.add))
                dve.wait_ge(S("ties_counted"), 1)
                then(V.tensor_copy(tot_s, bank[3][:, 0:NT]))
                then(V.memset(sel_s, 0.0))
                settle()
                then(V.tensor_tensor_scan(pre_s, tot_s, sel_s, 0.0, ALU.add, ALU.add))
                settle()
                then(V.tensor_tensor(pre_s, pre_s, tot_s, ALU.subtract))
                settle()
                then(V.tensor_tensor(pre_s, pre_s, bank[2][:, 0:NT], ALU.add))
                settle()
                then(V.tensor_scalar(pre_s, pre_s, need, None, ALU.is_lt))
                settle()
                then(V.tensor_tensor(pre_s, pre_s, eq_s, ALU.mult))
                settle()
                then(V.tensor_tensor(sel_s, pre_s, gt_s, ALU.add))
                settle()
                then(V.tensor_tensor(sel_s, sel_s, wts[:, :], ALU.mult))
                settle()
                for t in range(NT):
                    V.scalar_tensor_tensor(xnT[:, t, :], big[:, t, :], sel_s[:, t:t + 1], xnT[:, t, :], ALU.mult, ALU.add
                                           ).then_inc(S("result_made"), 1)

            @block.sync
            def _(sp):
                to = out.rearrange("(t p) c -> p t c", p=P)
                for n in range(7):
                    sp.wait_ge(S("result_made"), (n + 1) * XC)
                    sp.dma_start(to[:, n * XC:(n + 1) * XC, :], xnT[:, n * XC:(n + 1) * XC, :]).then_inc(S("result_out"), 16)
                sp.wait_ge(S("result_out"), 16 * 7)


_INS = ["x", "src", "dst", "L0_gnn_W", "L0_gnn_att_src", "L0_gnn_att_dst", "L0_gnn_bias", "L0_mix_Wqkv",
        "L0_mix_Wproj", "L0_mix_bproj", "L0_mix_ln_g", "L0_mix_ln_b", "L0_mix_Wg1", "L0_mix_bg1", "L0_mix_Wg2",
        "L0_mix_bg2", "L0_ffn_wr", "L0_ffn_br", "L0_ffn_w1", "L0_ffn_b1", "L0_ffn_w2", "L0_ffn_b2"]
FAR = 1 << 20


def kernel(**inputs):
    import concourse.bacc as bacc
    from concourse.bass_utils import run_bass_kernel_spmd

    nc = bacc.Bacc("TRN2", target_bir_lowering=False, num_devices=1, dynamic_dma_scratch_size=4096)
    n_nodes, n_edges = inputs["x"].shape[0], inputs["src"].shape[0]
    padded = {"x": (-(-n_nodes // P) * P, 0), "src": (-(-n_edges // IE) * IE, 0), "dst": (-(-n_edges // IE) * IE, FAR)}
    arrays, args = {}, []
    for name in _INS:
        a = np.ascontiguousarray(inputs[name])
        if name in padded:
            rows, value = padded[name]
            full = np.full((rows, *a.shape[1:]), value, a.dtype)
            full[:a.shape[0]] = a
            a = full
        arrays[f"in_{name}"] = a
        args.append(nc.dram_tensor(f"in_{name}", a.shape, mybir.dt.from_np(a.dtype), kind="ExternalInput").ap())
    out = nc.dram_tensor("out_0", arrays["in_x"].shape, F32, kind="ExternalOutput").ap()
    gps_layer(nc, *args, out, n_nodes)
    r = run_bass_kernel_spmd(nc, [arrays], core_ids=[0])
    return r.results[0]["out_0"][:n_nodes]
```

```python
from contextlib import ExitStack

import numpy as np

import concourse.bass as bass
from concourse import mybir

F32 = mybir.dt.float32
BF16 = mybir.dt.bfloat16
I32 = mybir.dt.int32
ALU = mybir.AluOpType
ACT = mybir.ActivationFunctionType
AX_X = mybir.AxisListType.X
RMAX = bass.bass_isa.ReduceOp.max

P = 128
C = 256
CT = C // P
HEADS = 4
HD = C // HEADS
GH = 64
FF = 1024
FT = FF // P
MIX_HD = 32
EPS = 1e-5
BIG = 1e30
LOWEST = -3e38

TG = 4
GI = 4
TI = TG * GI
GE = TG * P
IE = TI * P
AW = C + HEADS
WA = C + 2 * HEADS + GH
SPLIT = 3 * HEADS
RW = 266
SW = C + 2 * HEADS + 1
LAG_MERGE, LAG_SUM, LAG_FF1, LAG_FF2 = 6, 7, 8, 9


def sweep(eng, lo, hi, peel, rest, body):
    i = lo
    while i < hi and (i < lo + peel or i % 2):
        body(i, i % 2)
        i += 1
    pairs = (hi - rest - i) // 2
    with eng.Fori(i // 2, i // 2 + pairs) as half:
        for u in range(2):
            body(half * 2 + u, u)
    for i in range(i + 2 * pairs, hi):
        body(i, i % 2)


def known_below(i, n):
    return isinstance(i, int) and i < n


def number(eng, v):
    return v if isinstance(v, int) else eng.snap(eng.to_reg(v))


def gps_layer(nc, x, src, dst, W, att_src, att_dst, gnn_bias, Wqkv, Wproj, bproj, ln_g, ln_b, Wg1, bg1, Wg2, bg2,
              wr, br, w1, b1, w2, b2, out, n_nodes):
    NT = x.shape[0] // P
    NI = src.shape[0] // IE
    NG = NI * GI
    KEEP = n_nodes // 2 - 1
    ROWS = NT * P + P
    XC = NT // 7

    with ExitStack() as ctx:
        def sb(name, shape, dt=F32):
            return ctx.enter_context(nc.sbuf_tensor(name, shape, dt))

        named = {}

        def S(name):
            if name not in named:
                named[name] = ctx.enter_context(nc.semaphore(name))
            return named[name]

        bank = [ctx.enter_context(nc.psum_tensor(f"bank{n}", [P, 512], F32)) for n in range(8)]

        def scratch(name, shape, dt=F32):
            return nc.dram_tensor(name, shape, dt, kind="Internal").ap()

        feat_d = scratch("feat_d", [NT * P, AW])
        adst_d = scratch("adst_d", [ROWS, SPLIT], BF16)
        hid_d = scratch("hid_d", [NT, GH, P])
        part_d = [scratch(f"part{n}_d", [ROWS, SW]) for n in range(2)]
        brk_d = scratch("brk_d", [NI, GI, HEADS, GE])
        dloc_d = scratch("dloc_d", [NI, IE], BF16)
        srow_d = scratch("srow_d", [1, C])

        xnT = sb("xnT", [P, NT, C])
        big = sb("big", [P, NT, C])
        ring = sb("ring", [P, 2 * TI, RW])
        hot = sb("hot", [P, TI, P])
        hotT = sb("hotT", [P, IE], BF16)
        ident = sb("ident", [P, P])
        ones = sb("ones", [P, P])
        iota_row = sb("iota_row", [P, P])
        iota_col = sb("iota_col", [P, 1])
        iota_i = sb("iota_i", [P, P], I32)
        iota_ci = sb("iota_ci", [P, 1], I32)
        srcT = sb("srcT", [P, NI, TI], I32)
        dlocT = sb("dlocT", [P, NI, TI], BF16)
        lastT = sb("lastT", [P, NI, TI], BF16)
        idx = sb("idx", [P, 2, TI], I32)
        base_i = sb("base_i", [1, NG], I32)
        adst_s = sb("adst_s", [P, NT, HEADS])
        adst_p = sb("adst_p", [P, NT, SPLIT], BF16)
        stat = sb("stat", [P, 2, GI, SPLIT], BF16)
        lk = sb("lk", [P, 2, TG, TI])
        diff = sb("diff", [P, TG, TI])
        brk = sb("brk", [TI, GE + 1])
        dlb = sb("dlb", [P, IE], BF16)
        w1_s = sb("w1_s", [P, CT, FF])
        w2_s = sb("w2_s", [P, FT, C])
        b1_s = sb("b1_s", [P, FT])
        wproj_s = sb("wproj_s", [P, CT, C])
        wqc_s = sb("wqc_s", [P, CT, C])
        wg2_s = sb("wg2_s", [GH, C])
        hbg2 = sb("hbg2", [P, CT])
        lng = sb("lng", [P, CT])
        lnb = sb("lnb", [P, CT])
        b1row = sb("b1row", [P, GH])
        gbrow = sb("gbrow", [P, C])
        prow = sb("prow", [P, C])
        wrrow = sb("wrrow", [P, C])
        b2row = sb("b2row", [P, C])
        brc = sb("brc", [P, 1])
        epsc = sb("epsc", [P, 1])
        padneg = sb("padneg", [P, NT])
        wts = sb("wts", [P, NT])
        rstd = sb("rstd", [P, NT])
        rstd2 = sb("rstd2", [P, NT])
        mean = sb("mean", [P, NT])
        xs = sb("xs", [P, 2, C])
        sa = sb("sa", [P, 2, C])
        sc = sb("sc", [P, 2, C])
        sd = sb("sd", [P, 2, C])
        parts = sb("parts", [P, 2, 2, SW])
        late = sb("late", [P, 3 * C])
        xn2, xn2T = late[:, 0:C], late[:, C:2 * C]
        junk = sb("junk", [P, C], BF16)
        hidT = sb("hidT", [GH, 2, P])
        hT = sb("hT", [P, FT, P])
        forth = sb("forth", [TI, GE])
        srow = sb("srow", [TI, GE])
        wout = sb("wout", [P, 2, SW])
        mg = sb("mg", [P, 2, 64])
        bn = sb("bn", [P, 2, 10])

        wk_s = hT[:, 0:4, :].rearrange("p a b -> p (a b)").rearrange("p (t n) -> p t n", t=CT)
        st = hT[:, 4:8, :].rearrange("p a b -> p (a b)")[:, 0:6 * NT].rearrange("p (t s) -> p t s", s=6)
        wa_s = late[:, 0:CT * WA].rearrange("p (t n) -> p t n", t=CT)
        rmax = wout[:, 0, 0:C]
        cmax = wout[:, 1, 0:C]

        def row(v, n):
            return v.rearrange("(a n) -> a n", a=1).to_broadcast([P, n])

        flat_ring = ring[:, :, :].rearrange("p a b -> p (a b)")
        ed_i = flat_ring.bitcast(I32)[0:NI, 0:2 * IE]
        ed_f = xnT[:, 2:18, :].rearrange("p a b -> p (a b)")[0:NI, 0:2 * IE]
        br_f = flat_ring[0:NI, 2 * IE:3 * IE]
        dl_f = flat_ring[0:NI, 3 * IE:4 * IE]
        dl_b = dlb[0:NI, :]
        V = nc.vector
        A = nc.scalar
        T = nc.tensor

        def chain(eng, name):
            count = [0]

            def then(ins):
                count[0] += 1
                ins.then_inc(S(name), 1)

            def settle():
                eng.wait_ge(S(name), count[0])

            return then, settle

        with nc.Block() as block:
            wide = [
                (wa_s[:, :, 0:C], W.rearrange("(t p) n -> p t n", p=P)),
                (wa_s[:, :, C + 2 * HEADS:WA], Wg1.rearrange("(t p) n -> p t n", p=P)),
                (wk_s, Wqkv.rearrange("(t p) n -> p t n", p=P)[:, :, C:2 * C]),
                (wproj_s[:, :, :], Wproj.rearrange("(t p) n -> p t n", p=P)),
                (w1_s[:, :, :], w1.rearrange("(t p) n -> p t n", p=P)),
                (w2_s[:, :, :], w2.rearrange("(t p) n -> p t n", p=P)),
                (wg2_s[:, :], Wg2),
                (sa[:, 0, :], row(att_src.rearrange("h d -> (h d)"), C)),
                (sa[:, 1, :], row(att_dst.rearrange("h d -> (h d)"), C)),
                (gbrow[:, :], row(gnn_bias, C)),
                (prow[:, :], row(bproj, C)),
                (wrrow[:, :], row(wr.rearrange("c o -> (c o)"), C)),
                (b2row[:, :], row(b2, C)),
                (b1row[:, :], row(bg1, GH)),
                (brc[:, :], row(br, 1)),
            ]
            columns = [
                (b1_s[:, :], b1.rearrange("(t p) -> p t", p=P)),
                (hbg2[:, :], bg2.rearrange("(t p) -> p t", p=P)),
                (lng[:, :], ln_g.rearrange("(t p) -> p t", p=P)),
                (lnb[:, :], ln_b.rearrange("(t p) -> p t", p=P)),
                (base_i[:, :], dst.rearrange("(a g e) -> a g e", a=1, e=GE)[:, :, 0]),
            ]
            n_weights = 16 * len(wide + columns)

            @block.sync
            def _(sp):
                sp.dma_start(ed_i[:, 0:IE], src.rearrange("(k e) -> k e", e=IE)).then_inc(S("edges_in"), 16)
                sp.dma_start(ed_i[:, IE:2 * IE], dst.rearrange("(k e) -> k e", e=IE)).then_inc(S("edges_in"), 16)
                for o, i in wide:
                    sp.dma_start(o, i).then_inc(S("weights_in"), 16)
                with nc.allow_non_contiguous_dma(reason="small columns"):
                    for o, i in columns:
                        sp.dma_start(o, i).then_inc(S("weights_in"), 16)
                for n in range(7):
                    sp.dma_start(big[:, n * XC:(n + 1) * XC, :],
                                 x.rearrange("(t p) c -> p t c", p=P)[:, n * XC:(n + 1) * XC, :]).then_inc(S(f"x{n}_in"), 16)
                sp.wait_ge(S("breaks_made"), 1)
                for h in range(HEADS):
                    sp.dma_start(brk_d[:, :, h, :], br_f.rearrange("k (g e) -> k g e", g=GI)).then_inc(S("lists_out"), 16)
                sp.wait_ge(S("dloc_made"), 1)
                sp.dma_start(dloc_d, dl_b).then_inc(S("lists_out"), 16)
                sp.wait_ge(S("weights_in"), n_weights)

            @block.gpsimd
            def _(pool):
                pool.iota(iota_i[:, :], pattern=[[1, P]], base=0, channel_multiplier=0).then_inc(S("pool_made"), 1)
                pool.iota(iota_ci[:, :], pattern=[[0, 1]], base=0, channel_multiplier=1).then_inc(S("pool_made"), 1)
                pool.memset(hot[:, 0:3, :], 0.0).then_inc(S("zeroed"), 1)
                for a, v in ((ones[:, :], 1.0), (brk[:, :], 0.0),
                             (padneg[:, :], 0.0), (rmax, LOWEST), (epsc[:, :], EPS)):
                    pool.memset(a, v).then_inc(S("pool_made"), 1)

            @block.vector
            def _(dve):
                then, settle = chain(dve, "dve1")
                dve.wait_ge(S("pool_made"), 7)
                then(V.tensor_copy(iota_row[:, :], iota_i[:, :]))
                then(V.tensor_copy(iota_col[:, :], iota_ci[:, :]))
                settle()
                dve.wait_ge(S("edges_in"), 32)
                then(V.tensor_copy(ed_f, ed_i))
                V.tensor_scalar(ident[:, :], iota_row[:, :], iota_col[:, 0:1], None, ALU.is_equal).then_inc(S("ident_made"), 1)
                then(V.tensor_scalar(padneg[:, NT - 1:NT], iota_col[:, 0:1], float(n_nodes - (NT - 1) * P), -BIG,
                                     ALU.is_ge, ALU.mult))
                settle()
                d = ed_f[:, IE:2 * IE]
                then(V.tensor_tensor(br_f[:, 0:IE - 1], d[:, 1:IE], d[:, 0:IE - 1], ALU.not_equal))
                for g in range(GI):
                    then(V.tensor_scalar(dl_f[:, g * GE:(g + 1) * GE], d[:, g * GE:(g + 1) * GE],
                                         d[:, g * GE:g * GE + 1], None, ALU.subtract))
                settle()
                for g in range(GI):
                    then(V.memset(br_f[:, (g + 1) * GE - 1:(g + 1) * GE], 1.0))
                V.tensor_copy(dl_b.rearrange("k (g j p) -> k g j p", g=GI, j=TG), dl_f.rearrange("k (g p j) -> k g j p", g=GI, j=TG)).then_inc(S("dloc_made"), 1)
                settle()
                dve.wait_ge(S("dloc_made"), 1)
                V.memset(mg[:, 0, 0:1], 0.0).then_inc(S("lists_made"), 1)
                for n, to in enumerate((srcT, dlocT, lastT)):
                    for half in range(2):
                        dve.wait_ge(S("lists_turned"), 2 * n + half + 1)
                        V.tensor_copy(to[:, :, half * 8:half * 8 + 8].rearrange("p k q -> p q k"),
                                      bank[2 + half][:, 0:8 * NI].rearrange("p (q k) -> p q k", q=8)
                                      ).then_inc(S("lists_copied"), 1)
                V.tensor_scalar(br_f, br_f, LOWEST, None, ALU.mult).then_inc(S("breaks_made"), 1)
                dve.wait_ge(S("weights_in"), n_weights)
                for n in range(2):
                    for t in range(CT):
                        then(V.tensor_tensor(xs[:, t, :], wa_s[:, t, 0:C], sa[:, n, :], ALU.mult))
                    settle()
                    for t in range(CT):
                        then(V.tensor_reduce(wa_s[:, t, C + n * HEADS:C + (n + 1) * HEADS],
                                             xs[:, t, :].rearrange("p (h d) -> p h d", h=HEADS), AX_X, ALU.add))
                    settle()
                then(V.tensor_scalar(wproj_s[:, :, :], wproj_s[:, :, :], 0.5, None, ALU.mult))
                then(V.tensor_scalar(hbg2[:, :], hbg2[:, :], 0.5, None, ALU.mult))
                then(V.tensor_scalar(prow[:, :], prow[:, :], 0.5, None, ALU.add))
                for t in range(CT):
                    V.tensor_scalar(sc[:, 0, t * P:(t + 1) * P], ones[:, :], lnb[:, t:t + 1], None,
                                    ALU.mult).then_inc(S("lnb_spread"), 1)
                dve.wait_ge(S("lnb_used"), 1)
                then(V.tensor_tensor(b1row[:, :], b1row[:, :], bank[0][:, 0:GH], ALU.add))
                for t in range(CT):
                    then(V.tensor_scalar(wa_s[:, t, C + 2 * HEADS:WA], wa_s[:, t, C + 2 * HEADS:WA], lng[:, t:t + 1],
                                         None, ALU.mult))
                for n in range(7):
                    dve.wait_ge(S(f"x{n}_in"), 16)
                    for t in range(n * XC, (n + 1) * XC):
                        then(V.bn_stats(st[:, t, :], big[:, t, :]))
                settle()
                a, b, c, e = (xs[:, 0, j * 64:j * 64 + NT] for j in range(4))
                then(V.tensor_tensor(a, st[:, :, 1], st[:, :, 4], ALU.add))
                then(V.tensor_tensor(b, st[:, :, 1], st[:, :, 4], ALU.subtract))
                then(V.tensor_tensor(c, st[:, :, 2], st[:, :, 5], ALU.add))
                settle()
                then(V.tensor_scalar(mean[:, :], a, 0.5, None, ALU.mult))
                then(V.tensor_tensor(b, b, b, ALU.mult))
                then(V.tensor_scalar(c, c, 1.0 / C, None, ALU.mult))
                settle()
                then(V.scalar_tensor_tensor(c, b, 0.25, c, ALU.mult, ALU.add))
                settle()
                then(V.tensor_copy(b, c))
                settle()

                def inverse_root(o, v, s, n):
                    then(V.tensor_scalar(v, v, EPS, None, ALU.add))
                    settle()
                    V.tensor_copy(s, v).then_inc(S("root_asked"), 1)
                    dve.wait_ge(S("root_made"), n)
                    then(V.reciprocal(o, s))
                    settle()
                    then(V.tensor_tensor(s, o, o, ALU.mult))
                    settle()
                    then(V.tensor_tensor(s, s, v, ALU.mult))
                    settle()
                    then(V.tensor_scalar(s, s, -0.5, 1.5, ALU.mult, ALU.add))
                    settle()
                    then(V.tensor_tensor(o, o, s, ALU.mult))
                    settle()

                inverse_root(rstd[:, :], c, e, 1)
                then(V.tensor_tensor(b, b, rstd[:, :], ALU.mult))
                settle()
                then(V.tensor_tensor(b, b, rstd[:, :], ALU.mult))
                settle()
                inverse_root(rstd2[:, :], b, e, 2)

            @block.scalar
            def _(act):
                for n in range(2):
                    act.wait_ge(S("root_asked"), n + 1)
                    e = xs[:, 0, 192:192 + NT]
                    A.activation(e, e, ACT.Sqrt).then_inc(S("root_made"), 1)

            @block.tensor
            def _(pe):
                pe.wait_ge(S("ident_made"), 1)
                pe.wait_ge(S("lists_made"), 1)
                for n, lists in enumerate((ed_f[:, 0:IE], dl_f, br_f)):
                    for half in range(2):
                        if n:
                            pe.wait_ge(S("lists_copied"), 2 * n - 1 + half)
                        for q in range(8 * half, 8 * half + 8):
                            at = lists.rearrange("k (g p j) -> k g p j", g=GI, j=TG)[:, q // TG, :, q % TG]
                            mm = T.transpose(bank[2 + half][:, (q % 8) * NI:(q % 8 + 1) * NI], at, ident[0:NI, 0:NI])
                        mm.then_inc(S("lists_turned"), 1)
                pe.wait_ge(S("lnb_spread"), CT)
                for t in range(CT):
                    mm = T.matmul(bank[0][:, 0:GH], sc[:, 0, t * P:(t + 1) * P], wa_s[:, t, C + 2 * HEADS:WA],
                                  start=(t == 0), stop=(t == CT - 1))
                mm.then_inc(S("lnb_used"), 1)

        gate_cols = slice(C + 2 * HEADS, WA)
        feat = parts[:, :, :, :].rearrange("p u a b -> p u (a b)")
        with nc.Block() as block:
            @block.sync
            def _(sp):
                zero = hot[:, 0:3, :].rearrange("p a b -> p (a b)")
                sp.wait_ge(S("zeroed"), 1)
                for n in range(2):
                    sp.dma_start(part_d[n].rearrange("(t p) c -> p t c", p=P),
                                 zero[:, 0:SW].unsqueeze(1).to_broadcast([P, ROWS // P, SW])).then_inc(S("zeros_out"), 16)
                sp.dma_start(adst_d[NT * P:ROWS, :], zero[:, 0:SPLIT // 2].bitcast(BF16)).then_inc(S("zeros_out"), 16)

                def store(i, u):
                    sp.wait_ge(S("feat_made"), i + 1)
                    sp.dma_start(feat_d[bass.ds(i * P, P), :], feat[:, u, 0:AW]).then_inc(S(f"feat_out{u}"), 16)
                    if not known_below(i, 1):
                        store_hidden(i - 1, 1 - u)

                def store_hidden(i, u):
                    sp.wait_ge(S("hidT_made"), i + 1)
                    sp.dma_start(hid_d[bass.ds(i, 1), :, :].rearrange("a b c -> (a b) c"),
                                 hidT[:, u, :]).then_inc(S(f"hid_out{u}"), 16)

                sweep(sp, 0, NT, 2, 0, store)
                store_hidden(NT - 1, (NT - 1) % 2)
                for u in range(2):
                    sp.wait_ge(S(f"feat_out{u}"), 16 * ((NT + 1 - u) // 2))
                    sp.wait_ge(S(f"hid_out{u}"), 16 * ((NT + 1 - u) // 2))
                sp.wait_ge(S("lists_out"), 16 * (HEADS + 1))

            @block.vector
            def _(dve):
                def first(i, u):
                    if not known_below(i, 2):
                        dve.wait_ge(S("turned"), i - 1)
                    V.tensor_scalar(xs[:, u, :], big[:, bass.ds(i, 1), :].rearrange("p a c -> p (a c)"),
                                    mean[:, bass.ds(i, 1)], rstd[:, bass.ds(i, 1)], ALU.subtract,
                                    ALU.mult).then_inc(S("normed"), 1)

                def second(i, u):
                    dve.wait_ge(S("turned"), i + 1)
                    if not known_below(i, 2):
                        dve.wait_ge(S("keys_done"), i - 1)
                        dve.wait_ge(S("xnT_kept"), i - 1)
                    V.tensor_copy(sa[:, u, :], bank[u][:, 0:C]).then_inc(S("turn_copied"), 1)

                def third(i, u):
                    dve.wait_ge(S("feat_done"), i + 1)
                    if not known_below(i, 2):
                        dve.wait_ge(S(f"feat_out{u}"), 8 * (i - u))
                    V.tensor_copy(feat[:, u, 0:AW], bank[2 + u][:, 0:AW]).then_inc(S("feat_made"), 1)
                    V.tensor_copy(adst_s[:, bass.ds(i, 1), :].rearrange("p a h -> p (a h)"),
                                  bank[2 + u][:, AW:AW + HEADS]).then_inc(S("adst_made"), 1)
                    if not known_below(i, 2):
                        dve.wait_ge(S("hid_made"), i - 1)
                    V.scalar_tensor_tensor(sc[:, u, 0:GH], bank[2 + u][:, gate_cols], rstd2[:, bass.ds(i, 1)],
                                           b1row[:, :], ALU.mult, ALU.add).then_inc(S("hid_asked"), 1)

                def fourth(i, u):
                    dve.wait_ge(S("keys_kept"), i + 1)
                    if not known_below(i, 1):
                        dve.wait_ge(S("key_max"), i)
                    V.tensor_tensor(rmax, rmax, big[:, bass.ds(i, 1), :].rearrange("p a c -> p (a c)"),
                                    ALU.max).then_inc(S("key_max"), 1)
                    dve.wait_ge(S("hid_turned"), i + 1)
                    if not known_below(i, 2):
                        dve.wait_ge(S(f"hid_out{u}"), 8 * (i - u))
                    V.tensor_copy(hidT[:, u, :], bank[6 + u][0:GH, 0:P]).then_inc(S("hidT_made"), 1)

                def body(i, u):
                    if not isinstance(i, int) or i + 1 < NT:
                        second(i + 1, 1 - u)
                    if not isinstance(i, int) or i + 2 < NT:
                        first(i + 2, u)
                    third(i, u)
                    if not known_below(i, 1):
                        fourth(i - 1, 1 - u)

                first(0, 0)
                first(1, 1)
                second(0, 0)
                sweep(dve, 0, NT, 4, 3, body)
                fourth(NT - 1, (NT - 1) % 2)

            @block.scalar
            def _(act):
                def keep_turned(i, u):
                    act.wait_ge(S("turn_copied"), i + 1)
                    A.activation(xnT[:, bass.ds(i, 1), :].rearrange("p a c -> p (a c)"), sa[:, u, :],
                                 ACT.Copy).then_inc(S("xnT_kept"), 1)

                def body(i, u):
                    if not isinstance(i, int) or i + 1 < NT:
                        keep_turned(i + 1, 1 - u)
                    act.wait_ge(S("keys_done"), i + 1)
                    A.activation(big[:, bass.ds(i, 1), :].rearrange("p a c -> p (a c)"), bank[4 + u][:, 0:C],
                                 ACT.Identity, bias=padneg[:, bass.ds(i, 1)]).then_inc(S("keys_kept"), 1)
                    act.wait_ge(S("hid_asked"), i + 1)
                    if not known_below(i, 2):
                        act.wait_ge(S("hid_turned"), i - 1)
                    A.activation(sd[:, u, 0:GH], sc[:, u, 0:GH], ACT.Gelu).then_inc(S("hid_made"), 1)

                keep_turned(0, 0)
                sweep(act, 0, NT, 4, 3, body)

            @block.tensor
            def _(pe):
                def turn(i, u):
                    pe.wait_ge(S("normed"), i + 1)
                    if not known_below(i, 2):
                        pe.wait_ge(S("turn_copied"), i - 1)
                    for t in range(CT):
                        mm = T.transpose(bank[u][:, t * P:(t + 1) * P], xs[:, u, t * P:(t + 1) * P], ident[:, :])
                    mm.then_inc(S("turned"), 1)

                def products(i, u):
                    pe.wait_ge(S("turn_copied"), i + 1)
                    if not known_below(i, 2):
                        pe.wait_ge(S("hid_asked"), i - 1)
                    for t in range(CT):
                        mm = T.matmul(bank[2 + u][:, 0:WA], sa[:, u, t * P:(t + 1) * P], wa_s[:, t, :],
                                      start=(t == 0), stop=(t == CT - 1))
                    mm.then_inc(S("feat_done"), 1)
                    if not known_below(i, 2):
                        pe.wait_ge(S("keys_kept"), i - 1)
                    for t in range(CT):
                        mm = T.matmul(bank[4 + u][:, 0:C], sa[:, u, t * P:(t + 1) * P], wk_s[:, t, :],
                                      start=(t == 0), stop=(t == CT - 1))
                    mm.then_inc(S("keys_done"), 1)

                def hidden(i, u):
                    pe.wait_ge(S("hid_made"), i + 1)
                    if not known_below(i, 2):
                        pe.wait_ge(S("hidT_made"), i - 1)
                    T.matmul(bank[6 + u][0:GH, 0:P], sd[:, u, 0:GH], ident[:, :], start=True, stop=True).then_inc(S("hid_turned"), 1)

                def body(i, u):
                    if not isinstance(i, int) or i + 1 < NT:
                        turn(i + 1, 1 - u)
                    products(i, u)
                    if not known_below(i, 1):
                        hidden(i - 1, 1 - u)

                turn(0, 0)
                sweep(pe, 0, NT, 4, 3, body)
                hidden(NT - 1, (NT - 1) % 2)


        def gather(pool, u, g):
            for j in range(TG):
                q = g * TG + j
                pool.indirect_dma_start(
                    out=ring[:, u * TI + q, 0:AW], out_offset=None, in_=feat_d,
                    in_offset=bass.IndirectOffsetOnAxis(ap=idx[:, u, q:q + 1], axis=0),
                ).then_inc(S(f"rows_in{u}{g}"), 16)

        wq_s = hT[:, 0:4, :].rearrange("p a b -> p (a b)").rearrange("p (t n) -> p t n", t=CT)
        with nc.Block() as block:
            @block.gpsimd
            def _(pool):
                pool.partition_all_reduce(cmax, rmax, P, RMAX).then_inc(S("cmax_made"), 1)
                pool.wait_ge(S("idx_made"), 2)
                for u in range(2):
                    for g in range(GI):
                        gather(pool, u, g)

            @block.sync
            def _(sp):
                sp.dma_start(wq_s, Wqkv.rearrange("(t p) n -> p t n", p=P)[:, :, 0:C]).then_inc(S("wqv_in"), 16)
                sp.dma_start(feat[:, :, 0:C], Wqkv.rearrange("(t p) n -> p t n", p=P)[:, :, 2 * C:3 * C]
                             ).then_inc(S("wqv_in"), 16)

                def load(i, u):
                    if not known_below(i, 2):
                        sp.wait_ge(S("renormed"), i - 1)
                    sp.dma_start(xs[:, u, :], x[bass.ds(i * P, P), :]).then_inc(S(f"x_again{u}"), 16)

                sp.wait_ge(S("adst_split"), 3)
                with nc.allow_non_contiguous_dma(reason="small rows"):
                    sp.dma_start(adst_d[0:NT * P, :].rearrange("(t p) c -> p t c", p=P), adst_p[:, :, :]
                                 ).then_inc(S("adst_out"), 16)
                sweep(sp, 0, NT, 2, 0, load)
                sp.wait_ge(S("adst_out"), 16)
                sp.wait_ge(S("zeros_out"), 48)

            @block.vector
            def _(dve):
                def prepare(i, u):
                    if not known_below(i, 2):
                        dve.wait_ge(S("context_added"), i - 1)
                        dve.wait_ge(S("exp_added"), i - 1)
                    V.tensor_tensor(sa[:, u, :], big[:, bass.ds(i, 1), :].rearrange("p a c -> p (a c)"), cmax,
                                    ALU.subtract).then_inc(S("keys_less"), 1)
                    dve.wait_ge(S(f"x_again{u}"), 8 * (i - u) + 16)
                    V.tensor_scalar(sc[:, u, :], xs[:, u, :], mean[:, bass.ds(i, 1)], rstd[:, bass.ds(i, 1)],
                                    ALU.subtract, ALU.mult).then_inc(S("renormed"), 1)

                def body(i, u):
                    if not isinstance(i, int) or i + 1 < NT:
                        prepare(i + 1, 1 - u)
                    dve.wait_ge(S("keys_exp"), i + 1)
                    if not known_below(i, 1):
                        dve.wait_ge(S("exp_added"), i)
                    V.tensor_tensor(rmax, rmax, sa[:, u, :], ALU.add).then_inc(S("exp_added"), 1)

                then, settle = chain(dve, "dve3")
                for u in range(2):
                    V.tensor_copy(idx[:, u, :], srcT[:, u, :]).then_inc(S("idx_made"), 1)
                for n in range(3):
                    part = adst_p[:, :, n * HEADS:(n + 1) * HEADS]
                    V.tensor_copy(part, adst_s[:, :, :]).then_inc(S("adst_split"), 1)
                    if n < 2:
                        dve.wait_ge(S("adst_split"), n + 1)
                        then(V.tensor_tensor(adst_s[:, :, :], adst_s[:, :, :], part, ALU.subtract))
                        settle()
                dve.wait_ge(S("cmax_made"), 1)
                then(V.memset(rmax, 0.0))
                settle()
                prepare(0, 0)
                sweep(dve, 0, NT, 4, 3, body)
                dve.wait_ge(S("context_added"), NT)
                dve.wait_ge(S("exp_summed"), 1)
                V.tensor_copy(srow[0:1, 0:C], bank[2][0:1, 0:C]).then_inc(S("totals_kept"), 1)
                for t in range(CT):
                    V.tensor_copy(sc[:, t, :], bank[t][:, 0:C]).then_inc(S("totals_kept"), 1)
                then(V.memset(sd[:, 0, 0:P], 0.0))
                settle()
                for b in range(P // MIX_HD):
                    s = slice(b * MIX_HD, (b + 1) * MIX_HD)
                    then(V.memset(sd[s, 0, s], 1.0))
                dve.wait_ge(S("sums_turned"), 1)
                then(V.reciprocal(mg[:, 0, 0:CT], bank[3][:, 0:CT]))
                settle()
                for t in range(CT):
                    dve.wait_ge(S("context_made"), CT)
                    V.scalar_tensor_tensor(xs[:, 0, t * P:(t + 1) * P], bank[4][:, t * P:(t + 1) * P],
                                           mg[:, 0, t:t + 1], sd[:, 0, 0:P], ALU.mult,
                                           ALU.mult).then_inc(S("context_kept"), 1)
                dve.wait_ge(S("wq_turned"), 1)
                for t in range(CT):
                    V.tensor_copy(sa[:, t, :], bank[5 + t][:, 0:C]).then_inc(S("wq_kept"), 1)
                dve.wait_ge(S("folded"), 1)
                then(V.tensor_copy(wqc_s[:, :, :], bank[7][:, :].rearrange("p (t n) -> p t n", t=CT)))
                settle()

            @block.scalar
            def _(act):
                def body(i, u):
                    act.wait_ge(S("keys_less"), i + 1)
                    A.activation(sa[:, u, :], sa[:, u, :], ACT.Exp).then_inc(S("keys_exp"), 1)

                sweep(act, 0, NT, 2, 2, body)

            @block.tensor
            def _(pe):
                def body(i, u):
                    pe.wait_ge(S("keys_exp"), i + 1)
                    pe.wait_ge(S("renormed"), i + 1)
                    s, e = known_below(i, 1), isinstance(i, int) and i == NT - 1
                    for t in range(CT):
                        mm = T.matmul(bank[t][:, 0:C], sc[:, u, t * P:(t + 1) * P], sa[:, u, :], start=s, stop=e)
                    mm.then_inc(S("context_added"), 1)

                sweep(pe, 0, NT, 2, 2, body)
                pe.wait_ge(S("exp_added"), NT)
                T.matmul(bank[2][0:1, 0:C], ones[:, 0:1], rmax, start=True, stop=True).then_inc(S("exp_summed"), 1)
                pe.wait_ge(S("totals_kept"), 1 + CT)
                for t in range(CT):
                    mm = T.matmul(bank[3][:, t:t + 1], srow[0:1, t * P:(t + 1) * P], ones[0:1, 0:1], start=True, stop=True)
                mm.then_inc(S("sums_turned"), 1)
                pe.wait_ge(S("wqv_in"), 32)
                for t in range(CT):
                    for c in range(CT):
                        mm = T.matmul(bank[4][:, t * P:(t + 1) * P], sc[:, c, t * P:(t + 1) * P],
                                      feat[:, c, t * P:(t + 1) * P], start=(c == 0), stop=(c == CT - 1))
                    mm.then_inc(S("context_made"), 1)
                for t in range(CT):
                    for c in range(CT):
                        mm = T.transpose(bank[5 + t][:, c * P:(c + 1) * P], wq_s[:, c, t * P:(t + 1) * P], ident[:, :])
                mm.then_inc(S("wq_turned"), 1)
                pe.wait_ge(S("wq_kept"), CT)
                pe.wait_ge(S("context_kept"), CT)
                for c in range(CT):
                    for t in range(CT):
                        mm = T.matmul(bank[7][:, c * C + t * P:c * C + (t + 1) * P], sa[:, t, c * P:(c + 1) * P],
                                      xs[:, 0, t * P:(t + 1) * P], start=True, stop=True)
                mm.then_inc(S("folded"), 1)

        bk_e, bk_t, bk_m, bk_o = bank[0], bank[1], bank[4], bank[5]
        MCOL = TI * SPLIT
        slot = [slice(u * TI, (u + 1) * TI) for u in range(2)]

        def tile(a, i):
            return a[:, bass.ds(i, 1), :].rearrange("p a c -> p (a c)")

        def by_head(a):
            return a.rearrange("p (h d) -> p h d", h=HEADS)

        def steps(eng, parts_of_body):
            def body(k, u):
                for lo, hi, f in parts_of_body:
                    if not isinstance(k, int) or lo <= k < hi:
                        f(k - lo, (u - lo) % 2)
            loop_from = LAG_FF2 + 2 + (LAG_FF2 % 2)
            for k in range(loop_from):
                body(k, k % 2)
            loop_to = NI - 2 - NI % 2
            with eng.Fori(loop_from // 2, loop_to // 2) as half:
                for u in range(2):
                    body(half * 2 + u, u)
            for k in range(loop_to, NT + LAG_FF2):
                body(k, k % 2)

        EDGES = lambda f: (0, NI, f)
        WINDOWS = lambda f: (1, NI + 1, f)
        MERGE = lambda f: (LAG_MERGE, NT + LAG_MERGE, f)
        SUM = lambda f: (LAG_SUM, NT + LAG_SUM, f)
        FF1 = lambda f: (LAG_FF1, NT + LAG_FF1, f)
        FF2 = lambda f: (LAG_FF2, NT + LAG_FF2, f)

        with nc.Block() as block:
            @block.gpsimd
            def _(pool):
                def refill(k, u):
                    k = k + 2
                    for g in range(GI):
                        made, used = number(pool, k + 1), number(pool, GI * (k - 2) + g + 1)
                        pool.wait_ge(S("idx_made"), 2)
                        if g == 0:
                            pool.wait_ge(S("idx_made"), made)
                        pool.wait_ge(S("sums_done"), used)
                        gather(pool, u, g)

                steps(pool, [(2, NI, refill)])

            @block.sync
            def _(sp):
                def base(k, g):
                    return sp.value_load(base_i[0:1, bass.ds(k * GI + g, 1)], min_val=0, max_val=n_nodes - 1)

                def prefetch(k, u):
                    if not known_below(k, 1):
                        sp.wait_ge(S("hotT_made"), k)
                    sp.dma_start(dlb[:, :], dloc_d[bass.ds(k, 1), :].to_broadcast([P, IE])).then_inc(S("dlb_in"), 16)
                    first = [base(k, g) for g in range(GI)]
                    if not known_below(k, 2):
                        sp.wait_ge(S("scores_done"), k - 1)
                    for g in range(GI):
                        sp.dma_start(stat[:, u, g, :], adst_d[bass.ds(first[g], P), :]
                                     ).then_inc(S(f"stat_in{u}"), 16)

                def prefetch_breaks(k, u):
                    if not known_below(k, 1):
                        sp.wait_ge(S("max_made"), k)
                    sp.dma_start(brk[:, 1:GE + 1], brk_d[bass.ds(k, 1), :, :, :].rearrange("a g h e -> (a g h) e")
                                 ).then_inc(S("brk_in"), 16)

                def ahead(k, u):
                    prefetch(k + 1, 1 - u)

                def breaks_ahead(k, u):
                    prefetch_breaks(k + 1, 1 - u)

                def windows(k, u):
                    for g in range(GI):
                        first = base(k, g)
                        sp.wait_ge(S("sums_kept"), GI * k + g + 1)
                        if not (known_below(k, 1) and g < 2):
                            sp.wait_ge(S(f"window_out{g % 2}"), 16 * (2 * k + g // 2))
                        sp.dma_start(part_d[g % 2][bass.ds(first, P), :], wout[:, g % 2, :]
                                     ).then_inc(S(f"window_out{g % 2}"), 16)

                def load_node(i, u):
                    upto = i + LAG_MERGE - 1
                    upto = number(sp, 32 * (min(upto, NI) if isinstance(i, int) else upto))
                    free = None if known_below(i, 2) else number(sp, i - 1)
                    sp.wait_ge(S("idx_made"), 2)
                    if free is not None:
                        sp.wait_ge(S("x1_made"), free)
                        sp.wait_ge(S("merged"), free)
                        sp.wait_ge(S("gate_done"), free)
                    for n in range(2):
                        sp.wait_ge(S(f"window_out{n}"), upto)
                    rows = bass.ds(i * P, P)
                    sp.dma_start(hidT[:, u, :], hid_d[bass.ds(i, 1), :, :].rearrange("a b c -> (a b) c")
                                 ).then_inc(S(f"node_in{u}"), 16)
                    for n in range(2):
                        sp.dma_start(parts[:, u, n, :], part_d[n][rows, :]).then_inc(S(f"node_in{u}"), 16)
                    sp.dma_start(xs[:, u, :], x[rows, :]).then_inc(S(f"node_in{u}"), 16)

                prefetch(0, 0)
                prefetch_breaks(0, 0)
                steps(sp, [MERGE(load_node), (0, NI - 1, ahead), WINDOWS(windows), (0, NI - 1, breaks_ahead)])

            @block.vector
            def _(dve):
                def products(i, u):
                    dve.wait_ge(S("gate_made"), i + 1)
                    dve.wait_ge(S("mix_done"), i + 1)
                    V.scalar_tensor_tensor(sc[:, u, :], sc[:, u, :], 1.0, bk_m[:, 0:C], ALU.add,
                                           ALU.mult).then_inc(S("prod_made"), 1)

                def one_hots(k, u):
                    dve.wait_ge(S("dlb_in"), 16 * k + 16)
                    if not known_below(k, 1):
                        dve.wait_ge(S("scores_done"), k)
                    V.tensor_scalar(hotT[:, :], dlb[:, :], iota_col[:, 0:1], None, ALU.is_equal
                                    ).then_inc(S("hotT_made"), 1)

                def hots_ahead(k, u):
                    one_hots(k + 1, 1 - u)

                def edge_hot(k, g):
                    if not known_below(k, 1):
                        dve.wait_ge(S("sums_done"), GI * (k - 1) + g + 1)
                    tiles = slice(g * TG, (g + 1) * TG)
                    V.tensor_tensor(hot[:, tiles, :], iota_row[:, :].unsqueeze(1).to_broadcast([P, TG, P]),
                                    dlocT[:, bass.ds(k, 1), tiles].rearrange("p a q -> p (a q)").unsqueeze(2)
                                    .to_broadcast([P, TG, P]), ALU.is_equal).then_inc(S("hot_made"), 1)

                def edge_hots(k, u):
                    for g in range(GI):
                        edge_hot(k, g)

                def merge_weights(i, u):
                    m = mg[:, u, :]
                    dve.wait_ge(S(f"node_in{u}"), 32 * (i - u) + 64)
                    V.tensor_scalar(m[:, 0:2], parts[:, u, :, SW - 1], 1.0, BIG, ALU.subtract, ALU.mult
                                    ).then_inc(S("merge_a"), 1)
                    dve.wait_ge(S("merge_a"), i + 1)
                    V.tensor_tensor(m[:, 2:10].rearrange("p (n h) -> p n h", n=2), parts[:, u, :, C + HEADS:C + 2 * HEADS],
                                    m[:, 0:2].unsqueeze(2).to_broadcast([P, 2, HEADS]), ALU.add).then_inc(S("merge_b"), 1)
                    dve.wait_ge(S("merge_b"), i + 1)
                    V.tensor_tensor(m[:, 10:14], m[:, 2:6], m[:, 6:10], ALU.max).then_inc(S("merge_c"), 1)
                    dve.wait_ge(S("merge_c"), i + 1)
                    V.tensor_tensor(m[:, 14:22].rearrange("p (n h) -> p n h", n=2),
                                    m[:, 2:10].rearrange("p (n h) -> p n h", n=2),
                                    m[:, 10:14].unsqueeze(1).to_broadcast([P, 2, HEADS]), ALU.subtract
                                    ).then_inc(S("merge_asked"), 1)

                def scores(k, u):
                    to = lk[:, u, :, :].rearrange("p j x -> p (j x)")
                    dve.wait_ge(S("scores_done"), k + 1)
                    V.tensor_reduce(to.rearrange("p (q h) -> p q h", h=HEADS),
                                    bk_e[:, 0:MCOL].rearrange("p (q n h) -> p q h n", n=3, h=HEADS), AX_X, ALU.add
                                    ).then_inc(S("dst_summed"), 1)
                    for g in range(GI):
                        dve.wait_ge(S(f"rows_in{u}{g}"), 32 * (k - u) + 64)
                    if not (isinstance(k, int) and k + 2 >= NI):
                        V.tensor_copy(idx[:, u, :], srcT[:, bass.ds(k + 2, 1), :].rearrange("p a q -> p (a q)")
                                      ).then_inc(S("idx_made"), 1)
                    V.tensor_copy(ring[:, slot[u], SW - 1], lastT[:, bass.ds(k, 1), :].rearrange("p a q -> p (a q)")
                                  ).then_inc(S("lastcol_made"), 1)
                    dve.wait_ge(S("dst_summed"), k + 1)
                    four = lk[:, u, :, :].rearrange("p j (g h) -> p j g h", g=GI)
                    V.tensor_tensor(four, four, ring[:, slot[u], C:C + HEADS].rearrange("p (g j) h -> p j g h", g=GI),
                                    ALU.add).then_inc(S("src_added"), 1)
                    dve.wait_ge(S("src_added"), k + 1)
                    V.scalar_tensor_tensor(to, to, 0.2, to, ALU.mult, ALU.max).then_inc(S("leaky_made"), 1)

                def maxima(k, u):
                    dve.wait_ge(S("scores_turned"), k + 1)
                    dve.wait_ge(S("brk_in"), 16 * k + 16)
                    if not known_below(k, 1):
                        dve.wait_ge(S("max_turned"), k)
                    V.tensor_tensor_scan(forth[:, :], brk[:, 0:GE], bk_t[0:TI, :], LOWEST, ALU.add, ALU.max
                                         ).then_inc(S("forth_made"), 1)
                    dve.wait_ge(S("forth_made"), k + 1)
                    V.tensor_tensor_scan(srow[:, :][:, ::-1], brk[:, 1:GE + 1][:, ::-1], forth[:, :][:, ::-1],
                                         LOWEST, ALU.add, ALU.max).then_inc(S("max_made"), 1)

                def differences(k, u):
                    dve.wait_ge(S("max_turned"), k + 1)
                    if not known_below(k, 1):
                        dve.wait_ge(S("ex_made"), k)
                    V.tensor_tensor(diff[:, :, :].rearrange("p j x -> p (j x)"),
                                    lk[:, u, :, :].rearrange("p j x -> p (j x)"), bk_e[:, MCOL:MCOL + TG * TI],
                                    ALU.subtract).then_inc(S("diff_made"), 1)
                    last = lastT[:, bass.ds(k, 1), :].rearrange("p a q -> p (a q)")
                    V.tensor_tensor(ring[:, slot[u], C + HEADS:C + 2 * HEADS].rearrange("p (g j) h -> p j g h", g=GI),
                                    bk_e[:, MCOL:MCOL + TG * TI].rearrange("p (j g h) -> p j g h", j=TG, g=GI),
                                    last.rearrange("p (g j) -> p j g", g=GI).unsqueeze(3)
                                    .to_broadcast([P, TG, GI, HEADS]), ALU.mult).then_inc(S("maxcol_made"), 1)

                def outputs(i, u):
                    dve.wait_ge(S("ff2_done"), i + 1)
                    V.tensor_tensor(tile(big, i), bk_o[:, 0:C], b2row[:, :], ALU.add).then_inc(S("out_kept"), 1)

                def messages(k, u):
                    dve.wait_ge(S("ex_made"), k + 1)
                    for g in range(GI):
                        rows = ring[:, u * TI + g * TG:u * TI + (g + 1) * TG, :]
                        feats = rows[:, :, 0:C].rearrange("p q (h d) -> p q h d", h=HEADS)
                        V.tensor_tensor(feats, feats, rows[:, :, C:C + HEADS].unsqueeze(3)
                                        .to_broadcast([P, TG, HEADS, HD]), ALU.mult).then_inc(S("scaled"), 1)

                def merge(i, u):
                    m = mg[:, u, :]
                    two = lambda a: a.rearrange("p (n h) -> p n h", n=2)
                    dve.wait_ge(S("merge_exp"), i + 1)
                    V.tensor_tensor(two(m[:, 30:38]), two(m[:, 22:30]), parts[:, u, :, C:C + HEADS], ALU.mult
                                    ).then_inc(S("merge_d"), 1)
                    dve.wait_ge(S("merge_d"), i + 1)
                    V.tensor_tensor(m[:, 38:42], m[:, 30:34], m[:, 34:38], ALU.add).then_inc(S("merge_e"), 1)
                    dve.wait_ge(S("merge_e"), i + 1)
                    V.scalar_tensor_tensor(m[:, 42:46], m[:, 38:42], 0.0, m[:, 38:42], ALU.is_equal, ALU.add
                                           ).then_inc(S("merge_f"), 1)
                    dve.wait_ge(S("merge_f"), i + 1)
                    V.reciprocal(m[:, 46:50], m[:, 42:46]).then_inc(S("merge_g"), 1)
                    dve.wait_ge(S("merge_g"), i + 1)
                    V.tensor_tensor(two(m[:, 50:58]), two(m[:, 22:30]), m[:, 46:50].unsqueeze(1)
                                    .to_broadcast([P, 2, HEADS]), ALU.mult).then_inc(S("merge_h"), 1)
                    dve.wait_ge(S("merge_h"), i + 1)
                    for n, to in enumerate((sa[:, u, :], parts[:, u, 1, 0:C])):
                        V.tensor_tensor(by_head(to), by_head(parts[:, u, n, 0:C]),
                                        m[:, 50 + 4 * n:54 + 4 * n].unsqueeze(2).to_broadcast([P, HEADS, HD]), ALU.mult
                                        ).then_inc(S("merge_i"), 1)
                    dve.wait_ge(S("merge_i"), 2 * i + 2)
                    V.tensor_tensor(sa[:, u, :], sa[:, u, :], parts[:, u, 1, 0:C], ALU.add).then_inc(S("merged"), 1)
                    dve.wait_ge(S("merged"), i + 1)
                    V.tensor_tensor(sa[:, u, :], sa[:, u, :], gbrow[:, :], ALU.add).then_inc(S("gnn_made"), 1)

                def normed(i, u):
                    dve.wait_ge(S("rstd_made"), i + 1)
                    if not known_below(i, 1):
                        dve.wait_ge(S("xn2_turned"), i)
                    V.tensor_scalar(xn2, sd[:, u, :], bn[:, u, 6:7], bn[:, u, 9:10], ALU.subtract, ALU.mult
                                    ).then_inc(S("xn2_made"), 1)
                    dve.wait_ge(S("xn2_made"), i + 1)
                    if not known_below(i, 1):
                        dve.wait_ge(S("routed"), i)
                    V.tensor_tensor_reduce(junk[:, :], xn2, wrrow[:, :], 1.0, brc[:, 0:1], ALU.mult, ALU.add,
                                           mg[:, u, 60:61]).then_inc(S("route_made"), 1)
                    V.tensor_tensor(tile(xnT, i), sd[:, u, :], xn2, ALU.add).then_inc(S("rest_made"), 1)
                    dve.wait_ge(S("route_made"), i + 1)
                    V.tensor_tensor(wts[:, bass.ds(i, 1)], mg[:, u, 60:61], padneg[:, bass.ds(i, 1)], ALU.add
                                    ).then_inc(S("routed"), 1)

                def sums(i, u):
                    dve.wait_ge(S("proj_done"), i + 1)
                    V.tensor_tensor(sd[:, u, :], bk_t[:, 0:C], prow[:, :], ALU.add).then_inc(S("proj_read"), 1)
                    dve.wait_ge(S("proj_read"), i + 1)
                    dve.wait_ge(S("gnn_tanh"), i + 1)
                    V.scalar_tensor_tensor(sd[:, u, :], sa[:, u, :], 0.5, sd[:, u, :], ALU.mult, ALU.add
                                           ).then_inc(S("gnn_added"), 1)
                    dve.wait_ge(S("gnn_added"), i + 1)
                    V.tensor_tensor(sd[:, u, :], sd[:, u, :], xs[:, u, :], ALU.add).then_inc(S("x1_made"), 1)
                    dve.wait_ge(S("x1_made"), i + 1)
                    V.bn_stats(bn[:, u, 0:6], sd[:, u, :]).then_inc(S("bn_made"), 1)
                    dve.wait_ge(S("idx_made"), 2)
                    dve.wait_ge(S("bn_made"), i + 1)
                    V.bn_aggr(bn[:, u, 6:8], bn[:, u, 0:6]).then_inc(S("var_made"), 1)

                one_hots(0, 0)
                steps(dve, [WINDOWS(messages), SUM(products), EDGES(scores), MERGE(merge_weights), FF1(normed),
                            MERGE(merge), EDGES(maxima), EDGES(edge_hots), FF2(outputs), EDGES(differences),
                            (0, NI - 1, hots_ahead), SUM(sums)])

            @block.scalar
            def _(act):
                def exps(k, u):
                    act.wait_ge(S("diff_made"), k + 1)
                    A.activation(ring[:, slot[u], C:C + HEADS].rearrange("p (g j) h -> p j g h", g=GI),
                                 diff[:, :, :].rearrange("p j (g h) -> p j g h", g=GI), ACT.Exp).then_inc(S("ex_made"), 1)

                def merge_exp(i, u):
                    act.wait_ge(S("merge_asked"), i + 1)
                    A.activation(mg[:, u, 22:30], mg[:, u, 14:22], ACT.Exp).then_inc(S("merge_exp"), 1)

                def inverse_root(i, u):
                    act.wait_ge(S("var_made"), i + 1)
                    A.activation(bn[:, u, 8:9], bn[:, u, 7:8], ACT.Ln, bias=epsc[:, 0:1]).then_inc(S("ln_made"), 1)
                    act.wait_ge(S("ln_made"), i + 1)
                    A.activation(bn[:, u, 9:10], bn[:, u, 8:9], ACT.Exp, scale=-0.5).then_inc(S("rstd_made"), 1)

                def keep_one(k, g):
                    act.wait_ge(S("sums_done"), GI * k + g + 1)
                    if not (known_below(k, 1) and g < 2):
                        act.wait_ge(S(f"window_out{g % 2}"), 16 * (2 * k + g // 2))
                    A.activation(wout[:, g % 2, :], bank[2 + g % 2][:, 0:SW], ACT.Copy).then_inc(S("sums_kept"), 1)

                def keep_first(k, u):
                    keep_one(k, 0)

                def keep_others(k, u):
                    for g in range(1, GI):
                        keep_one(k, g)

                def gates(i, u):
                    act.wait_ge(S("gate_done"), i + 1)
                    if not known_below(i, 2):
                        act.wait_ge(S("proj_done"), i - 1)
                    for t in range(CT):
                        a = A.activation(sc[:, u, t * P:(t + 1) * P], bk_m[:, C + t * P:C + (t + 1) * P], ACT.Tanh,
                                         bias=hbg2[:, t:t + 1], scale=0.5)
                    a.then_inc(S("gate_made"), 1)
                    act.wait_ge(S("gnn_made"), i + 1)
                    A.activation(sa[:, u, :], sa[:, u, :], ACT.Tanh, scale=0.5).then_inc(S("gnn_tanh"), 1)

                def keep_turned(i, u):
                    act.wait_ge(S("xn2_turned"), i + 1)
                    if not known_below(i, 1):
                        act.wait_ge(S("ff1_done"), FT * i)
                    A.activation(xn2T, bank[7][:, 0:C], ACT.Copy).then_inc(S("xn2T_kept"), 1)

                def hidden(i, u):
                    if not known_below(i, 1):
                        act.wait_ge(S("ff2_done"), i)
                    for m in range(FT):
                        act.wait_ge(S("ff1_done"), FT * i + m // 4 * 4 + 4)
                        A.activation(hT[:, m, :], bank[6 + m // 4][:, (m % 4) * P:(m % 4 + 1) * P], ACT.Gelu_apprx_tanh,
                                     bias=b1_s[:, m:m + 1]).then_inc(S("gelu_made"), 1)

                steps(act, [FF1(inverse_root), WINDOWS(keep_first), MERGE(merge_exp), WINDOWS(keep_others),
                            FF1(keep_turned), MERGE(gates), EDGES(exps), FF1(hidden)])

            @block.tensor
            def _(pe):
                def mixer(i, u):
                    if not known_below(i, 1):
                        pe.wait_ge(S("prod_made"), i)
                    for t in range(CT):
                        for c in range(CT):
                            mm = T.matmul(bk_m[:, t * P:(t + 1) * P], wqc_s[:, c, t * P:(t + 1) * P],
                                          xnT[:, bass.ds(i, 1), c * P:(c + 1) * P].rearrange("p a c -> p (a c)"),
                                          start=(c == 0), stop=(c == CT - 1))
                    mm.then_inc(S("mix_done"), 1)
                    pe.wait_ge(S(f"node_in{u}"), 32 * (i - u) + 64)
                    if not known_below(i, 1):
                        pe.wait_ge(S("gate_made"), i)
                    for t in range(CT):
                        mm = T.matmul(bk_m[:, C + t * P:C + (t + 1) * P], wg2_s[:, t * P:(t + 1) * P], hidT[:, u, :],
                                      start=True, stop=True)
                    mm.then_inc(S("gate_done"), 1)

                def scores(k, u):
                    pe.wait_ge(S("hotT_made"), k + 1)
                    pe.wait_ge(S(f"stat_in{u}"), 32 * (k - u) + 64)
                    if not known_below(k, 1):
                        pe.wait_ge(S("maxcol_made"), k)
                    for g in range(GI):
                        for j in range(TG):
                            q = j * GI + g
                            mm = T.matmul(bk_e[:, q * SPLIT:(q + 1) * SPLIT], hotT[:, (g * TG + j) * P:(g * TG + j + 1) * P],
                                          stat[:, u, g, :], start=True, stop=True)
                    mm.then_inc(S("scores_done"), 1)

                def turn_scores(k, u):
                    pe.wait_ge(S("leaky_made"), k + 1)
                    if isinstance(k, int) and k <= LAG_SUM:
                        if k:
                            pe.wait_ge(S("forth_made"), k)
                    else:
                        pe.wait_ge(S("proj_read"), k - LAG_SUM)
                    for j in range(TG):
                        mm = T.transpose(bk_t[0:TI, :].rearrange("r (e j) -> r j e", j=TG)[:, j, :], lk[:, u, j, :],
                                         ident[:, :])
                    mm.then_inc(S("scores_turned"), 1)

                def turn_maxima(k, u):
                    pe.wait_ge(S("max_made"), k + 1)
                    for j in range(TG):
                        mm = T.matmul(bk_e[:, MCOL + j * TI:MCOL + (j + 1) * TI],
                                      srow[:, :].rearrange("r (e j) -> r j e", j=TG)[:, j, :],
                                      ident[0:TI, 0:TI], start=True, stop=True)
                    mm.then_inc(S("max_turned"), 1)

                def ff2(i, u):
                    pe.wait_ge(S("gelu_made"), FT * i + FT)
                    if not known_below(i, 1):
                        pe.wait_ge(S("out_kept"), i)
                    for m in range(FT):
                        mm = T.matmul(bk_o[:, 0:C], hT[:, m, :], w2_s[:, m, :], start=(m == 0), stop=(m == FT - 1))
                    mm.then_inc(S("ff2_done"), 1)

                def first_sums(k, u):
                    pe.wait_ge(S("lastcol_made"), k + 1)
                    pe.wait_ge(S("maxcol_made"), k + 1)
                    window_sums(k, u, (0, 1))

                def other_sums(k, u):
                    window_sums(k, u, (2, 3))

                def window_sums(k, u, groups):
                    for g in groups:
                        pe.wait_ge(S("hot_made"), GI * k + g + 1)
                        pe.wait_ge(S("scaled"), GI * k + g + 1)
                        if not (known_below(k, 1) and g < 2):
                            pe.wait_ge(S("sums_kept"), GI * k + g - 1)
                        for j in range(TG):
                            q = u * TI + g * TG + j
                            mm = T.matmul(bank[2 + g % 2][:, 0:SW], hot[:, g * TG + j, :], ring[:, q, 0:SW],
                                          start=(j == 0), stop=(j == TG - 1))
                        mm.then_inc(S("sums_done"), 1)

                def project(i, u):
                    pe.wait_ge(S("prod_made"), i + 1)
                    if not known_below(i, 1):
                        pe.wait_ge(S("proj_read"), i)
                    if not (isinstance(i, int) and i + LAG_SUM >= NI):
                        pe.wait_ge(S("forth_made"), i + LAG_SUM + 1)
                    for t in range(CT):
                        mm = T.matmul(bk_t[:, 0:C], sc[:, u, t * P:(t + 1) * P], wproj_s[:, t, :],
                                      start=(t == 0), stop=(t == CT - 1))
                    mm.then_inc(S("proj_done"), 1)

                def turn_normed(i, u):
                    pe.wait_ge(S("xn2_made"), i + 1)
                    if not known_below(i, 1):
                        pe.wait_ge(S("gelu_made"), FT * i)
                    for t in range(CT):
                        mm = T.transpose(bank[7][:, t * P:(t + 1) * P], xn2[:, t * P:(t + 1) * P], ident[:, :])
                    mm.then_inc(S("xn2_turned"), 1)

                def ff1(i, u):
                    pe.wait_ge(S("xn2T_kept"), i + 1)
                    for m in range(FT):
                        if m % 4 == 0 and not known_below(i, 1):
                            pe.wait_ge(S("gelu_made"), FT * (i - 1) + m + 4)
                        for t in range(CT):
                            mm = T.matmul(bank[6 + m // 4][:, (m % 4) * P:(m % 4 + 1) * P], w1_s[:, t, m * P:(m + 1) * P],
                                          xn2T[:, t * P:(t + 1) * P], start=(t == 0), stop=(t == CT - 1))
                        mm.then_inc(S("ff1_done"), 1)

                steps(pe, [EDGES(scores), WINDOWS(first_sums), MERGE(mixer), WINDOWS(other_sums), EDGES(turn_scores),
                           FF1(turn_normed), FF2(ff2), EDGES(turn_maxima), SUM(project), FF1(ff1)])

        ROUNDS = 8
        tail = flat_ring[:, 0:64 * P].rearrange("p (a b) -> p a b", b=P)
        lower, jtab = tail[:, 0, :], tail[:, 1, 0:15].bitcast(I32)
        v_s = tail[:, 2, 0:NT]
        cmp_s = tail[:, 4:12, :].rearrange("p a b -> p (a b)")[:, 0:15 * NT].rearrange("p (j t) -> p j t", j=15)
        cand = tail[:, 12, 0:15]
        cnt = tail[:, 13, 0:15]
        one = lambda n: tail[:, 14, n:n + 1]
        t_bits, sign, want, dig, more, thr, need = (one(n) for n in range(7))
        dig_i = one(8)
        eq_s, gt_s, pre_s, off_s, sel_s = (tail[:, 16 + n, 0:NT] for n in range(5))
        tot_s = tail[:, 21, 0:NT]
        n_steps = ROUNDS + 2
        with nc.Block() as block:
            @block.gpsimd
            def _(pool):
                pool.iota(hotT[:, 0:30].bitcast(I32), pattern=[[1, 15]], base=1, channel_multiplier=0
                          ).then_inc(S("digits_made"), 1)

            @block.tensor
            def _(pe):
                for n in range(n_steps):
                    pe.wait_ge(S("counted"), n + 1)
                    T.matmul(bank[n % 2][:, 0:15], ones[:, :], cnt, start=True, stop=True).then_inc(S("totalled"), 1)
                pe.wait_ge(S("ties_made"), 1)
                T.matmul(bank[2][:, 0:NT], lower, eq_s, start=True, stop=True)
                T.matmul(bank[3][:, 0:NT], ones[:, :], eq_s, start=True, stop=True).then_inc(S("ties_counted"), 1)

            @block.vector
            def _(dve):
                then, settle = chain(dve, "dve5")
                n_counts = [0]

                def total():
                    settle()
                    V.tensor_copy(off_s[:, 0:1], cnt[:, 0:1]).then_inc(S("counted"), 1)
                    n_counts[0] += 1
                    dve.wait_ge(S("totalled"), n_counts[0])
                    return bank[(n_counts[0] - 1) % 2]

                then(V.tensor_scalar(lower, iota_row[:, :], iota_col[:, 0:1], None, ALU.is_gt))
                then(V.memset(cnt, 0.0))
                settle()
                then(V.tensor_scalar(sel_s, wts[:, :], 0.0, 0.0, ALU.is_ge, ALU.add, accum_out=cnt[:, 0:1]))
                b = total()
                then(V.tensor_scalar(dig, b[:, 0:1], float(KEEP), None, ALU.is_ge))
                settle()
                then(V.tensor_scalar(sign, dig, 2.0, -1.0, ALU.mult, ALU.add))
                then(V.tensor_scalar(want, dig, float(2 * KEEP - NT * P - 1), float(NT * P + 1 - KEEP), ALU.mult, ALU.add))
                settle()
                then(V.tensor_scalar(v_s, wts[:, :], sign, None, ALU.mult))
                then(V.memset(t_bits, 0.0))
                dve.wait_ge(S("digits_made"), 1)
                for r in range(ROUNDS):
                    shift = 28 - 4 * r
                    J = 7 if r == 0 else 15
                    settle()
                    then(V.tensor_scalar(jtab, hotT[:, 0:30].bitcast(I32), shift, None, ALU.logical_shift_left))
                    settle()
                    then(V.tensor_tensor(cand[:, 0:J].bitcast(I32), jtab[:, 0:J], t_bits.bitcast(I32).to_broadcast([P, J]),
                                         ALU.bitwise_or))
                    settle()
                    then(V.tensor_tensor(cmp_s[:, 0:J, :], v_s.unsqueeze(1).to_broadcast([P, J, NT]),
                                         cand[:, 0:J].unsqueeze(2).to_broadcast([P, J, NT]), ALU.is_ge))
                    settle()
                    then(V.tensor_reduce(cnt[:, 0:J], cmp_s[:, 0:J, :], AX_X, ALU.add))
                    b = total()
                    then(V.tensor_scalar(sel_s[:, 0:J], b[:, 0:J], want, 0.0, ALU.is_ge, ALU.add, accum_out=dig))
                    settle()
                    then(V.tensor_scalar(dig_i.bitcast(I32), dig, float(1 << shift), None, ALU.mult))
                    settle()
                    then(V.tensor_tensor(t_bits.bitcast(I32), t_bits.bitcast(I32), dig_i.bitcast(I32), ALU.bitwise_or))
                settle()
                then(V.tensor_tensor(thr, t_bits, sign, ALU.mult))
                settle()
                then(V.tensor_scalar(gt_s, wts[:, :], thr, 0.0, ALU.is_gt, ALU.add, accum_out=cnt[:, 0:1]))
                V.tensor_scalar(eq_s, wts[:, :], thr, None, ALU.is_equal).then_inc(S("ties_made"), 1)
                b = total()
                then(V.tensor_scalar(need, b[:, 0:1], -1.0, float(KEEP), ALU.mult, ALU.add))
                dve.wait_ge(S("ties_counted"), 1)
                then(V.tensor_copy(tot_s, bank[3][:, 0:NT]))
                then(V.memset(sel_s, 0.0))
                settle()
                then(V.tensor_tensor_scan(pre_s, tot_s, sel_s, 0.0, ALU.add, ALU.add))
                settle()
                then(V.tensor_tensor(pre_s, pre_s, tot_s, ALU.subtract))
                settle()
                then(V.tensor_tensor(pre_s, pre_s, bank[2][:, 0:NT], ALU.add))
                settle()
                then(V.tensor_scalar(pre_s, pre_s, need, None, ALU.is_lt))
                settle()
                then(V.tensor_tensor(pre_s, pre_s, eq_s, ALU.mult))
                settle()
                then(V.tensor_tensor(sel_s, pre_s, gt_s, ALU.add))
                settle()
                then(V.tensor_tensor(sel_s, sel_s, wts[:, :], ALU.mult))
                settle()
                for t in range(NT):
                    V.scalar_tensor_tensor(xnT[:, t, :], big[:, t, :], sel_s[:, t:t + 1], xnT[:, t, :], ALU.mult, ALU.add
                                           ).then_inc(S("result_made"), 1)

            @block.sync
            def _(sp):
                to = out.rearrange("(t p) c -> p t c", p=P)
                for n in range(7):
                    sp.wait_ge(S("result_made"), (n + 1) * XC)
                    sp.dma_start(to[:, n * XC:(n + 1) * XC, :], xnT[:, n * XC:(n + 1) * XC, :]).then_inc(S("result_out"), 16)
                sp.wait_ge(S("result_out"), 16 * 7)


_INS = ["x", "src", "dst", "L0_gnn_W", "L0_gnn_att_src", "L0_gnn_att_dst", "L0_gnn_bias", "L0_mix_Wqkv",
        "L0_mix_Wproj", "L0_mix_bproj", "L0_mix_ln_g", "L0_mix_ln_b", "L0_mix_Wg1", "L0_mix_bg1", "L0_mix_Wg2",
        "L0_mix_bg2", "L0_ffn_wr", "L0_ffn_br", "L0_ffn_w1", "L0_ffn_b1", "L0_ffn_w2", "L0_ffn_b2"]
FAR = 1 << 20


def kernel(**inputs):
    import concourse.bacc as bacc
    from concourse.bass_utils import run_bass_kernel_spmd

    nc = bacc.Bacc("TRN2", target_bir_lowering=False, num_devices=1, dynamic_dma_scratch_size=4096)
    n_nodes, n_edges = inputs["x"].shape[0], inputs["src"].shape[0]
    padded = {"x": (-(-n_nodes // P) * P, 0), "src": (-(-n_edges // IE) * IE, 0), "dst": (-(-n_edges // IE) * IE, FAR)}
    arrays, args = {}, []
    for name in _INS:
        a = np.ascontiguousarray(inputs[name])
        if name in padded:
            rows, value = padded[name]
            full = np.full((rows, *a.shape[1:]), value, a.dtype)
            full[:a.shape[0]] = a
            a = full
        arrays[f"in_{name}"] = a
        args.append(nc.dram_tensor(f"in_{name}", a.shape, mybir.dt.from_np(a.dtype), kind="ExternalInput").ap())
    out = nc.dram_tensor("out_0", arrays["in_x"].shape, F32, kind="ExternalOutput").ap()
    gps_layer(nc, *args, out, n_nodes)
    r = run_bass_kernel_spmd(nc, [arrays], core_ids=[0])
    return r.results[0]["out_0"][:n_nodes]
```

```python
from contextlib import ExitStack

import numpy as np

import concourse.bass as bass
from concourse import mybir

F32 = mybir.dt.float32
BF16 = mybir.dt.bfloat16
I32 = mybir.dt.int32
ALU = mybir.AluOpType
ACT = mybir.ActivationFunctionType
AX_X = mybir.AxisListType.X
RMAX = bass.bass_isa.ReduceOp.max
RADD = bass.bass_isa.ReduceOp.add

P = 128
C = 256
CT = C // P
HEADS = 4
HD = C // HEADS
GH = 64
FF = 1024
FT = FF // P
MIX_HD = 32
EPS = 1e-5
BIG = 1e30
LOWEST = -3e38

TG = 4
GI = 4
TI = TG * GI
GE = TG * P
IE = TI * P
AW = C + HEADS
WA = C + 2 * HEADS + GH
SPLIT = 3 * HEADS
RW = 266
SW = C + 2 * HEADS + 1
LAG_MERGE, LAG_SUM, LAG_FF1, LAG_FF2 = 6, 7, 8, 9


def sweep(eng, lo, hi, peel, rest, body, n=2):
    i = lo
    while i < hi and (i < lo + peel or i % n):
        body(i, i % n)
        i += 1
    times = max(hi - rest - i, 0) // n
    if times < 2:
        times = 0
    else:
        with eng.Fori(i // n, i // n + times) as some:
            for u in range(n):
                body(some * n + u, u)
    for i in range(i + n * times, hi):
        body(i, i % n)


def known_below(i, n):
    return isinstance(i, int) and i < n


def number(eng, v):
    return v if isinstance(v, int) else eng.snap(eng.to_reg(v))


def gps_layer(nc, x, src, dst, W, att_src, att_dst, gnn_bias, Wqkv, Wproj, bproj, ln_g, ln_b, Wg1, bg1, Wg2, bg2,
              wr, br, w1, b1, w2, b2, out, n_nodes):
    NT = x.shape[0] // P
    NI = src.shape[0] // IE
    NG = NI * GI
    KEEP = n_nodes // 2 - 1
    ROWS = NT * P + P
    XC = NT // 7

    with ExitStack() as ctx:
        def sb(name, shape, dt=F32):
            return ctx.enter_context(nc.sbuf_tensor(name, shape, dt))

        named = {}

        def S(name):
            if name not in named:
                named[name] = ctx.enter_context(nc.semaphore(name))
            return named[name]

        bank = [ctx.enter_context(nc.psum_tensor(f"bank{n}", [P, 512], F32)) for n in range(8)]

        def scratch(name, shape, dt=F32):
            return nc.dram_tensor(name, shape, dt, kind="Internal").ap()

        feat_d = scratch("feat_d", [NT * P, AW])
        adst_d = scratch("adst_d", [ROWS, SPLIT], BF16)
        hid_d = scratch("hid_d", [NT, GH, P])
        parts_d = scratch("parts_d", [2, ROWS, SW])
        part_d = [parts_d[n, :, :] for n in range(2)]
        brk_d = scratch("brk_d", [NI, GI, HEADS, GE])
        dloc_d = scratch("dloc_d", [NI, IE], BF16)

        xnT = sb("xnT", [P, NT, C])
        big = sb("big", [P, NT, C])
        ring = sb("ring", [P, 2 * TI, RW])
        hot = sb("hot", [P, TI, P])
        hotT = sb("hotT", [P, IE], BF16)
        ident = sb("ident", [P, P])
        ones = sb("ones", [P, P])
        iota_row = sb("iota_row", [P, P])
        iota_col = sb("iota_col", [P, 1])
        iota_i = sb("iota_i", [P, P], I32)
        iota_ci = sb("iota_ci", [P, 1], I32)
        srcT = sb("srcT", [P, NI, TI], I32)
        dlocT = sb("dlocT", [P, NI, TI], BF16)
        lastT = sb("lastT", [P, NI, TI], BF16)
        idx = sb("idx", [P, 2, TI], I32)
        write_i = sb("write_i", [1, NG], I32)
        bad = sb("bad", [P, 4])
        bad_i = sb("bad_i", [1, 1], I32)
        gen_i = sb("gen_i", [P, 3], I32)
        base_i = sb("base_i", [1, NG], I32)
        adst_s = sb("adst_s", [P, NT, HEADS])
        adst_p = sb("adst_p", [P, NT, SPLIT], BF16)
        stat = sb("stat", [P, 2, GI, SPLIT], BF16)
        lk = sb("lk", [P, 2, TG, TI])
        diff = sb("diff", [P, TG, TI])
        brk = sb("brk", [TI, GE + 1])
        dlb = sb("dlb", [P, IE], BF16)
        w1_s = sb("w1_s", [P, CT, FF])
        w2_s = sb("w2_s", [P, FT, C])
        b1_s = sb("b1_s", [P, FT])
        wproj_s = sb("wproj_s", [P, CT, C])
        wqc_s = sb("wqc_s", [P, CT, C])
        wg2_s = sb("wg2_s", [GH, C])
        hbg2 = sb("hbg2", [P, CT])
        lng = sb("lng", [P, CT])
        lnb = sb("lnb", [P, CT])
        b1row = sb("b1row", [P, GH])
        gbrow = sb("gbrow", [P, C])
        prow = sb("prow", [P, C])
        wrrow = sb("wrrow", [P, C])
        b2row = sb("b2row", [P, C])
        brc = sb("brc", [P, 1])
        epsc = sb("epsc", [P, 1])
        padneg = sb("padneg", [P, NT])
        wts = sb("wts", [P, NT])
        rstd = sb("rstd", [P, NT])
        rstd2 = sb("rstd2", [P, NT])
        mean = sb("mean", [P, NT])
        xs = sb("xs", [P, 2, C])
        sa = sb("sa", [P, 2, C])
        sc = sb("sc", [P, 2, C])
        sd = sb("sd", [P, 2, C])
        parts = sb("parts", [P, 2, 2, SW])
        late = sb("late", [P, 3 * C])
        xn2, xn2T = late[:, 0:C], late[:, C:2 * C]
        junk = sb("junk", [P, C], BF16)
        hidT = sb("hidT", [GH, 2, P])
        hT = sb("hT", [P, FT, P])
        forth = sb("forth", [TI, GE])
        srow = sb("srow", [TI, GE])
        wout = sb("wout", [P, 2, SW])
        mg = sb("mg", [P, 2, 64])
        bn = sb("bn", [P, 2, 10])

        wk_s = hT[:, 0:4, :].rearrange("p a b -> p (a b)").rearrange("p (t n) -> p t n", t=CT)
        st = hT[:, 4:8, :].rearrange("p a b -> p (a b)")[:, 0:6 * NT].rearrange("p (t s) -> p t s", s=6)
        wa_s = late[:, 0:CT * WA].rearrange("p (t n) -> p t n", t=CT)
        rmax = wout[:, 0, 0:C]
        cmax, exp_sum, totals = late[:, 0:C], late[:, C:2 * C], late[0:1, 2 * C:3 * C]

        def row(v, n):
            return v.rearrange("(a n) -> a n", a=1).to_broadcast([P, n])

        flat_ring = ring[:, :, :].rearrange("p a b -> p (a b)")
        ed_i = flat_ring.bitcast(I32)[0:NI, 0:2 * IE]
        ed_f = xnT[:, 2:18, :].rearrange("p a b -> p (a b)")[0:NI, 0:2 * IE]
        br_f = flat_ring[0:NI, 2 * IE:3 * IE]
        dl_f = flat_ring[0:NI, 3 * IE:4 * IE]
        dl_b = dlb[0:NI, :]
        rises = flat_ring[0:NI, 0:IE - 1]
        zero = hot[:, 0:3, :].rearrange("p a b -> p (a b)")
        row_f = hot[0:1, 4:13, :].rearrange("p a b -> p (a b)")[:, 0:5 * NG].rearrange("p (n g) -> p n g", n=5)
        g_first, g_last, g_tmp, g_need, g_viol = (row_f[:, n, :] for n in range(5))
        last_i = hidT[0:1, :, :].rearrange("p a b -> p (a b)")[:, 0:NG].bitcast(I32)
        V = nc.vector
        A = nc.scalar
        T = nc.tensor

        def chain(eng, name):
            count = [0]

            def then(ins):
                count[0] += 1
                ins.then_inc(S(name), 1)

            def settle():
                eng.wait_ge(S(name), count[0])

            return then, settle

        with nc.Block() as block:
            wide = [
                (wa_s[:, :, 0:C], W.rearrange("(t p) n -> p t n", p=P)),
                (wa_s[:, :, C + 2 * HEADS:WA], Wg1.rearrange("(t p) n -> p t n", p=P)),
                (wk_s, Wqkv.rearrange("(t p) n -> p t n", p=P)[:, :, C:2 * C]),
                (wproj_s[:, :, :], Wproj.rearrange("(t p) n -> p t n", p=P)),
                (wg2_s[:, :], Wg2),
                (sa[:, 0, :], row(att_src.rearrange("h d -> (h d)"), C)),
                (sa[:, 1, :], row(att_dst.rearrange("h d -> (h d)"), C)),
                (gbrow[:, :], row(gnn_bias, C)),
                (prow[:, :], row(bproj, C)),
                (wrrow[:, :], row(wr.rearrange("c o -> (c o)"), C)),
                (b2row[:, :], row(b2, C)),
                (b1row[:, :], row(bg1, GH)),
                (brc[:, :], row(br, 1)),
            ]
            columns = [
                (b1_s[:, :], b1.rearrange("(t p) -> p t", p=P)),
                (hbg2[:, :], bg2.rearrange("(t p) -> p t", p=P)),
                (lng[:, :], ln_g.rearrange("(t p) -> p t", p=P)),
                (lnb[:, :], ln_b.rearrange("(t p) -> p t", p=P)),
                (base_i[:, :], dst.rearrange("(a g e) -> a g e", a=1, e=GE)[:, :, 0]),
                (last_i[:, :], dst.rearrange("(a g e) -> a g e", a=1, e=GE)[:, :, GE - 1]),
            ]
            later = [
                (w1_s[:, :, :], w1.rearrange("(t p) n -> p t n", p=P)),
                (w2_s[:, :, :], w2.rearrange("(t p) n -> p t n", p=P)),
            ]
            n_weights = 16 * len(wide + columns)

            @block.sync
            def _(sp):
                sp.dma_start(ed_i[:, 0:IE], src.rearrange("(k e) -> k e", e=IE)).then_inc(S("edges_in"), 16)
                sp.dma_start(ed_i[:, IE:2 * IE], dst.rearrange("(k e) -> k e", e=IE)).then_inc(S("edges_in"), 16)
                for o, i in wide:
                    sp.dma_start(o, i).then_inc(S("weights_in"), 16)
                with nc.allow_non_contiguous_dma(reason="small columns"):
                    for o, i in columns:
                        sp.dma_start(o, i).then_inc(S("weights_in"), 16)
                for n in range(7):
                    sp.dma_start(big[:, n * XC:(n + 1) * XC, :],
                                 x.rearrange("(t p) c -> p t c", p=P)[:, n * XC:(n + 1) * XC, :]).then_inc(S(f"x{n}_in"), 16)
                for o, i in later:
                    sp.dma_start(o, i).then_inc(S("ffn_in"), 16)
                sp.wait_ge(S("breaks_made"), 1)
                for h in range(HEADS):
                    sp.dma_start(brk_d[:, :, h, :], br_f.rearrange("k (g e) -> k g e", g=GI)).then_inc(S("lists_out"), 16)
                sp.wait_ge(S("dloc_made"), 1)
                sp.dma_start(dloc_d, dl_b).then_inc(S("lists_out"), 16)
                sp.wait_ge(S("zeroed"), 1)
                sp.dma_start(adst_d[NT * P:ROWS, :], zero[:, 0:SPLIT // 2].bitcast(BF16)).then_inc(S("zeros_out"), 16)
                sp.wait_ge(S("ffn_in"), 32)

            @block.gpsimd
            def _(pool):
                pool.iota(iota_i[:, :], pattern=[[1, P]], base=0, channel_multiplier=0).then_inc(S("pool_made"), 1)
                pool.iota(iota_ci[:, :], pattern=[[0, 1]], base=0, channel_multiplier=1).then_inc(S("pool_made"), 1)
                pool.memset(hot[:, 0:3, :], 0.0).then_inc(S("zeroed"), 1)
                for a, v in ((ones[:, :], 1.0), (brk[:, :], 0.0),
                             (padneg[:, :], 0.0), (rmax, LOWEST), (epsc[:, :], EPS)):
                    pool.memset(a, v).then_inc(S("pool_made"), 1)

                then, settle = chain(pool, "pool1")
                pool.wait_ge(S("pool_made"), 7)
                pool.wait_ge(S("edges_float"), 1)
                then(pool.memset(bad[:, :], 0.0))
                d = ed_f[:, IE:2 * IE]
                then(pool.tensor_tensor(rises, d[:, 1:IE], d[:, 0:IE - 1], ALU.subtract))
                pool.wait_ge(S("weights_in"), n_weights)
                first, last, t, need_row, viol = g_first, g_last, g_tmp, g_need, g_viol
                then(pool.tensor_copy(first, base_i[:, :]))
                then(pool.tensor_copy(last, last_i[:, :]))
                then(pool.iota(write_i[:, 0:NI], pattern=[[P, NI]], base=-(LAG_MERGE - 2) * P, channel_multiplier=0))
                settle()
                then(pool.tensor_scalar(rises, rises, 0.0, None, ALU.is_lt))
                then(pool.tensor_copy(need_row[:, 0:NI], write_i[:, 0:NI]))
                then(pool.tensor_scalar(last, last, float(n_nodes - 1), None, ALU.min))
                settle()
                then(pool.tensor_tensor(t, last, first, ALU.subtract))
                settle()
                then(pool.tensor_scalar(viol, t, float(P), None, ALU.is_ge))
                settle()
                for ahead, op in ((1, ALU.is_lt), (2, ALU.is_le)):
                    then(pool.tensor_tensor(t[:, 0:NG - ahead], first[:, ahead:NG], last[:, 0:NG - ahead], ALU.subtract))
                    settle()
                    then(pool.tensor_scalar(t[:, 0:NG - ahead], t[:, 0:NG - ahead], 0.0, None, op))
                    settle()
                    then(pool.tensor_tensor(viol[:, 0:NG - ahead], viol[:, 0:NG - ahead], t[:, 0:NG - ahead], ALU.add))
                    settle()
                then(pool.tensor_tensor(t[:, 0:NI], first.rearrange("p (k g) -> p k g", g=GI)[:, :, 0], need_row[:, 0:NI],
                                        ALU.subtract))
                settle()
                then(pool.tensor_scalar(t[:, 0:NI], t[:, 0:NI], 0.0, None, ALU.is_lt))
                settle()
                then(pool.tensor_tensor(viol[:, 0:NI], viol[:, 0:NI], t[:, 0:NI], ALU.add))
                settle()

            @block.vector
            def _(dve):
                then, settle = chain(dve, "dve1")
                dve.wait_ge(S("pool_made"), 7)
                then(V.tensor_copy(iota_row[:, :], iota_i[:, :]))
                then(V.tensor_copy(iota_col[:, :], iota_ci[:, :]))
                settle()
                dve.wait_ge(S("edges_in"), 32)
                V.tensor_copy(ed_f, ed_i).then_inc(S("edges_float"), 1)
                dve.wait_ge(S("edges_float"), 1)
                V.tensor_scalar(ident[:, :], iota_row[:, :], iota_col[:, 0:1], None, ALU.is_equal).then_inc(S("ident_made"), 1)
                then(V.tensor_scalar(padneg[:, NT - 1:NT], iota_col[:, 0:1], float(n_nodes - (NT - 1) * P), -BIG,
                                     ALU.is_ge, ALU.mult))
                settle()
                d = ed_f[:, IE:2 * IE]
                then(V.tensor_tensor(br_f[:, 0:IE - 1], d[:, 1:IE], d[:, 0:IE - 1], ALU.not_equal))
                for g in range(GI):
                    then(V.tensor_scalar(dl_f[:, g * GE:(g + 1) * GE], d[:, g * GE:(g + 1) * GE],
                                         d[:, g * GE:g * GE + 1], None, ALU.subtract))
                settle()
                for g in range(GI):
                    then(V.memset(br_f[:, (g + 1) * GE - 1:(g + 1) * GE], 1.0))
                V.tensor_copy(dl_b.rearrange("k (g j p) -> k g j p", g=GI, j=TG),
                              dl_f.rearrange("k (g p j) -> k g j p", g=GI, j=TG)).then_inc(S("dloc_made"), 1)
                settle()
                dve.wait_ge(S("dloc_made"), 1)
                V.memset(mg[:, 0, 0:1], 0.0).then_inc(S("lists_made"), 1)
                for n in range(7):
                    dve.wait_ge(S(f"x{n}_in"), 16)
                    for t in range(n * XC, (n + 1) * XC):
                        then(V.bn_stats(st[:, t, :], big[:, t, :]))
                    if n == 3:
                        dve.wait_ge(S("lists_turned"), 6)
                        V.tensor_scalar(br_f, br_f, LOWEST, None, ALU.mult).then_inc(S("breaks_made"), 1)
                dve.wait_ge(S("weights_in"), n_weights)
                for n in range(2):
                    for t in range(CT):
                        then(V.tensor_tensor(xs[:, t, :], wa_s[:, t, 0:C], sa[:, n, :], ALU.mult))
                    settle()
                    for t in range(CT):
                        then(V.tensor_reduce(wa_s[:, t, C + n * HEADS:C + (n + 1) * HEADS],
                                             xs[:, t, :].rearrange("p (h d) -> p h d", h=HEADS), AX_X, ALU.add))
                    settle()
                then(V.tensor_scalar(wproj_s[:, :, :], wproj_s[:, :, :], 0.5, None, ALU.mult))
                then(V.tensor_scalar(hbg2[:, :], hbg2[:, :], 0.5, None, ALU.mult))
                then(V.tensor_scalar(prow[:, :], prow[:, :], 0.5, None, ALU.add))
                for t in range(CT):
                    V.tensor_scalar(sc[:, 0, t * P:(t + 1) * P], ones[:, :], lnb[:, t:t + 1], None,
                                    ALU.mult).then_inc(S("lnb_spread"), 1)
                dve.wait_ge(S("lnb_used"), 1)
                then(V.tensor_tensor(b1row[:, :], b1row[:, :], bank[0][:, 0:GH], ALU.add))
                for t in range(CT):
                    then(V.tensor_scalar(wa_s[:, t, C + 2 * HEADS:WA], wa_s[:, t, C + 2 * HEADS:WA], lng[:, t:t + 1],
                                         None, ALU.mult))
                settle()
                a, b, c, e = (xs[:, 0, j * 64:j * 64 + NT] for j in range(4))
                then(V.tensor_tensor(a, st[:, :, 1], st[:, :, 4], ALU.add))
                then(V.tensor_tensor(b, st[:, :, 1], st[:, :, 4], ALU.subtract))
                then(V.tensor_tensor(c, st[:, :, 2], st[:, :, 5], ALU.add))
                settle()
                then(V.tensor_scalar(mean[:, :], a, 0.5, None, ALU.mult))
                then(V.tensor_tensor(b, b, b, ALU.mult))
                then(V.tensor_scalar(c, c, 1.0 / C, None, ALU.mult))
                settle()
                then(V.scalar_tensor_tensor(c, b, 0.25, c, ALU.mult, ALU.add))
                settle()
                then(V.tensor_copy(b, c))
                settle()

                def inverse_root(o, v, s, n):
                    then(V.tensor_scalar(v, v, EPS, None, ALU.add))
                    settle()
                    V.tensor_copy(s, v).then_inc(S("root_asked"), 1)
                    dve.wait_ge(S("root_made"), n)
                    then(V.reciprocal(o, s))
                    settle()
                    then(V.tensor_tensor(s, o, o, ALU.mult))
                    settle()
                    then(V.tensor_tensor(s, s, v, ALU.mult))
                    settle()
                    then(V.tensor_scalar(s, s, -0.5, 1.5, ALU.mult, ALU.add))
                    settle()
                    then(V.tensor_tensor(o, o, s, ALU.mult))
                    settle()

                inverse_root(rstd[:, :], c, e, 1)
                then(V.tensor_tensor(b, b, rstd[:, :], ALU.mult))
                settle()
                then(V.tensor_tensor(b, b, rstd[:, :], ALU.mult))
                settle()
                inverse_root(rstd2[:, :], b, e, 2)

            @block.scalar
            def _(act):
                for n, to in enumerate((srcT, dlocT, lastT)):
                    for half in range(2):
                        act.wait_ge(S("lists_turned"), 2 * n + half + 1)
                        A.activation(to[:, :, half * 8:half * 8 + 8].rearrange("p k q -> p q k"),
                                     bank[2 + half][:, 0:8 * NI].rearrange("p (q k) -> p q k", q=8), ACT.Copy
                                     ).then_inc(S("lists_copied"), 1)
                for n in range(2):
                    act.wait_ge(S("root_asked"), n + 1)
                    e = xs[:, 0, 192:192 + NT]
                    A.activation(e, e, ACT.Sqrt).then_inc(S("root_made"), 1)

            @block.tensor
            def _(pe):
                pe.wait_ge(S("ident_made"), 1)
                pe.wait_ge(S("lists_made"), 1)
                for n, lists in enumerate((ed_f[:, 0:IE], dl_f, br_f)):
                    for half in range(2):
                        if n:
                            pe.wait_ge(S("lists_copied"), 2 * n - 1 + half)
                        for q in range(8 * half, 8 * half + 8):
                            at = lists.rearrange("k (g p j) -> k g p j", g=GI, j=TG)[:, q // TG, :, q % TG]
                            mm = T.transpose(bank[2 + half][:, (q % 8) * NI:(q % 8 + 1) * NI], at, ident[0:NI, 0:NI])
                        mm.then_inc(S("lists_turned"), 1)
                pe.wait_ge(S("lnb_spread"), CT)
                for t in range(CT):
                    mm = T.matmul(bank[0][:, 0:GH], sc[:, 0, t * P:(t + 1) * P], wa_s[:, t, C + 2 * HEADS:WA],
                                  start=(t == 0), stop=(t == CT - 1))
                mm.then_inc(S("lnb_used"), 1)

        gate_cols = slice(C + 2 * HEADS, WA)
        feat = parts[:, :, :, :].rearrange("p u a b -> p u (a b)")
        with nc.Block() as block:
            @block.sync
            def _(sp):
                def clear(t):
                    sp.dma_start(parts_d[:, bass.ds(t * P, P), :].rearrange("n p c -> p n c"),
                                 zero[:, 0:SW].unsqueeze(1).to_broadcast([P, 2, SW])).then_inc(S("zeros_out"), 16)

                clear(NT)

                def store(i, u):
                    clear(i)
                    sp.wait_ge(S("feat_made"), i + 1)
                    sp.dma_start(feat_d[bass.ds(i * P, P), :], feat[:, u, 0:AW]).then_inc(S(f"feat_out{u}"), 16)
                    if not known_below(i, 1):
                        store_hidden(i - 1, 1 - u)

                def store_hidden(i, u):
                    sp.wait_ge(S("hidT_made"), i + 1)
                    sp.dma_start(hid_d[bass.ds(i, 1), :, :].rearrange("a b c -> (a b) c"),
                                 hidT[:, u, :]).then_inc(S(f"hid_out{u}"), 16)

                sweep(sp, 0, NT, 2, 0, store)
                store_hidden(NT - 1, (NT - 1) % 2)
                for u in range(2):
                    sp.wait_ge(S(f"feat_out{u}"), 16 * ((NT + 1 - u) // 2))
                    sp.wait_ge(S(f"hid_out{u}"), 16 * ((NT + 1 - u) // 2))
                sp.wait_ge(S("lists_out"), 16 * (HEADS + 1))

            @block.vector
            def _(dve):
                def first(i, u):
                    if not known_below(i, 2):
                        dve.wait_ge(S("turned"), i - 1)
                    V.tensor_scalar(xs[:, u, :], big[:, bass.ds(i, 1), :].rearrange("p a c -> p (a c)"),
                                    mean[:, bass.ds(i, 1)], rstd[:, bass.ds(i, 1)], ALU.subtract,
                                    ALU.mult).then_inc(S("normed"), 1)

                def second(i, u):
                    dve.wait_ge(S("turned"), i + 1)
                    if not known_below(i, 2):
                        dve.wait_ge(S("keys_done"), i - 1)
                        dve.wait_ge(S("xnT_kept"), i - 1)
                    V.tensor_copy(sa[:, u, :], bank[u][:, 0:C]).then_inc(S("turn_copied"), 1)

                def third(i, u):
                    dve.wait_ge(S("feat_done"), i + 1)
                    if not known_below(i, 2):
                        dve.wait_ge(S(f"feat_out{u}"), 8 * (i - u))
                    V.tensor_copy(feat[:, u, 0:AW], bank[2 + u][:, 0:AW]).then_inc(S("feat_made"), 1)
                    V.tensor_copy(adst_s[:, bass.ds(i, 1), :].rearrange("p a h -> p (a h)"),
                                  bank[2 + u][:, AW:AW + HEADS]).then_inc(S("adst_made"), 1)
                    if not known_below(i, 2):
                        dve.wait_ge(S("hid_made"), i - 1)
                    V.scalar_tensor_tensor(sc[:, u, 0:GH], bank[2 + u][:, gate_cols], rstd2[:, bass.ds(i, 1)],
                                           b1row[:, :], ALU.mult, ALU.add).then_inc(S("hid_asked"), 1)

                def fourth(i, u):
                    dve.wait_ge(S("keys_kept"), i + 1)
                    if not known_below(i, 1):
                        dve.wait_ge(S("key_max"), i)
                    V.tensor_tensor(rmax, rmax, big[:, bass.ds(i, 1), :].rearrange("p a c -> p (a c)"),
                                    ALU.max).then_inc(S("key_max"), 1)
                    dve.wait_ge(S("hid_turned"), i + 1)
                    if not known_below(i, 2):
                        dve.wait_ge(S(f"hid_out{u}"), 8 * (i - u))
                    V.tensor_copy(hidT[:, u, :], bank[6 + u][0:GH, 0:P]).then_inc(S("hidT_made"), 1)

                def body(i, u):
                    if not isinstance(i, int) or i + 1 < NT:
                        second(i + 1, 1 - u)
                    if not isinstance(i, int) or i + 2 < NT:
                        first(i + 2, u)
                    third(i, u)
                    if not known_below(i, 1):
                        fourth(i - 1, 1 - u)

                first(0, 0)
                first(1, 1)
                second(0, 0)
                sweep(dve, 0, NT, 4, 3, body)
                fourth(NT - 1, (NT - 1) % 2)

            @block.scalar
            def _(act):
                def keep_turned(i, u):
                    act.wait_ge(S("turn_copied"), i + 1)
                    A.activation(xnT[:, bass.ds(i, 1), :].rearrange("p a c -> p (a c)"), sa[:, u, :],
                                 ACT.Copy).then_inc(S("xnT_kept"), 1)

                def body(i, u):
                    if not isinstance(i, int) or i + 1 < NT:
                        keep_turned(i + 1, 1 - u)
                    act.wait_ge(S("keys_done"), i + 1)
                    A.activation(big[:, bass.ds(i, 1), :].rearrange("p a c -> p (a c)"), bank[4 + u][:, 0:C],
                                 ACT.Identity, bias=padneg[:, bass.ds(i, 1)]).then_inc(S("keys_kept"), 1)
                    act.wait_ge(S("hid_asked"), i + 1)
                    if not known_below(i, 2):
                        act.wait_ge(S("hid_turned"), i - 1)
                    A.activation(sd[:, u, 0:GH], sc[:, u, 0:GH], ACT.Gelu).then_inc(S("hid_made"), 1)

                keep_turned(0, 0)
                sweep(act, 0, NT, 4, 3, body)

            @block.tensor
            def _(pe):
                def turn(i, u):
                    pe.wait_ge(S("normed"), i + 1)
                    if not known_below(i, 2):
                        pe.wait_ge(S("turn_copied"), i - 1)
                    for t in range(CT):
                        mm = T.transpose(bank[u][:, t * P:(t + 1) * P], xs[:, u, t * P:(t + 1) * P], ident[:, :])
                    mm.then_inc(S("turned"), 1)

                def products(i, u):
                    pe.wait_ge(S("turn_copied"), i + 1)
                    if not known_below(i, 2):
                        pe.wait_ge(S("hid_asked"), i - 1)
                    for t in range(CT):
                        mm = T.matmul(bank[2 + u][:, 0:WA], sa[:, u, t * P:(t + 1) * P], wa_s[:, t, :],
                                      start=(t == 0), stop=(t == CT - 1))
                    mm.then_inc(S("feat_done"), 1)
                    if not known_below(i, 2):
                        pe.wait_ge(S("keys_kept"), i - 1)
                    for t in range(CT):
                        mm = T.matmul(bank[4 + u][:, 0:C], sa[:, u, t * P:(t + 1) * P], wk_s[:, t, :],
                                      start=(t == 0), stop=(t == CT - 1))
                    mm.then_inc(S("keys_done"), 1)

                def hidden(i, u):
                    made, free = number(pe, i + 1), None
                    if not known_below(i, 2):
                        free = number(pe, i - 1)
                    pe.wait_ge(S("ident_made"), 1)
                    pe.wait_ge(S("hid_made"), made)
                    if free is not None:
                        pe.wait_ge(S("hidT_made"), free)
                    T.transpose(bank[6 + u][0:GH, 0:P], sd[:, u, 0:GH], ident[:, :]).then_inc(S("hid_turned"), 1)

                def body(i, u):
                    if not isinstance(i, int) or i + 1 < NT:
                        turn(i + 1, 1 - u)
                    products(i, u)
                    if not known_below(i, 1):
                        hidden(i - 1, 1 - u)

                turn(0, 0)
                sweep(pe, 0, NT, 4, 3, body)
                hidden(NT - 1, (NT - 1) % 2)

        x_slot = [xs[:, 0, :], xs[:, 1, :], sa[:, 0, :], sa[:, 1, :]]
        less_mean = rstd2

        def gather(pool, u, g):
            for j in range(TG):
                q = g * TG + j
                pool.indirect_dma_start(
                    out=ring[:, u * TI + q, 0:AW], out_offset=None, in_=feat_d,
                    in_offset=bass.IndirectOffsetOnAxis(ap=idx[:, u, q:q + 1], axis=0),
                ).then_inc(S(f"rows_in{u}{g}"), 16)

        wq_s = hT[:, 0:4, :].rearrange("p a b -> p (a b)").rearrange("p (t n) -> p t n", t=CT)
        with nc.Block() as block:
            @block.gpsimd
            def _(pool):
                pool.partition_all_reduce(cmax, rmax, P, RMAX).then_inc(S("cmax_made"), 1)
                pool.wait_ge(S("order_checked"), 1)
                then, settle = chain(pool, "pool3")
                then(pool.partition_all_reduce(bad[:, 3:4], bad[:, 2:3], P, RADD))
                settle()
                then(pool.tensor_scalar(bad[0:1, 0:1], bad[0:1, 3:4], 1.0, None, ALU.min))
                settle()
                then(pool.tensor_copy(bad_i[:, :], bad[0:1, 0:1]))
                then(pool.tensor_scalar(g_tmp, g_first, -1.0, float(NT * P), ALU.mult, ALU.add))
                settle()
                then(pool.tensor_scalar(g_tmp, g_tmp, bad[0:1, 0:1], None, ALU.mult))
                settle()
                then(pool.tensor_tensor(g_tmp, g_tmp, g_first, ALU.add))
                settle()
                then(pool.tensor_copy(write_i[:, :], g_tmp))
                settle()

            @block.sync
            def _(sp):
                sp.wait_ge(S("adst_split"), 3)
                with nc.allow_non_contiguous_dma(reason="small rows"):
                    sp.dma_start(adst_d[0:NT * P, :].rearrange("(t p) c -> p t c", p=P), adst_p[:, :, :]
                                 ).then_inc(S("adst_out"), 16)
                sp.wait_ge(S("adst_out"), 16)
                sp.wait_ge(S("zeros_out"), 16 * (NT + 2))

            @block.vector
            def _(dve):
                then, settle = chain(dve, "dve3")
                for u in range(2):
                    V.tensor_copy(idx[:, u, :], srcT[:, u, :]).then_inc(S("idx_made"), 1)
                then(V.tensor_reduce(bad[0:NI, 0:1], rises, AX_X, ALU.add))
                then(V.tensor_reduce(bad[0:1, 1:2], g_viol, AX_X, ALU.add))
                settle()
                V.tensor_tensor(bad[:, 2:3], bad[:, 0:1], bad[:, 1:2], ALU.add).then_inc(S("order_checked"), 1)
                then(V.scalar_tensor_tensor(less_mean[:, :], mean[:, :], -1.0, rstd[:, :], ALU.mult, ALU.mult))
                for n in range(3):
                    part = adst_p[:, :, n * HEADS:(n + 1) * HEADS]
                    V.tensor_copy(part, adst_s[:, :, :]).then_inc(S("adst_split"), 1)
                    if n < 2:
                        dve.wait_ge(S("adst_split"), n + 1)
                        then(V.tensor_tensor(adst_s[:, :, :], adst_s[:, :, :], part, ALU.subtract))
                        settle()
        g_rows, g_held, g_new = parts[:, 0, 0, :], parts[:, 0, 1, :], parts[:, 1, 0, :]
        g_spread, g_same, g_pen, g_max = hot[:, 0:4, :], hot[:, 4, :], hot[:, 5, :], hot[:, 8:12, :]
        g_dst = stat[:, 0, 0, :]
        m = mg[:, 0, :]

        def every_tile(eng, body):
            with eng.If(eng.value_load(bad_i[0:1, 0:1], min_val=0, max_val=1) > 0):
                body(0)
                with eng.Fori(1, NI * TI) as i:
                    body(i)

        with nc.Block() as block:
            @block.sync
            def _(sp):
                def body(i):
                    if not known_below(i, 1):
                        sp.wait_ge(S("gen_put"), 16 * i)
                    with nc.allow_non_contiguous_dma(reason="a column of indices"):
                        for n, a in enumerate((src, dst)):
                            sp.dma_start(gen_i[:, n:n + 1], a.rearrange("(t p) -> t p", p=P)[bass.ds(i, 1), :]
                                         .rearrange("a p -> p a")).then_inc(S("gen_in"), 16)

                every_tile(sp, body)

            @block.gpsimd
            def _(pool):
                def body(i):
                    made, put, new = number(pool, i + 1), number(pool, 16 * i), number(pool, i + 1)
                    pool.wait_ge(S("idx_made"), 2)
                    pool.wait_ge(S("gen_clamped"), made)
                    if not known_below(i, 1):
                        pool.wait_ge(S("gen_put"), put)
                    for to, table, n in ((g_rows[:, 0:AW], feat_d, 0), (g_dst, adst_d, 2), (g_held, part_d[0], 2)):
                        pool.indirect_dma_start(out=to, out_offset=None, in_=table,
                                                in_offset=bass.IndirectOffsetOnAxis(ap=gen_i[:, n:n + 1], axis=0)
                                                ).then_inc(S("gen_rows"), 16)
                    pool.wait_ge(S("idx_made"), 2)
                    pool.wait_ge(S("gen_new"), new)
                    pool.indirect_dma_start(out=part_d[0], out_offset=bass.IndirectOffsetOnAxis(ap=gen_i[:, 2:3], axis=0),
                                            in_=g_new, in_offset=None).then_inc(S("gen_put"), 16)

                every_tile(pool, body)

            @block.tensor
            def _(pe):
                def body(i):
                    pe.wait_ge(S("gen_spread"), 5 * i + 1)
                    T.matmul(bank[0][:, 0:P], g_spread[:, 0, :], ident[:, :], start=True, stop=True
                             ).then_inc(S("gen_turned"), 1)
                    pe.wait_ge(S("gen_spread"), 5 * i + 5)
                    for h in range(HEADS):
                        mm = T.matmul(bank[1][:, h * P:(h + 1) * P], g_spread[:, h, :], ident[:, :], start=True, stop=True)
                    mm.then_inc(S("gen_turned"), 1)
                    pe.wait_ge(S("gen_scaled"), 2 * i + 2)
                    T.matmul(bank[2][:, 0:AW], g_same, g_rows[:, 0:AW], start=True, stop=True).then_inc(S("gen_summed"), 1)

                every_tile(pe, body)

            @block.scalar
            def _(act):
                def body(i):
                    act.wait_ge(S("gen_asked"), 2 * i + 2)
                    A.activation(m[:, 32:40], m[:, 24:32], ACT.Exp).then_inc(S("gen_exp"), 1)

                every_tile(act, body)

            @block.vector
            def _(dve):
                steps_of_tile = [0]

                def body(i):
                    count = [0]

                    def then(ins):
                        count[0] += 1
                        ins.then_inc(S("gen_dve"), 1)

                    def settle():
                        dve.wait_ge(S("gen_dve"), steps_of_tile[0] * i + count[0])

                    dve.wait_ge(S("gen_in"), 32 * i + 32)
                    then(V.tensor_copy(m[:, 0:1], gen_i[:, 1:2]))
                    settle()
                    then(V.tensor_scalar(m[:, 0:1], m[:, 0:1], float(ROWS - 1), None, ALU.min))
                    settle()
                    V.tensor_copy(gen_i[:, 2:3], m[:, 0:1]).then_inc(S("gen_clamped"), 1)
                    V.tensor_scalar(g_spread[:, 0, :], ones[:, :], m[:, 0:1], None, ALU.mult).then_inc(S("gen_spread"), 1)
                    dve.wait_ge(S("gen_turned"), 2 * i + 1)
                    then(V.tensor_scalar(g_same, bank[0][:, 0:P], m[:, 0:1], None, ALU.is_equal))
                    settle()
                    then(V.tensor_scalar(g_pen, g_same, 1.0, BIG, ALU.subtract, ALU.mult))
                    dve.wait_ge(S("gen_rows"), 48 * i + 48)
                    then(V.tensor_reduce(m[:, 4:8], g_dst.rearrange("p (n h) -> p h n", n=3), AX_X, ALU.add))
                    settle()
                    then(V.tensor_tensor(m[:, 4:8], m[:, 4:8], g_rows[:, C:C + HEADS], ALU.add))
                    settle()
                    then(V.scalar_tensor_tensor(m[:, 4:8], m[:, 4:8], 0.2, m[:, 4:8], ALU.mult, ALU.max))
                    settle()
                    for h in range(HEADS):
                        V.tensor_scalar(g_spread[:, h, :], ones[:, :], m[:, 4 + h:5 + h], None, ALU.mult
                                        ).then_inc(S("gen_spread"), 1)
                    dve.wait_ge(S("gen_turned"), 2 * i + 2)
                    then(V.tensor_tensor(g_max, bank[1][:, :].rearrange("p (h n) -> p h n", h=HEADS),
                                         g_pen.unsqueeze(1).to_broadcast([P, HEADS, P]), ALU.add))
                    then(V.tensor_scalar(m[:, 12:13], g_held[:, SW - 1:SW], 1.0, BIG, ALU.subtract, ALU.mult))
                    settle()
                    then(V.tensor_reduce(m[:, 8:12], g_max, AX_X, ALU.max))
                    then(V.tensor_scalar(m[:, 16:20], g_held[:, C + HEADS:C + 2 * HEADS], m[:, 12:13], None, ALU.add))
                    settle()
                    then(V.tensor_tensor(m[:, 20:24], m[:, 8:12], m[:, 16:20], ALU.max))
                    settle()
                    V.tensor_tensor(m[:, 24:28], m[:, 16:20], m[:, 20:24], ALU.subtract).then_inc(S("gen_asked"), 1)
                    V.tensor_tensor(m[:, 28:32], m[:, 4:8], m[:, 20:24], ALU.subtract).then_inc(S("gen_asked"), 1)
                    dve.wait_ge(S("gen_exp"), i + 1)
                    V.tensor_copy(g_rows[:, C:C + HEADS], m[:, 36:40]).then_inc(S("gen_scaled"), 1)
                    feats = g_rows[:, 0:C].rearrange("p (h d) -> p h d", h=HEADS)
                    V.tensor_tensor(feats, feats, m[:, 36:40].unsqueeze(2).to_broadcast([P, HEADS, HD]), ALU.mult
                                    ).then_inc(S("gen_scaled"), 1)
                    then(V.tensor_tensor(g_new[:, 0:C].rearrange("p (h d) -> p h d", h=HEADS),
                                         g_held[:, 0:C].rearrange("p (h d) -> p h d", h=HEADS),
                                         m[:, 32:36].unsqueeze(2).to_broadcast([P, HEADS, HD]), ALU.mult))
                    then(V.tensor_tensor(g_new[:, C:C + HEADS], g_held[:, C:C + HEADS], m[:, 32:36], ALU.mult))
                    then(V.tensor_copy(g_new[:, C + HEADS:C + 2 * HEADS], m[:, 20:24]))
                    then(V.memset(g_new[:, SW - 1:SW], 1.0))
                    settle()
                    dve.wait_ge(S("gen_summed"), i + 1)
                    V.tensor_tensor(g_new[:, 0:AW], g_new[:, 0:AW], bank[2][:, 0:AW], ALU.add).then_inc(S("gen_new"), 1)
                    steps_of_tile[0] = count[0]

                every_tile(dve, body)

        bk_e, bk_t, bk_m, bk_o = bank[0], bank[1], bank[4], bank[5]
        MCOL = TI * SPLIT
        slot = [slice(u * TI, (u + 1) * TI) for u in range(2)]

        def tile(a, i):
            return a[:, bass.ds(i, 1), :].rearrange("p a c -> p (a c)")

        def by_head(a):
            return a.rearrange("p (h d) -> p h d", h=HEADS)

        def steps(eng, parts_of_body):
            loop_from = LAG_FF2 + 2 + (LAG_FF2 % 2)

            def body(k, u):
                for lo, hi, f in parts_of_body:
                    if lo <= (k if isinstance(k, int) else loop_from) < hi:
                        f(k - lo, (u - lo) % 2)
            for k in range(loop_from):
                body(k, k % 2)
            loop_to = NI - 2 - NI % 2
            with eng.Fori(loop_from // 2, loop_to // 2) as half:
                for u in range(2):
                    body(half * 2 + u, u)
            for k in range(loop_to, NT + LAG_FF2):
                body(k, k % 2)

        CHUNKS = [(0, 12)] + [(n, n + 4) for n in range(12, 44, 4)] + [(44, NT)]
        CONTEXT_A = lambda f: (0, 5, lambda k, u: f(2 * k + 1, u))
        CONTEXT_B = lambda f: (0, 4, lambda k, u: f(2 * k + 2, u))
        FOLD = lambda f: (5, 6, f)
        ROUNDS = 8
        SEARCH = [lambda f, k=NT + LAG_FF1 - 1 + n: (k, k + 1, f) for n in range(2)]
        DIGITS = [0, 2, ROUNDS]
        EDGES = lambda f: (0, NI, f)
        WINDOWS = lambda f: (1, NI + 1, f)
        MERGE = lambda f: (LAG_MERGE, NT + LAG_MERGE, f)
        SUM = lambda f: (LAG_SUM, NT + LAG_SUM, f)
        FF1 = lambda f: (LAG_FF1, NT + LAG_FF1, f)
        FF2 = lambda f: (LAG_FF2, NT - 1 + LAG_FF2, f)

        tail = flat_ring[:, 0:64 * P].rearrange("p (a b) -> p a b", b=P)
        lower, jtab = tail[:, 0, :], tail[:, 1, 0:15].bitcast(I32)
        v_s = tail[:, 2, 0:NT]
        cmp_s = tail[:, 4:12, :].rearrange("p a b -> p (a b)")[:, 0:15 * NT].rearrange("p (j t) -> p j t", j=15)
        cand = tail[:, 12, 0:15]
        cnt = tail[:, 13, 0:15]
        one = lambda n: tail[:, 14, n:n + 1]
        t_bits, sign, want, dig, more, thr, need = (one(n) for n in range(7))
        dig_i = one(8)
        eq_s, gt_s, pre_s, off_s, sel_s = (tail[:, 16 + n, 0:NT] for n in range(5))
        tot_s = tail[:, 21, 0:NT]

        with nc.Block() as block:
            @block.gpsimd
            def _(pool):
                def fill(k, u):
                    for g in range(GI):
                        made, used = number(pool, k + 1), None
                        if not known_below(k, 2):
                            used = number(pool, GI * (k - 2) + g + 1)
                        pool.wait_ge(S("idx_made"), 2)
                        if g == 0:
                            pool.wait_ge(S("idx_made"), made)
                        if used is not None:
                            pool.wait_ge(S("sums_done"), used)
                        gather(pool, u, g)

                steps(pool, [EDGES(fill)])
                pool.wait_ge(S("scores_done"), NI)
                pool.iota(hotT[:, 0:30].bitcast(I32), pattern=[[1, 15]], base=1, channel_multiplier=0
                          ).then_inc(S("digits_made"), 1)

            @block.sync
            def _(sp):
                def base(k, g):
                    return sp.value_load(base_i[0:1, bass.ds(k * GI + g, 1)], min_val=0, max_val=n_nodes - 1)

                def prefetch(k, u):
                    if not known_below(k, 1):
                        sp.wait_ge(S("hotT_made"), k)
                    sp.dma_start(dlb[:, :], dloc_d[bass.ds(k, 1), :].to_broadcast([P, IE])).then_inc(S("dlb_in"), 16)
                    first = [base(k, g) for g in range(GI)]
                    if not known_below(k, 2):
                        sp.wait_ge(S("scores_done"), k - 1)
                    for g in range(GI):
                        sp.dma_start(stat[:, u, g, :], adst_d[bass.ds(first[g], P), :]
                                     ).then_inc(S(f"stat_in{u}"), 16)

                def prefetch_breaks(k, u):
                    if not known_below(k, 1):
                        sp.wait_ge(S("max_made"), k)
                    sp.dma_start(brk[:, 1:GE + 1], brk_d[bass.ds(k, 1), :, :, :].rearrange("a g h e -> (a g h) e")
                                 ).then_inc(S("brk_in"), 16)

                def ahead(k, u):
                    prefetch(k + 1, 1 - u)

                def breaks_ahead(k, u):
                    prefetch_breaks(k + 1, 1 - u)

                def windows(k, u):
                    for g in range(GI):
                        first = sp.value_load(write_i[0:1, bass.ds(k * GI + g, 1)], min_val=0, max_val=NT * P)
                        sp.wait_ge(S("sums_kept"), GI * k + g + 1)
                        if not (known_below(k, 1) and g < 2):
                            sp.wait_ge(S(f"window_out{g % 2}"), 16 * (2 * k + g // 2))
                        sp.dma_start(part_d[g % 2][bass.ds(first, P), :], wout[:, g % 2, :]
                                     ).then_inc(S(f"window_out{g % 2}"), 16)

                def load_node(i, u):
                    upto = i + LAG_MERGE - 1
                    upto = number(sp, 32 * (min(upto, NI) if isinstance(i, int) else upto))
                    free = None if known_below(i, 2) else number(sp, i - 1)
                    sp.wait_ge(S("idx_made"), 2)
                    if known_below(i, 2):
                        sp.wait_ge(S("wqc_kept"), 1)
                    if free is not None:
                        sp.wait_ge(S("x1_made"), free)
                        sp.wait_ge(S("merged"), free)
                        sp.wait_ge(S("gate_done"), free)
                    for n in range(2):
                        sp.wait_ge(S(f"window_out{n}"), upto)
                    rows = bass.ds(i * P, P)
                    sp.dma_start(hidT[:, u, :], hid_d[bass.ds(i, 1), :, :].rearrange("a b c -> (a b) c")
                                 ).then_inc(S(f"node_in{u}"), 16)
                    sp.dma_start(parts[:, u, :, :], parts_d[:, rows, :].rearrange("n p c -> p n c")
                                 ).then_inc(S(f"node_in{u}"), 16)
                    sp.dma_start(xs[:, u, :], x[rows, :]).then_inc(S(f"node_in{u}"), 16)

                def load_again(i, u):
                    if not known_below(i, 4):
                        sp.wait_ge(S("renormed"), i - 3)
                    sp.dma_start(x_slot[u], x[bass.ds(i * P, P), :]).then_inc(S(f"x_again{u}"), 16)

                def context(k, u):
                    lo, hi = CHUNKS[k]
                    sweep(sp, lo + 4 if lo else 0, min(hi + 4, NT), 0 if lo else 4, 0, load_again, n=4)

                for i in range(4):
                    load_again(i, i)
                prefetch(0, 0)
                prefetch_breaks(0, 0)
                sweep(sp, 4, CHUNKS[0][1] + 4, 0, 0, load_again, n=4)
                sp.dma_start(wq_s, Wqkv.rearrange("(t p) n -> p t n", p=P)[:, :, 0:C]).then_inc(S("wqv_in"), 16)
                sp.dma_start(feat[:, :, 0:C], Wqkv.rearrange("(t p) n -> p t n", p=P)[:, :, 2 * C:3 * C]
                             ).then_inc(S("wqv_in"), 16)

                steps(sp, [CONTEXT_A(context), MERGE(load_node), (0, NI - 1, ahead), WINDOWS(windows), CONTEXT_B(context),
                           (0, NI - 1, breaks_ahead)])

            @block.vector
            def _(dve):
                keys = lambda i: big[:, bass.ds(i, 1), :].rearrange("p a c -> p (a c)")

                def less(i):
                    V.tensor_tensor(keys(i), keys(i), cmax, ALU.subtract).then_inc(S("keys_less"), 1)

                def context_tile(i, u):
                    if not isinstance(i, int) or i + 2 < NT:
                        less(i + 2)
                    dve.wait_ge(S("keys_exp"), i + 1)
                    if not known_below(i, 1):
                        dve.wait_ge(S("exp_added"), i)
                    V.tensor_tensor(exp_sum, exp_sum, keys(i), ALU.add).then_inc(S("exp_added"), 1)

                def context(k, u):
                    lo, hi = CHUNKS[k]
                    sweep(dve, lo, hi, 2 if lo == 0 else 0, 3 if hi == NT else 0, context_tile)

                def fold(k, u):
                    then, settle = chain(dve, "dve_fold")
                    dve.wait_ge(S("context_added"), NT)
                    dve.wait_ge(S("exp_summed"), 1)
                    V.tensor_copy(totals, bank[6][0:1, 0:C]).then_inc(S("totals_kept"), 1)
                    for t in range(CT):
                        V.tensor_copy(sc[:, t, :], bank[4 + t][:, 0:C]).then_inc(S("totals_kept"), 1)
                    then(V.memset(sd[:, 0, 0:P], 0.0))
                    settle()
                    for b in range(P // MIX_HD):
                        s = slice(b * MIX_HD, (b + 1) * MIX_HD)
                        then(V.memset(sd[s, 0, s], 1.0))
                    dve.wait_ge(S("sums_turned"), 1)
                    then(V.reciprocal(mg[:, 0, 0:CT], bank[7][:, 0:CT]))
                    settle()
                    for t in range(CT):
                        dve.wait_ge(S("context_made"), CT)
                        V.scalar_tensor_tensor(xs[:, 0, t * P:(t + 1) * P], bank[6][:, t * P:(t + 1) * P],
                                               mg[:, 0, t:t + 1], sd[:, 0, 0:P], ALU.mult,
                                               ALU.mult).then_inc(S("context_kept"), 1)
                    dve.wait_ge(S("wq_turned"), 1)
                    for t in range(CT):
                        V.tensor_copy(sa[:, t, :], bank[4 + t][:, 0:C]).then_inc(S("wq_kept"), 1)
                    dve.wait_ge(S("folded"), 1)
                    V.tensor_copy(wqc_s[:, :, :], bank[7][:, :].rearrange("p (t n) -> p t n", t=CT)).then_inc(S("wqc_kept"), 1)

                def products(i, u):
                    dve.wait_ge(S("gate_made"), i + 1)
                    dve.wait_ge(S("mix_done"), i + 1)
                    V.scalar_tensor_tensor(sc[:, u, :], sc[:, u, :], 1.0, bk_m[:, 0:C], ALU.add,
                                           ALU.mult).then_inc(S("prod_made"), 1)

                def one_hots(k, u):
                    dve.wait_ge(S("dlb_in"), 16 * k + 16)
                    if not known_below(k, 1):
                        dve.wait_ge(S("scores_done"), k)
                    V.tensor_scalar(hotT[:, :], dlb[:, :], iota_col[:, 0:1], None, ALU.is_equal
                                    ).then_inc(S("hotT_made"), 1)

                def hots_ahead(k, u):
                    one_hots(k + 1, 1 - u)

                def edge_hot(k, g):
                    if not known_below(k, 1):
                        dve.wait_ge(S("sums_done"), GI * (k - 1) + g + 1)
                    tiles = slice(g * TG, (g + 1) * TG)
                    V.tensor_tensor(hot[:, tiles, :], iota_row[:, :].unsqueeze(1).to_broadcast([P, TG, P]),
                                    dlocT[:, bass.ds(k, 1), tiles].rearrange("p a q -> p (a q)").unsqueeze(2)
                                    .to_broadcast([P, TG, P]), ALU.is_equal).then_inc(S("hot_made"), 1)

                def edge_hots(k, u):
                    for g in range(GI):
                        edge_hot(k, g)

                def merge_weights(i, u):
                    m = mg[:, u, :]
                    dve.wait_ge(S(f"node_in{u}"), 24 * (i - u) + 48)
                    V.tensor_scalar(m[:, 0:2], parts[:, u, :, SW - 1], 1.0, BIG, ALU.subtract, ALU.mult
                                    ).then_inc(S("merge_steps"), 1)
                    dve.wait_ge(S("merge_steps"), 8 * i + 1)
                    V.tensor_tensor(m[:, 2:10].rearrange("p (n h) -> p n h", n=2), parts[:, u, :, C + HEADS:C + 2 * HEADS],
                                    m[:, 0:2].unsqueeze(2).to_broadcast([P, 2, HEADS]), ALU.add).then_inc(S("merge_steps"), 1)
                    dve.wait_ge(S("merge_steps"), 8 * i + 2)
                    V.tensor_tensor(m[:, 10:14], m[:, 2:6], m[:, 6:10], ALU.max).then_inc(S("merge_steps"), 1)
                    dve.wait_ge(S("merge_steps"), 8 * i + 3)
                    V.tensor_tensor(m[:, 14:22].rearrange("p (n h) -> p n h", n=2),
                                    m[:, 2:10].rearrange("p (n h) -> p n h", n=2),
                                    m[:, 10:14].unsqueeze(1).to_broadcast([P, 2, HEADS]), ALU.subtract
                                    ).then_inc(S("merge_asked"), 1)

                def scores(k, u):
                    to = lk[:, u, :, :].rearrange("p j x -> p (j x)")
                    dve.wait_ge(S("scores_done"), k + 1)
                    V.tensor_reduce(to.rearrange("p (q h) -> p q h", h=HEADS),
                                    bk_e[:, 0:MCOL].rearrange("p (q n h) -> p q h n", n=3, h=HEADS), AX_X, ALU.add
                                    ).then_inc(S("dst_summed"), 1)
                    for g in range(GI):
                        dve.wait_ge(S(f"rows_in{u}{g}"), 32 * (k - u) + 64)
                    if not (isinstance(k, int) and k + 2 >= NI):
                        V.tensor_copy(idx[:, u, :], srcT[:, bass.ds(k + 2, 1), :].rearrange("p a q -> p (a q)")
                                      ).then_inc(S("idx_made"), 1)
                    V.tensor_copy(ring[:, slot[u], SW - 1], lastT[:, bass.ds(k, 1), :].rearrange("p a q -> p (a q)")
                                  ).then_inc(S("lastcol_made"), 1)
                    dve.wait_ge(S("dst_summed"), k + 1)
                    four = lk[:, u, :, :].rearrange("p j (g h) -> p j g h", g=GI)
                    V.tensor_tensor(four, four, ring[:, slot[u], C:C + HEADS].rearrange("p (g j) h -> p j g h", g=GI),
                                    ALU.add).then_inc(S("src_added"), 1)
                    dve.wait_ge(S("src_added"), k + 1)
                    V.scalar_tensor_tensor(to, to, 0.2, to, ALU.mult, ALU.max).then_inc(S("leaky_made"), 1)

                def maxima(k, u):
                    dve.wait_ge(S("scores_turned"), k + 1)
                    dve.wait_ge(S("brk_in"), 16 * k + 16)
                    if not known_below(k, 1):
                        dve.wait_ge(S("max_turned"), k)
                    V.tensor_tensor_scan(forth[:, :], brk[:, 0:GE], bk_t[0:TI, :], LOWEST, ALU.add, ALU.max
                                         ).then_inc(S("forth_made"), 1)
                    dve.wait_ge(S("forth_made"), k + 1)
                    V.tensor_tensor_scan(srow[:, :][:, ::-1], brk[:, 1:GE + 1][:, ::-1], forth[:, :][:, ::-1],
                                         LOWEST, ALU.add, ALU.max).then_inc(S("max_made"), 1)

                def differences(k, u):
                    dve.wait_ge(S("max_turned"), k + 1)
                    if not known_below(k, 1):
                        dve.wait_ge(S("ex_made"), k)
                    V.tensor_tensor(diff[:, :, :].rearrange("p j x -> p (j x)"),
                                    lk[:, u, :, :].rearrange("p j x -> p (j x)"), bk_e[:, MCOL:MCOL + TG * TI],
                                    ALU.subtract).then_inc(S("diff_made"), 1)
                    last = lastT[:, bass.ds(k, 1), :].rearrange("p a q -> p (a q)")
                    V.tensor_tensor(ring[:, slot[u], C + HEADS:C + 2 * HEADS].rearrange("p (g j) h -> p j g h", g=GI),
                                    bk_e[:, MCOL:MCOL + TG * TI].rearrange("p (j g h) -> p j g h", j=TG, g=GI),
                                    last.rearrange("p (g j) -> p j g", g=GI).unsqueeze(3)
                                    .to_broadcast([P, TG, GI, HEADS]), ALU.mult).then_inc(S("maxcol_made"), 1)

                def outputs(i, u):
                    dve.wait_ge(S("ff2_done"), i + 1)
                    V.tensor_tensor(tile(big, i), bk_o[:, 0:C], b2row[:, :], ALU.add).then_inc(S("out_kept"), 1)

                def messages(k, u):
                    dve.wait_ge(S("ex_made"), k + 1)
                    for g in range(GI):
                        rows = ring[:, u * TI + g * TG:u * TI + (g + 1) * TG, :]
                        feats = rows[:, :, 0:C].rearrange("p q (h d) -> p q h d", h=HEADS)
                        V.tensor_tensor(feats, feats, rows[:, :, C:C + HEADS].unsqueeze(3)
                                        .to_broadcast([P, TG, HEADS, HD]), ALU.mult).then_inc(S("scaled"), 1)

                def merge(i, u):
                    m = mg[:, u, :]
                    two = lambda a: a.rearrange("p (n h) -> p n h", n=2)
                    dve.wait_ge(S("merge_exp"), i + 1)
                    V.tensor_tensor(two(m[:, 30:38]), two(m[:, 22:30]), parts[:, u, :, C:C + HEADS], ALU.mult
                                    ).then_inc(S("merge_steps"), 1)
                    dve.wait_ge(S("merge_steps"), 8 * i + 4)
                    V.tensor_tensor(m[:, 38:42], m[:, 30:34], m[:, 34:38], ALU.add).then_inc(S("merge_steps"), 1)
                    dve.wait_ge(S("merge_steps"), 8 * i + 5)
                    V.scalar_tensor_tensor(m[:, 42:46], m[:, 38:42], 0.0, m[:, 38:42], ALU.is_equal, ALU.add
                                           ).then_inc(S("merge_steps"), 1)
                    dve.wait_ge(S("merge_steps"), 8 * i + 6)
                    V.reciprocal(m[:, 46:50], m[:, 42:46]).then_inc(S("merge_steps"), 1)
                    dve.wait_ge(S("merge_steps"), 8 * i + 7)
                    V.tensor_tensor(two(m[:, 50:58]), two(m[:, 22:30]), m[:, 46:50].unsqueeze(1)
                                    .to_broadcast([P, 2, HEADS]), ALU.mult).then_inc(S("merge_steps"), 1)
                    dve.wait_ge(S("merge_steps"), 8 * i + 8)
                    for n, to in enumerate((sa[:, u, :], parts[:, u, 1, 0:C])):
                        V.tensor_tensor(by_head(to), by_head(parts[:, u, n, 0:C]),
                                        m[:, 50 + 4 * n:54 + 4 * n].unsqueeze(2).to_broadcast([P, HEADS, HD]), ALU.mult
                                        ).then_inc(S("merge_i"), 1)
                    dve.wait_ge(S("merge_i"), 2 * i + 2)
                    V.tensor_tensor(sa[:, u, :], sa[:, u, :], parts[:, u, 1, 0:C], ALU.add).then_inc(S("merged"), 1)
                    dve.wait_ge(S("merged"), i + 1)
                    V.tensor_tensor(sa[:, u, :], sa[:, u, :], gbrow[:, :], ALU.add).then_inc(S("gnn_made"), 1)

                def normed(i, u):
                    dve.wait_ge(S("rstd_made"), i + 1)
                    if not known_below(i, 1):
                        dve.wait_ge(S("xn2_turned"), i)
                    V.tensor_scalar(xn2, sd[:, u, :], bn[:, u, 6:7], bn[:, u, 9:10], ALU.subtract, ALU.mult
                                    ).then_inc(S("xn2_made"), 1)
                    dve.wait_ge(S("xn2_made"), i + 1)
                    if not known_below(i, 1):
                        dve.wait_ge(S("routed"), i)
                    V.tensor_tensor_reduce(junk[:, :], xn2, wrrow[:, :], 1.0, brc[:, 0:1], ALU.mult, ALU.add,
                                           mg[:, u, 60:61]).then_inc(S("route_made"), 1)
                    V.tensor_tensor(tile(xnT, i), sd[:, u, :], xn2, ALU.add).then_inc(S("rest_made"), 1)
                    dve.wait_ge(S("route_made"), i + 1)
                    V.tensor_tensor(wts[:, bass.ds(i, 1)], mg[:, u, 60:61], padneg[:, bass.ds(i, 1)], ALU.add
                                    ).then_inc(S("routed"), 1)

                def sums(i, u):
                    dve.wait_ge(S("proj_done"), i + 1)
                    V.tensor_tensor(sd[:, u, :], bk_t[:, 0:C], prow[:, :], ALU.add).then_inc(S("proj_read"), 1)
                    dve.wait_ge(S("proj_read"), i + 1)
                    dve.wait_ge(S("gnn_tanh"), i + 1)
                    V.scalar_tensor_tensor(sd[:, u, :], sa[:, u, :], 0.5, sd[:, u, :], ALU.mult, ALU.add
                                           ).then_inc(S("gnn_added"), 1)
                    dve.wait_ge(S("gnn_added"), i + 1)
                    V.tensor_tensor(sd[:, u, :], sd[:, u, :], xs[:, u, :], ALU.add).then_inc(S("x1_made"), 1)
                    dve.wait_ge(S("x1_made"), i + 1)
                    V.bn_stats(bn[:, u, 0:6], sd[:, u, :]).then_inc(S("bn_made"), 1)
                    dve.wait_ge(S("idx_made"), 2)
                    dve.wait_ge(S("bn_made"), i + 1)
                    V.bn_aggr(bn[:, u, 6:8], bn[:, u, 0:6]).then_inc(S("var_made"), 1)

                V.memset(exp_sum, 0.0).then_inc(S("exp_zeroed"), 1)
                dve.wait_ge(S("exp_zeroed"), 1)
                less(0)
                less(1)
                then, settle = chain(dve, "dve5")
                n_counts = [0]

                def total():
                    settle()
                    V.tensor_copy(off_s[:, 0:1], cnt[:, 0:1]).then_inc(S("counted"), 1)
                    n_counts[0] += 1
                    dve.wait_ge(S("totalled"), n_counts[0])
                    return bank[(n_counts[0] - 1) % 2]

                def find_sign(k, u):
                    dve.wait_ge(S("sums_done"), GI * NI)
                    dve.wait_ge(S("routed"), NT)
                    then(V.tensor_scalar(lower, iota_row[:, :], iota_col[:, 0:1], None, ALU.is_gt))
                    then(V.memset(cnt, 0.0))
                    settle()
                    then(V.tensor_scalar(sel_s, wts[:, :], 0.0, 0.0, ALU.is_ge, ALU.add, accum_out=cnt[:, 0:1]))
                    b = total()
                    then(V.tensor_scalar(dig, b[:, 0:1], float(KEEP), None, ALU.is_ge))
                    settle()
                    then(V.tensor_scalar(sign, dig, 2.0, -1.0, ALU.mult, ALU.add))
                    then(V.tensor_scalar(want, dig, float(2 * KEEP - NT * P - 1), float(NT * P + 1 - KEEP), ALU.mult, ALU.add))
                    settle()
                    then(V.tensor_scalar(v_s, wts[:, :], sign, None, ALU.mult))
                    then(V.memset(t_bits, 0.0))
                    dve.wait_ge(S("digits_made"), 1)

                def find_digits(lo, hi):
                    for r in range(lo, hi):
                        shift = 28 - 4 * r
                        J = 7 if r == 0 else 15
                        settle()
                        then(V.tensor_scalar(jtab, hotT[:, 0:30].bitcast(I32), shift, None, ALU.logical_shift_left))
                        settle()
                        then(V.tensor_tensor(cand[:, 0:J].bitcast(I32), jtab[:, 0:J], t_bits.bitcast(I32).to_broadcast([P, J]),
                                             ALU.bitwise_or))
                        settle()
                        then(V.tensor_tensor(cmp_s[:, 0:J, :], v_s.unsqueeze(1).to_broadcast([P, J, NT]),
                                             cand[:, 0:J].unsqueeze(2).to_broadcast([P, J, NT]), ALU.is_ge))
                        settle()
                        then(V.tensor_reduce(cnt[:, 0:J], cmp_s[:, 0:J, :], AX_X, ALU.add))
                        b = total()
                        then(V.tensor_scalar(sel_s[:, 0:J], b[:, 0:J], want, 0.0, ALU.is_ge, ALU.add, accum_out=dig))
                        settle()
                        then(V.tensor_scalar(dig_i.bitcast(I32), dig, float(1 << shift), None, ALU.mult))
                        settle()
                        then(V.tensor_tensor(t_bits.bitcast(I32), t_bits.bitcast(I32), dig_i.bitcast(I32), ALU.bitwise_or))

                def select_and_end(k, u):
                    select()
                    outputs(NT - 1, (NT - 1) % 2)

                def select():
                    settle()
                    then(V.tensor_tensor(thr, t_bits, sign, ALU.mult))
                    settle()
                    then(V.tensor_scalar(gt_s, wts[:, :], thr, 0.0, ALU.is_gt, ALU.add, accum_out=cnt[:, 0:1]))
                    V.tensor_scalar(eq_s, wts[:, :], thr, None, ALU.is_equal).then_inc(S("ties_made"), 1)
                    b = total()
                    then(V.tensor_scalar(need, b[:, 0:1], -1.0, float(KEEP), ALU.mult, ALU.add))
                    dve.wait_ge(S("ties_counted"), 1)
                    then(V.tensor_copy(tot_s, bank[3][:, 0:NT]))
                    then(V.memset(sel_s, 0.0))
                    settle()
                    then(V.tensor_tensor_scan(pre_s, tot_s, sel_s, 0.0, ALU.add, ALU.add))
                    settle()
                    then(V.tensor_tensor(pre_s, pre_s, tot_s, ALU.subtract))
                    settle()
                    then(V.tensor_tensor(pre_s, pre_s, bank[2][:, 0:NT], ALU.add))
                    settle()
                    then(V.tensor_scalar(pre_s, pre_s, need, None, ALU.is_lt))
                    settle()
                    then(V.tensor_tensor(pre_s, pre_s, eq_s, ALU.mult))
                    settle()
                    then(V.tensor_tensor(sel_s, pre_s, gt_s, ALU.add))
                    settle()
                    then(V.tensor_tensor(sel_s, sel_s, wts[:, :], ALU.mult))
                    settle()

                one_hots(0, 0)
                context(0, 0)
                steps(dve, [CONTEXT_A(context), WINDOWS(messages), SUM(products), EDGES(scores), MERGE(merge_weights), FF1(normed),
                            MERGE(merge), EDGES(maxima), CONTEXT_B(context), EDGES(edge_hots), FF2(outputs), EDGES(differences),
                            (0, NI - 1, hots_ahead), SUM(sums), FOLD(fold),
                            SEARCH[0](find_sign), *(SEARCH[n](lambda k, u, n=n: find_digits(DIGITS[n], DIGITS[n + 1]))
                                                    for n in range(2)), SEARCH[1](select_and_end)])

            @block.scalar
            def _(act):
                def context_tile(i, u):
                    act.wait_ge(S("keys_less"), i + 1)
                    keys = big[:, bass.ds(i, 1), :].rearrange("p a c -> p (a c)")
                    A.activation(keys, keys, ACT.Exp).then_inc(S("keys_exp"), 1)
                    if not isinstance(i, int) or i + 1 < NT:
                        renorm(i + 1, (u + 1) % 4)

                def renorm(i, u):
                    if not known_below(i, 2):
                        act.wait_ge(S("context_added"), i - 1)
                    act.wait_ge(S(f"x_again{u}"), 4 * (i - u) + 16)
                    A.activation(sc[:, u % 2, :], x_slot[u], ACT.Identity, bias=less_mean[:, bass.ds(i, 1)],
                                 scale=rstd[:, bass.ds(i, 1)]).then_inc(S("renormed"), 1)

                def context(k, u):
                    lo, hi = CHUNKS[k]
                    sweep(act, lo, hi, 4 if lo == 0 else 0, 1 if hi == NT else 0, context_tile, n=4)

                def exps(k, u):
                    act.wait_ge(S("diff_made"), k + 1)
                    A.activation(ring[:, slot[u], C:C + HEADS].rearrange("p (g j) h -> p j g h", g=GI),
                                 diff[:, :, :].rearrange("p j (g h) -> p j g h", g=GI), ACT.Exp).then_inc(S("ex_made"), 1)

                def merge_exp(i, u):
                    act.wait_ge(S("merge_asked"), i + 1)
                    A.activation(mg[:, u, 22:30], mg[:, u, 14:22], ACT.Exp).then_inc(S("merge_exp"), 1)

                def inverse_root(i, u):
                    act.wait_ge(S("var_made"), i + 1)
                    A.activation(bn[:, u, 8:9], bn[:, u, 7:8], ACT.Ln, bias=epsc[:, 0:1]).then_inc(S("ln_made"), 1)
                    act.wait_ge(S("ln_made"), i + 1)
                    A.activation(bn[:, u, 9:10], bn[:, u, 8:9], ACT.Exp, scale=-0.5).then_inc(S("rstd_made"), 1)

                def keep_one(k, g):
                    act.wait_ge(S("sums_done"), GI * k + g + 1)
                    if not (known_below(k, 1) and g < 2):
                        act.wait_ge(S(f"window_out{g % 2}"), 16 * (2 * k + g // 2))
                    A.activation(wout[:, g % 2, :], bank[2 + g % 2][:, 0:SW], ACT.Copy).then_inc(S("sums_kept"), 1)

                def keep_first(k, u):
                    keep_one(k, 0)

                def keep_others(k, u):
                    for g in range(1, GI):
                        keep_one(k, g)

                def gates(i, u):
                    act.wait_ge(S("gate_done"), i + 1)
                    if not known_below(i, 2):
                        act.wait_ge(S("proj_done"), i - 1)
                    for t in range(CT):
                        a = A.activation(sc[:, u, t * P:(t + 1) * P], bk_m[:, C + t * P:C + (t + 1) * P], ACT.Tanh,
                                         bias=hbg2[:, t:t + 1], scale=0.5)
                    a.then_inc(S("gate_made"), 1)
                    act.wait_ge(S("gnn_made"), i + 1)
                    A.activation(sa[:, u, :], sa[:, u, :], ACT.Tanh, scale=0.5).then_inc(S("gnn_tanh"), 1)

                def keep_turned(i, u):
                    act.wait_ge(S("xn2_turned"), i + 1)
                    if not known_below(i, 1):
                        act.wait_ge(S("ff1_done"), FT * i)
                    A.activation(xn2T, bank[7][:, 0:C], ACT.Copy).then_inc(S("xn2T_kept"), 1)

                def hidden(i, u):
                    if not known_below(i, 1):
                        act.wait_ge(S("ff2_done"), i)
                    for m in range(FT):
                        act.wait_ge(S("ff1_done"), FT * i + m // 4 * 4 + 4)
                        A.activation(hT[:, m, :], bank[6 + m // 4][:, (m % 4) * P:(m % 4 + 1) * P], ACT.Gelu_apprx_tanh,
                                     bias=b1_s[:, m:m + 1]).then_inc(S("gelu_made"), 1)

                renorm(0, 0)
                context(0, 0)
                steps(act, [CONTEXT_A(context), FF1(inverse_root), WINDOWS(keep_first), MERGE(merge_exp), WINDOWS(keep_others),
                            MERGE(gates), FF1(keep_turned), CONTEXT_B(context), EDGES(exps), FF1(hidden)])

            @block.tensor
            def _(pe):
                def context_tile(i, u):
                    pe.wait_ge(S("keys_exp"), i + 1)
                    pe.wait_ge(S("renormed"), i + 1)
                    s, e = known_below(i, 1), isinstance(i, int) and i == NT - 1
                    for t in range(CT):
                        mm = T.matmul(bank[4 + t][:, 0:C], sc[:, u, t * P:(t + 1) * P],
                                      big[:, bass.ds(i, 1), :].rearrange("p a c -> p (a c)"), start=s, stop=e)
                    mm.then_inc(S("context_added"), 1)

                def context(k, u):
                    lo, hi = CHUNKS[k]
                    sweep(pe, lo, hi, 2 if lo == 0 else 0, 2 if hi == NT else 0, context_tile)

                def fold(k, u):
                    pe.wait_ge(S("exp_added"), NT)
                    T.matmul(bank[6][0:1, 0:C], ones[:, 0:1], exp_sum, start=True, stop=True).then_inc(S("exp_summed"), 1)
                    pe.wait_ge(S("totals_kept"), 1 + CT)
                    for t in range(CT):
                        mm = T.matmul(bank[7][:, t:t + 1], totals[:, t * P:(t + 1) * P], ones[0:1, 0:1], start=True, stop=True)
                    mm.then_inc(S("sums_turned"), 1)
                    pe.wait_ge(S("wqv_in"), 32)
                    for t in range(CT):
                        for c in range(CT):
                            mm = T.matmul(bank[6][:, t * P:(t + 1) * P], sc[:, c, t * P:(t + 1) * P],
                                          feat[:, c, t * P:(t + 1) * P], start=(c == 0), stop=(c == CT - 1))
                        mm.then_inc(S("context_made"), 1)
                    for t in range(CT):
                        for c in range(CT):
                            mm = T.transpose(bank[4 + t][:, c * P:(c + 1) * P], wq_s[:, c, t * P:(t + 1) * P], ident[:, :])
                    mm.then_inc(S("wq_turned"), 1)
                    pe.wait_ge(S("wq_kept"), CT)
                    pe.wait_ge(S("context_kept"), CT)
                    for c in range(CT):
                        for t in range(CT):
                            mm = T.matmul(bank[7][:, c * C + t * P:c * C + (t + 1) * P], sa[:, t, c * P:(c + 1) * P],
                                          xs[:, 0, t * P:(t + 1) * P], start=True, stop=True)
                    mm.then_inc(S("folded"), 1)

                def mixer(i, u):
                    if known_below(i, 1):
                        pe.wait_ge(S("wqc_kept"), 1)
                    else:
                        pe.wait_ge(S("prod_made"), i)
                    for t in range(CT):
                        for c in range(CT):
                            mm = T.matmul(bk_m[:, t * P:(t + 1) * P], wqc_s[:, c, t * P:(t + 1) * P],
                                          xnT[:, bass.ds(i, 1), c * P:(c + 1) * P].rearrange("p a c -> p (a c)"),
                                          start=(c == 0), stop=(c == CT - 1))
                    mm.then_inc(S("mix_done"), 1)
                    pe.wait_ge(S(f"node_in{u}"), 24 * (i - u) + 48)
                    if not known_below(i, 1):
                        pe.wait_ge(S("gate_made"), i)
                    for t in range(CT):
                        mm = T.matmul(bk_m[:, C + t * P:C + (t + 1) * P], wg2_s[:, t * P:(t + 1) * P], hidT[:, u, :],
                                      start=True, stop=True)
                    mm.then_inc(S("gate_done"), 1)

                def scores(k, u):
                    pe.wait_ge(S("hotT_made"), k + 1)
                    pe.wait_ge(S(f"stat_in{u}"), 32 * (k - u) + 64)
                    if not known_below(k, 1):
                        pe.wait_ge(S("maxcol_made"), k)
                    for g in range(GI):
                        for j in range(TG):
                            q = j * GI + g
                            mm = T.matmul(bk_e[:, q * SPLIT:(q + 1) * SPLIT], hotT[:, (g * TG + j) * P:(g * TG + j + 1) * P],
                                          stat[:, u, g, :], start=True, stop=True)
                    mm.then_inc(S("scores_done"), 1)

                def turn_scores(k, u):
                    pe.wait_ge(S("leaky_made"), k + 1)
                    if isinstance(k, int) and k <= LAG_SUM:
                        if k:
                            pe.wait_ge(S("forth_made"), k)
                    else:
                        pe.wait_ge(S("proj_read"), k - LAG_SUM)
                    for j in range(TG):
                        mm = T.transpose(bk_t[0:TI, :].rearrange("r (e j) -> r j e", j=TG)[:, j, :], lk[:, u, j, :],
                                         ident[:, :])
                    mm.then_inc(S("scores_turned"), 1)

                def turn_maxima(k, u):
                    made = number(pe, k + 1)
                    pe.wait_ge(S("idx_made"), 2)
                    pe.wait_ge(S("max_made"), made)
                    for j in range(TG):
                        mm = T.transpose(bk_e[:, MCOL + j * TI:MCOL + (j + 1) * TI],
                                         srow[:, :].rearrange("r (e j) -> r j e", j=TG)[:, j, :], ident[0:TI, 0:TI])
                    mm.then_inc(S("max_turned"), 1)

                def ff2(i, u):
                    pe.wait_ge(S("gelu_made"), FT * i + FT)
                    if not known_below(i, 1):
                        pe.wait_ge(S("out_kept"), i)
                    ff2_products(range(FT))

                def ff2_products(some):
                    for m in some:
                        mm = T.matmul(bk_o[:, 0:C], hT[:, m, :], w2_s[:, m, :], start=(m == 0), stop=(m == FT - 1))
                        if m == FT - 1:
                            mm.then_inc(S("ff2_done"), 1)

                def first_sums(k, u):
                    pe.wait_ge(S("lastcol_made"), k + 1)
                    pe.wait_ge(S("maxcol_made"), k + 1)
                    window_sums(k, u, (0, 1))

                def other_sums(k, u):
                    window_sums(k, u, (2, 3))

                def window_sums(k, u, groups):
                    for g in groups:
                        pe.wait_ge(S("hot_made"), GI * k + g + 1)
                        pe.wait_ge(S("scaled"), GI * k + g + 1)
                        if not (known_below(k, 1) and g < 2):
                            pe.wait_ge(S("sums_kept"), GI * k + g - 1)
                        for j in range(TG):
                            q = u * TI + g * TG + j
                            mm = T.matmul(bank[2 + g % 2][:, 0:SW], hot[:, g * TG + j, :], ring[:, q, 0:SW],
                                          start=(j == 0), stop=(j == TG - 1))
                        mm.then_inc(S("sums_done"), 1)

                def project(i, u):
                    pe.wait_ge(S("prod_made"), i + 1)
                    if not known_below(i, 1):
                        pe.wait_ge(S("proj_read"), i)
                    if not (isinstance(i, int) and i + LAG_SUM >= NI):
                        pe.wait_ge(S("forth_made"), i + LAG_SUM + 1)
                    for t in range(CT):
                        mm = T.matmul(bk_t[:, 0:C], sc[:, u, t * P:(t + 1) * P], wproj_s[:, t, :],
                                      start=(t == 0), stop=(t == CT - 1))
                    mm.then_inc(S("proj_done"), 1)

                def turn_normed(i, u):
                    pe.wait_ge(S("xn2_made"), i + 1)
                    if not known_below(i, 1):
                        pe.wait_ge(S("gelu_made"), FT * i)
                    for t in range(CT):
                        mm = T.transpose(bank[7][:, t * P:(t + 1) * P], xn2[:, t * P:(t + 1) * P], ident[:, :])
                    mm.then_inc(S("xn2_turned"), 1)

                def ff1(i, u):
                    pe.wait_ge(S("xn2T_kept"), i + 1)
                    for m in range(FT):
                        if m % 4 == 0 and not known_below(i, 1):
                            pe.wait_ge(S("gelu_made"), FT * (i - 1) + m + 4)
                        for t in range(CT):
                            mm = T.matmul(bank[6 + m // 4][:, (m % 4) * P:(m % 4 + 1) * P], w1_s[:, t, m * P:(m + 1) * P],
                                          xn2T[:, t * P:(t + 1) * P], start=(t == 0), stop=(t == CT - 1))
                        mm.then_inc(S("ff1_done"), 1)

                def totals_of(lo, hi):
                    for n in range(lo, hi):
                        pe.wait_ge(S("counted"), n + 1)
                        T.matmul(bank[n % 2][:, 0:15], ones[:, :], cnt, start=True, stop=True).then_inc(S("totalled"), 1)
                        spare = 2 * (n - DIGITS[1] - 1)
                        if 0 <= spare < FT:
                            pe.wait_ge(S("gelu_made"), FT * NT)
                            pe.wait_ge(S("out_kept"), NT - 1)
                            ff2_products(range(spare, spare + 2))

                def ties(k, u):
                    pe.wait_ge(S("ties_made"), 1)
                    pe.wait_ge(S("sums_kept"), GI * NI)
                    T.matmul(bank[2][:, 0:NT], lower, eq_s, start=True, stop=True)
                    T.matmul(bank[3][:, 0:NT], ones[:, :], eq_s, start=True, stop=True).then_inc(S("ties_counted"), 1)

                context(0, 0)
                steps(pe, [CONTEXT_A(context), EDGES(scores), WINDOWS(first_sums), MERGE(mixer), WINDOWS(other_sums), EDGES(turn_scores),
                           CONTEXT_B(context), FF2(ff2), FF1(turn_normed), EDGES(turn_maxima), SUM(project), FF1(ff1), FOLD(fold),
                           SEARCH[0](lambda k, u: totals_of(0, 1 + DIGITS[1])),
                           SEARCH[1](lambda k, u: totals_of(1 + DIGITS[1], ROUNDS + 2)), SEARCH[1](ties)])

        with nc.Block() as block:
            @block.vector
            def _(dve):
                for t in range(NT):
                    V.scalar_tensor_tensor(xnT[:, t, :], big[:, t, :], sel_s[:, t:t + 1], xnT[:, t, :], ALU.mult, ALU.add
                                           ).then_inc(S("result_made"), 1)

            @block.sync
            def _(sp):
                to = out.rearrange("(t p) c -> p t c", p=P)
                for n in range(7):
                    sp.wait_ge(S("result_made"), (n + 1) * XC)
                    sp.dma_start(to[:, n * XC:(n + 1) * XC, :], xnT[:, n * XC:(n + 1) * XC, :]).then_inc(S("result_out"), 16)
                sp.wait_ge(S("result_out"), 16 * 7)


_INS = ["x", "src", "dst", "L0_gnn_W", "L0_gnn_att_src", "L0_gnn_att_dst", "L0_gnn_bias", "L0_mix_Wqkv",
        "L0_mix_Wproj", "L0_mix_bproj", "L0_mix_ln_g", "L0_mix_ln_b", "L0_mix_Wg1", "L0_mix_bg1", "L0_mix_Wg2",
        "L0_mix_bg2", "L0_ffn_wr", "L0_ffn_br", "L0_ffn_w1", "L0_ffn_b1", "L0_ffn_w2", "L0_ffn_b2"]
FAR = 1 << 20


def kernel(**inputs):
    import concourse.bacc as bacc
    from concourse.bass_utils import run_bass_kernel_spmd

    nc = bacc.Bacc("TRN2", target_bir_lowering=False, num_devices=1, dynamic_dma_scratch_size=4096)
    n_nodes, n_edges = inputs["x"].shape[0], inputs["src"].shape[0]
    padded = {"x": (-(-n_nodes // P) * P, 0), "src": (-(-n_edges // IE) * IE, 0), "dst": (-(-n_edges // IE) * IE, FAR)}
    arrays, args = {}, []
    for name in _INS:
        a = np.ascontiguousarray(inputs[name])
        if name in padded:
            rows, value = padded[name]
            full = np.full((rows, *a.shape[1:]), value, a.dtype)
            full[:a.shape[0]] = a
            a = full
        arrays[f"in_{name}"] = a
        args.append(nc.dram_tensor(f"in_{name}", a.shape, mybir.dt.from_np(a.dtype), kind="ExternalInput").ap())
    out = nc.dram_tensor("out_0", arrays["in_x"].shape, F32, kind="ExternalOutput").ap()
    gps_layer(nc, *args, out, n_nodes)
    r = run_bass_kernel_spmd(nc, [arrays], core_ids=[0])
    return r.results[0]["out_0"][:n_nodes]
```
